# Optimizing a Trainium2 kernel written in Bass

```python
import numpy as np
import jax
import jax.numpy as jnp

def _softmax(x, axis=-1):
    return jax.nn.softmax(x, axis=axis)

def _gelu(x):
    return jax.nn.gelu(x, approximate=True)

def _silu(x):
    return jax.nn.silu(x)

def _sigmoid(x):
    return jax.nn.sigmoid(x)

def _layernorm(x, axis=-1, eps=1e-05):
    m = jnp.mean(x, axis=axis, keepdims=True)
    v = jnp.var(x, axis=axis, keepdims=True)
    return (x - m) / jnp.sqrt(v + eps)

def _scatter_add(tgt, idx, src, axis=0):
    return tgt.at[idx].add(src)

def _segment_sum(src, seg, n):
    return jax.ops.segment_sum(src, seg, n)
kernel_name = 'mk_xattn_ffn_d2_seqx_r8_64a6a6'

def setup_inputs(seed: int=0):
    np.random.seed(seed)
    _w = jnp.asarray

    def _rec_inputs():
        import jax
        import jax.numpy as jnp
        _rk = jax.random.key(seed)
        x = -0.0002928 + 1 * jax.random.normal(jax.random.fold_in(_rk, 1), (4, 512, 128), jnp.float32)
        _lenS = 512 - jax.random.randint(jax.random.fold_in(_rk, 7), (4,), 0, max(1, 512 // 4) + 1, jnp.int32)
        _lenS2 = 32 - jax.random.randint(jax.random.fold_in(_rk, 8), (4,), 0, max(1, 32 // 4) + 1, jnp.int32)
        _ctx_1024P = jax.random.normal(jax.random.fold_in(_rk, 11), (4, 16, 128), jnp.float32)
        _ctx_1024c = jax.random.dirichlet(jax.random.fold_in(_rk, 511), 0.3 * jnp.ones((16,), jnp.float32), (4, 32))
        _ctx_1024t = jnp.einsum('bsk,bkd->bsd', _ctx_1024c, _ctx_1024P)
        _ctx_1024t = _ctx_1024t * jax.lax.rsqrt(jnp.mean(jnp.square(_ctx_1024t)) + 1e-12) * 0.953939
        ctx_1024 = -1.39393e-06 + 0.999914 * (_ctx_1024t + 0.3 * jax.random.normal(jax.random.fold_in(_rk, 611), (4, 32, 128), jnp.float32))
        _validS = jnp.arange(512)[None, :] < _lenS[:, None]
        _validS2 = jnp.arange(32)[None, :] < _lenS2[:, None]
        _causal = jnp.tril(jnp.ones((512, 512), dtype=bool))
        mask_BxS2_bf1 = jnp.ones((4, 32), dtype=bool)
        return (x, ctx_1024, mask_BxS2_bf1)
    x, ctx_1024, mask_BxS2_bf1 = _rec_inputs()

    def _L0_xattn_setup():
        import jax, jax.numpy as jnp
        import numpy as np
        QUERY_DIM = 128
        KEY_DIM = 128
        NUM_HEADS = 16
        HEAD_DIM = QUERY_DIM // NUM_HEADS
        key = jax.random.key(seed)
        ks = jax.random.split(key, 11)
        B, Sq, Sk = (2, 256, 256)
        s = 0.02
        return {'q': jax.random.normal(ks[0], (B, Sq, QUERY_DIM), jnp.float32), 'k': jax.random.normal(ks[1], (B, Sk, KEY_DIM), jnp.float32), 'v': jax.random.normal(ks[2], (B, Sk, KEY_DIM), jnp.float32), 'Wq': jax.random.normal(ks[3], (QUERY_DIM, QUERY_DIM), jnp.float32) * s, 'bq': jnp.zeros((QUERY_DIM,), jnp.float32), 'Wk': jax.random.normal(ks[4], (KEY_DIM, QUERY_DIM), jnp.float32) * s, 'bk': jnp.zeros((QUERY_DIM,), jnp.float32), 'Wv': jax.random.normal(ks[5], (KEY_DIM, QUERY_DIM), jnp.float32) * s, 'bv': jnp.zeros((QUERY_DIM,), jnp.float32), 'Wo': jax.random.normal(ks[6], (QUERY_DIM, QUERY_DIM), jnp.float32) * s, 'bo': jnp.zeros((QUERY_DIM,), jnp.float32)}
    _L0_xattn_all = _L0_xattn_setup()
    _L0_xattn_in = {k: v for k, v in _L0_xattn_all.items() if k in ('Wq', 'bq', 'Wk', 'bk', 'Wv', 'bv', 'Wo', 'bo')}
    del _L0_xattn_all

    def _L0_ffn_setup():
        import jax, jax.numpy as jnp
        import numpy as np
        N_EXPERTS = 8
        TOP_K = 2
        key = jax.random.key(seed)
        k1, k2, k3, k4 = jax.random.split(key, 4)
        B, T, C, H, E = (2, 256, 128, 512, N_EXPERTS)
        x = jax.random.normal(k1, (B, T, C), dtype=jnp.float32)
        router_w = jax.random.normal(k2, (E, C), dtype=jnp.float32) * 0.02
        w1 = jax.random.normal(k3, (E, C, H), dtype=jnp.float32) * (1.0 / np.sqrt(C))
        w2 = jax.random.normal(k4, (E, H, C), dtype=jnp.float32) * (1.0 / np.sqrt(H))
        return {'x': x, 'router_w': router_w, 'w1': w1, 'w2': w2}
    _L0_ffn_all = _L0_ffn_setup()
    _L0_ffn_in = {k: v for k, v in _L0_ffn_all.items() if k in ('router_w', 'w1', 'w2')}
    del _L0_ffn_all

    def _L1_xattn_setup():
        import jax, jax.numpy as jnp
        import numpy as np
        N_HEADS = 16
        D_MODEL = 128
        HEAD_DIM = D_MODEL // N_HEADS
        MASK_FILL = -100000000.0

        def _split_heads(x):
            B, S, _ = x.shape
            return x.reshape(B, S, N_HEADS, HEAD_DIM).transpose(0, 2, 1, 3)
        key = jax.random.key(seed)
        ks = jax.random.split(key, 12)
        B, L, P = (2, 256, 256)
        s = 1.0 / np.sqrt(D_MODEL).astype(np.float32)
        inp = {'q': jax.random.normal(ks[0], (B, L, D_MODEL), dtype=jnp.float32), 'k': jax.random.normal(ks[1], (B, P, D_MODEL), dtype=jnp.float32), 'v': jax.random.normal(ks[2], (B, P, D_MODEL), dtype=jnp.float32), 'attention_mask': jnp.ones((B, P), dtype=bool), 'Wq': jax.random.normal(ks[3], (D_MODEL, D_MODEL), dtype=jnp.float32) * s, 'bq': jnp.zeros((D_MODEL,), dtype=jnp.float32), 'Wk': jax.random.normal(ks[4], (D_MODEL, D_MODEL), dtype=jnp.float32) * s, 'bk': jnp.zeros((D_MODEL,), dtype=jnp.float32), 'Wv': jax.random.normal(ks[5], (D_MODEL, D_MODEL), dtype=jnp.float32) * s, 'bv': jnp.zeros((D_MODEL,), dtype=jnp.float32), 'Wo': jax.random.normal(ks[6], (D_MODEL, D_MODEL), dtype=jnp.float32) * s, 'bo': jnp.zeros((D_MODEL,), dtype=jnp.float32)}
        return inp
    _L1_xattn_all = _L1_xattn_setup()
    _L1_xattn_in = {k: v for k, v in _L1_xattn_all.items() if k in ('Wq', 'bq', 'Wk', 'bk', 'Wv', 'bv', 'Wo', 'bo')}
    del _L1_xattn_all

    def _L1_ffn_setup():
        import jax, jax.numpy as jnp
        import numpy as np
        DIM = 128
        HIDDEN = 512
        E = 8
        B, S = (2, 512)
        key = jax.random.key(seed)
        ks = jax.random.split(key, 8)
        sd = 1.0 / np.sqrt(DIM)
        sh = 1.0 / np.sqrt(HIDDEN)
        return {'x': jax.random.normal(ks[0], (B, S, DIM), dtype=jnp.float32), 'router_w': jax.random.uniform(ks[1], (DIM, E), jnp.float32, -sd, sd), 'router_b': jax.random.uniform(ks[2], (E,), jnp.float32, -sd, sd), 'w1': jax.random.uniform(ks[3], (E, DIM, 2 * HIDDEN), jnp.float32, -sd, sd), 'b1': jax.random.uniform(ks[4], (E, 2 * HIDDEN), jnp.float32, -sd, sd), 'w2': jax.random.uniform(ks[5], (E, HIDDEN, DIM), jnp.float32, -sh, sh), 'b2': jax.random.uniform(ks[6], (E, DIM), jnp.float32, -sh, sh)}
    _L1_ffn_all = _L1_ffn_setup()
    _L1_ffn_in = {k: v for k, v in _L1_ffn_all.items() if k in ('router_w', 'router_b', 'w1', 'b1', 'w2', 'b2')}
    del _L1_ffn_all
    return {'x': x, 'ctx_1024': ctx_1024, 'mask_BxS2_bf1': mask_BxS2_bf1, 'L0_xattn_Wq': _L0_xattn_in['Wq'], 'L0_xattn_bq': _L0_xattn_in['bq'], 'L0_xattn_Wk': _L0_xattn_in['Wk'], 'L0_xattn_bk': _L0_xattn_in['bk'], 'L0_xattn_Wv': _L0_xattn_in['Wv'], 'L0_xattn_bv': _L0_xattn_in['bv'], 'L0_xattn_Wo': _L0_xattn_in['Wo'], 'L0_xattn_bo': _L0_xattn_in['bo'], 'L0_ffn_router_w': _L0_ffn_in['router_w'], 'L0_ffn_w1': _L0_ffn_in['w1'], 'L0_ffn_w2': _L0_ffn_in['w2'], 'L1_xattn_Wq': _L1_xattn_in['Wq'], 'L1_xattn_bq': _L1_xattn_in['bq'], 'L1_xattn_Wk': _L1_xattn_in['Wk'], 'L1_xattn_bk': _L1_xattn_in['bk'], 'L1_xattn_Wv': _L1_xattn_in['Wv'], 'L1_xattn_bv': _L1_xattn_in['bv'], 'L1_xattn_Wo': _L1_xattn_in['Wo'], 'L1_xattn_bo': _L1_xattn_in['bo'], 'L1_ffn_router_w': _L1_ffn_in['router_w'], 'L1_ffn_router_b': _L1_ffn_in['router_b'], 'L1_ffn_w1': _L1_ffn_in['w1'], 'L1_ffn_b1': _L1_ffn_in['b1'], 'L1_ffn_w2': _L1_ffn_in['w2'], 'L1_ffn_b2': _L1_ffn_in['b2']}

def reference(x, ctx_1024, mask_BxS2_bf1, L0_xattn_Wq, L0_xattn_bq, L0_xattn_Wk, L0_xattn_bk, L0_xattn_Wv, L0_xattn_bv, L0_xattn_Wo, L0_xattn_bo, L0_ffn_router_w, L0_ffn_w1, L0_ffn_w2, L1_xattn_Wq, L1_xattn_bq, L1_xattn_Wk, L1_xattn_bk, L1_xattn_Wv, L1_xattn_bv, L1_xattn_Wo, L1_xattn_bo, L1_ffn_router_w, L1_ffn_router_b, L1_ffn_w1, L1_ffn_b1, L1_ffn_w2, L1_ffn_b2):
    import jax
    import jax.numpy as jnp

    def _L0_xattn_ref(q, k, v, Wq, bq, Wk, bk, Wv, bv, Wo, bo):
        import jax, jax.numpy as jnp
        import numpy as np
        QUERY_DIM = 128
        KEY_DIM = 128
        NUM_HEADS = 16
        HEAD_DIM = QUERY_DIM // NUM_HEADS
        B, Sq, _ = q.shape
        Sk = k.shape[1]
        scale = HEAD_DIM ** (-0.5)
        qh = (q @ Wq + bq).reshape(B, Sq, NUM_HEADS, HEAD_DIM).transpose(0, 2, 1, 3)
        kh = (k @ Wk + bk).reshape(B, Sk, NUM_HEADS, HEAD_DIM).transpose(0, 2, 1, 3)
        vh = (v @ Wv + bv).reshape(B, Sk, NUM_HEADS, HEAD_DIM).transpose(0, 2, 1, 3)
        scores = jnp.einsum('bhqd,bhkd->bhqk', qh, kh) * scale
        attn = jax.nn.softmax(scores, axis=-1)
        out = jnp.einsum('bhqk,bhkd->bhqd', attn, vh)
        out = out.transpose(0, 2, 1, 3).reshape(B, Sq, QUERY_DIM)
        return out @ Wo + bo

    def _L0_ffn_ref(x, router_w, w1, w2):
        import jax, jax.numpy as jnp
        import numpy as np
        N_EXPERTS = 8
        TOP_K = 2
        B, T, C = x.shape
        E = N_EXPERTS
        xf = x.reshape(-1, C)
        logits = jnp.einsum('nc,ec->ne', xf, router_w)
        probs = jax.nn.softmax(logits, axis=-1)
        top_w, top_i = jax.lax.top_k(probs, TOP_K)
        top_w = top_w / jnp.sum(top_w, axis=-1, keepdims=True)
        comb = jnp.einsum('nk,nke->ne', top_w, jax.nn.one_hot(top_i, E, dtype=xf.dtype))
        h = jax.nn.gelu(jnp.einsum('nc,ech->enh', xf, w1), approximate=False)
        y = jnp.einsum('enh,ehc->enc', h, w2)
        out = jnp.einsum('ne,enc->nc', comb, y)
        return out.reshape(B, T, C)

    def _L1_xattn_ref(q, k, v, attention_mask, Wq, bq, Wk, bk, Wv, bv, Wo, bo):
        import jax, jax.numpy as jnp
        import numpy as np
        N_HEADS = 16
        D_MODEL = 128
        HEAD_DIM = D_MODEL // N_HEADS
        MASK_FILL = -100000000.0

        def _split_heads(x):
            B, S, _ = x.shape
            return x.reshape(B, S, N_HEADS, HEAD_DIM).transpose(0, 2, 1, 3)
        qm = _split_heads(q @ Wq.T + bq)
        km = _split_heads(k @ Wk.T + bk)
        vm = _split_heads(v @ Wv.T + bv)
        scores = jnp.einsum('bnlh,bnph->bnlp', qm, km) / np.sqrt(HEAD_DIM).astype(np.float32)
        mask = attention_mask[:, None, None, :]
        scores = jnp.where(mask, scores, MASK_FILL)
        attn = jax.nn.softmax(scores, axis=-1)
        out = jnp.einsum('bnlp,bnph->bnlh', attn, vm)
        B, _, L, _ = out.shape
        out = out.transpose(0, 2, 1, 3).reshape(B, L, D_MODEL)
        return out @ Wo.T + bo

    def _L1_ffn_ref(x, router_w, router_b, w1, b1, w2, b2):
        import jax, jax.numpy as jnp
        import numpy as np
        DIM = 128
        HIDDEN = 512
        E = 8
        B, S = (2, 512)
        logits = jnp.einsum('bsd,de->bse', x, router_w) + router_b
        probs = jax.nn.softmax(logits, axis=-1)
        top1 = jnp.argmax(probs, axis=-1)
        out = jnp.zeros_like(x)
        for i in range(E):
            h = jnp.einsum('bsd,df->bsf', x, w1[i]) + b1[i]
            a, g = jnp.split(h, 2, axis=-1)
            y = jnp.einsum('bsh,hd->bsd', a * jax.nn.sigmoid(g), w2[i]) + b2[i]
            out = out + jnp.where((top1 == i)[..., None], y, 0.0)
        return out
    x = x + _L0_xattn_ref(_layernorm(x, axis=-1), ctx_1024, ctx_1024, L0_xattn_Wq, L0_xattn_bq, L0_xattn_Wk, L0_xattn_bk, L0_xattn_Wv, L0_xattn_bv, L0_xattn_Wo, L0_xattn_bo)
    x = x + _L0_ffn_ref(_layernorm(x, axis=-1), L0_ffn_router_w, L0_ffn_w1, L0_ffn_w2)
    x = x + _L1_xattn_ref(_layernorm(x, axis=-1), ctx_1024, ctx_1024, mask_BxS2_bf1, L1_xattn_Wq, L1_xattn_bq, L1_xattn_Wk, L1_xattn_bk, L1_xattn_Wv, L1_xattn_bv, L1_xattn_Wo, L1_xattn_bo)
    x = x + _L1_ffn_ref(_layernorm(x, axis=-1), L1_ffn_router_w, L1_ffn_router_b, L1_ffn_w1, L1_ffn_b1, L1_ffn_w2, L1_ffn_b2)
    return x

_drawn_inputs = setup_inputs


def setup_inputs(seed=0):
    import zlib

    import numpy as np

    out = dict(_drawn_inputs(seed))
    spreads = {'L0_xattn_bq': (0.0, 0.8),
     'L0_xattn_bk': (0.0, 0.8),
     'L0_xattn_bv': (0.0, 0.1),
     'L0_xattn_bo': (0.0, 0.1),
     'L1_xattn_bq': (0.0, 0.1),
     'L1_xattn_bk': (0.0, 0.8),
     'L1_xattn_bv': (0.0, 0.1),
     'L1_xattn_bo': (0.0, 0.1)}
    factors = {'L0_xattn_Wq': 7.848, 'L0_xattn_Wk': 6.531, 'L1_ffn_b1': 4.588, 'L1_ffn_b2': 2.715}
    for name, (base, spread) in spreads.items():
        noise = np.random.default_rng([zlib.crc32(name.encode()), seed]).standard_normal(out[name].shape)
        drawn = base * np.exp(spread * noise) if base else spread * noise
        out[name] = jnp.asarray(drawn.astype(out[name].dtype))
    for name, factor in factors.items():
        out[name] = (out[name] * factor).astype(out[name].dtype)
    return out
```

```python
from contextlib import ExitStack

import numpy as np
import concourse.bass as bass
from concourse import mybir
from concourse.alu_op_type import AluOpType as ALU

ACT = mybir.ActivationFunctionType
F32 = mybir.dt.float32
F16 = mybir.dt.float16
BF16 = mybir.dt.bfloat16
I32 = mybir.dt.int32
U8 = mybir.dt.uint8
AX = mybir.AxisListType.X

P = 128
BATCH, SEQ, DIM = 4, 512, 128
KEYS, HEADS = 32, 16
HD = DIM // HEADS
TOKENS = BATCH * SEQ
TILES = TOKENS // P
TPB = SEQ // P
EXPERTS = 8
HID = 512
CH = HID // P
HK = HEADS * KEYS
HPC = P // KEYS
VW = HPC * (HD + 1)
BLOCK = 4
EPS = 1e-5
SCALE = float(HD) ** -0.5
FILL = -1e8 / SCALE
TOPK = (2, 1)
CONSTS = 16
SLOT_TILES = tuple(k * TILES + EXPERTS - 1 for k in TOPK)
MAXT = max(SLOT_TILES)


DMA = 16
CREDIT = BLOCK


def ready(eng, sem, count):
    eng.wait_ge(sem, count + CREDIT)


def free(eng, sem, count):
    eng.wait_ge(sem, count + CREDIT)


def settle(eng, sem):
    eng.sem_inc(sem, 1)


def pipelined(eng, n, stages):
    most = max(lag for lag, _ in stages)
    assert most <= BLOCK

    def block(b, steps):
        for s in range(steps):
            for lag, emit in stages:
                item = b * BLOCK + (s - lag)
                if isinstance(item, int) and not 0 <= item < n:
                    continue
                emit(item, (s - lag) % BLOCK, b + (s - lag) // BLOCK)

    block(0, BLOCK)
    full = n // BLOCK
    with eng.Fori(1, full) as b:
        block(b, BLOCK)
    block(full, n - full * BLOCK + most)


def build(nc, a, out):
    ctx = ExitStack()
    with ctx:
        def sb(name, shape, dt=F32):
            return ctx.enter_context(nc.sbuf_tensor(name, shape, dt))

        def sem(name):
            return ctx.enter_context(nc.semaphore(name))

        def cols(t, i, w=P):
            return t[:, bass.ds(i * w, w)]

        xn_dram = nc.dram_tensor("xn_rows", [TOKENS, DIM], F32, kind="Internal").ap()
        xx_dram = nc.dram_tensor("xn_x_rows", [TOKENS, 2 * DIM], F32, kind="Internal").ap()
        y_dram = nc.dram_tensor("expert_rows", [SLOT_TILES[0] * P, DIM], F32, kind="Internal").ap()
        b1_dram = nc.dram_tensor("b1_parts", [3, EXPERTS * 2 * HID], BF16, kind="Internal").ap()
        b2_dram = nc.dram_tensor("b2_parts", [3, EXPERTS * DIM], BF16, kind="Internal").ap()
        out_rows = out.rearrange("b s d -> (b s) d")

        x = sb("x", [P, TILES * DIM])
        ident = sb("ident", [P, P])
        headmask = sb("headmask", [P, HEADS])
        groupmask = sb("groupmask", [P, HPC])
        before = sb("before", [P, P], F16)
        ones16 = sb("ones16", [P, P], F16)
        onesb = sb("onesb", [P, P], BF16)
        iota_row = sb("iota_row", [P, P], F16)
        iota_tiles = sb("iota_tiles", [P, MAXT], F16)
        tile_no = sb("tile_no", [P, MAXT])
        prefer = sb("prefer", [P, EXPERTS])
        steps128 = sb("steps128", [P, TILES])
        token1 = sb("token1", [P, TILES])
        carry = sb("carry", [P, EXPERTS * TILES])
        ones8 = sb("ones8", [P, EXPERTS])
        eps = sb("eps", [P, 1])
        minus_half = sb("minus_half", [P, 1])

        ctx_sb = sb("ctx_sb", [P, DIM])
        ctxT = sb("ctxT", [P, P])
        ctxrep = sb("ctxrep", [P, BATCH * P])
        wload = sb("wload", [P, 4 * DIM])
        wq, wk, wv, wo, kT = [], [], [], [], []
        bq, bk, bv, bo, kbd, vaug = [], [], [], [], [], []
        for L in range(2):
            wq.append(sb(f"wq{L}", [P, DIM]))
            wk.append(sb(f"wk{L}", [P, DIM]))
            wv.append(sb(f"wv{L}", [P, DIM]))
            wo.append(sb(f"wo{L}", [P, DIM]))
            kT.append(sb(f"kT{L}", [P, P]))
            bq.append(sb(f"bq{L}", [P, 1]))
            bk.append(sb(f"bk{L}", [P, 1]))
            bv.append(sb(f"bv{L}", [P, DIM]))
            bo.append(sb(f"bo{L}", [P, DIM]))
            kbd.append(sb(f"kbd{L}", [P, BATCH * HK]))
            vaug.append(sb(f"vaug{L}", [P, BATCH * CH * VW]))
        vrows = sb("vrows", [P, 2 * BATCH * DIM])
        mask8 = sb("mask8", [P, P], U8)
        maskf = sb("maskf", [P, P])
        maskrow = sb("maskrow", [1, BATCH * HK], BF16)
        rw_in = sb("rw_in", [EXPERTS, DIM])
        rw = [sb("rw0", [P, EXPERTS]), sb("rw1", [P, EXPERTS])]
        rb = sb("rb", [P, EXPERTS])
        w1 = [sb("w1_0", [P, EXPERTS * HID]), sb("w1_1", [P, EXPERTS * 2 * HID])]
        w2 = [sb("w2_0", [P, EXPERTS * HID]), sb("w2_1", [P, EXPERTS * HID])]
        NB1, NB2 = EXPERTS * 2 * HID // P, EXPERTS * DIM // P
        bias_in = sb("bias_in", [P, NB1 + NB2])
        bias_left = sb("bias_left", [P, 2, NB1 + NB2])
        bias_parts = sb("bias_parts", [P, 3, NB1 + NB2], BF16)
        b1 = sb("b1", [3, EXPERTS * 2 * HID], BF16)
        b2 = sb("b2", [3, EXPERTS * DIM], BF16)

        bst = sb("bst", [P, BLOCK * 6])
        mv = sb("mv", [P, BLOCK * 2])
        vareps = sb("vareps", [P, BLOCK])
        rstd = sb("rstd", [P, BLOCK])
        bst2 = sb("bst2", [P, BLOCK * 6])
        mv2 = sb("mv2", [P, BLOCK * 2])
        vareps2 = sb("vareps2", [P, BLOCK])
        rstd2 = sb("rstd2", [P, BLOCK])
        xn = sb("xn", [P, BLOCK * DIM])
        xn2 = sb("xn2", [P, BLOCK * DIM])
        xb = sb("xb", [P, BLOCK * DIM])
        xT = sb("xT", [P, 2 * P])
        xT2 = sb("xT2", [P, 2 * P])
        qT = sb("qT", [P, 2 * P])
        mx = sb("mx", [P, 2 * HEADS])
        shifted = sb("shifted", [P, 2 * HK])
        probs = sb("probs", [P, 2 * HK])
        probsT = sb("probsT", [P, 2 * HK])
        rsum = sb("rsum", [P, 2 * HEADS])
        heads_out = sb("heads_out", [P, 2 * DIM])
        headsT = sb("headsT", [P, 2 * P])
        y1g = sb("y1g", [P, BLOCK * DIM])
        y2g = sb("y2g", [P, BLOCK * DIM])
        xpart = sb("xpart", [P, BLOCK * DIM])

        TE = TILES * EXPERTS
        lg = sb("lg", [P, TE])
        pr = sb("pr", [P, TE])
        red = sb("red", [P, 8, TILES])
        tmp = sb("tmp", [P, TE])
        tmp2 = sb("tmp2", [P, TE])
        oh = [sb("oh0", [P, TE]), sb("oh1", [P, TE])]
        oh16 = sb("oh16", [P, TE], F16)
        tot = sb("tot", [P, TE])
        incl = sb("incl", [P, TE])
        slotmat = sb("slotmat", [P, TE])
        cmp = sb("cmp", [P, EXPERTS * TILES])
        etile = sb("etile", [P, 4, EXPERTS])
        cmpj = sb("cmpj", [P, MAXT * EXPERTS])
        etabf = sb("etabf", [P, MAXT])
        etab = [sb("etab0", [P, MAXT], I32), sb("etab1", [P, MAXT], I32)]
        gate = [sb("gate0", [P, TILES]), sb("gate1", [P, TILES])]
        slotf = sb("slotf", [P, 2 * TILES])
        slot = [sb("slots_0", [P, 2 * TILES], I32), sb("slots_1", [P, 2 * TILES], I32)]
        slot_r = sb("slot_r", [P, 2 * TILES], I32)
        slot_j = sb("slot_j", [P, 2 * TILES], I32)
        rowf = sb("rowf", [P, 2 * TILES])
        colf = sb("colf", [P, 2 * TILES])
        rowhot = sb("rowhot", [P, 2 * TILES * P], F16)
        colhot = sb("colhot", [P, 2 * TILES * MAXT], F16)
        tabf = sb("tabf", [P, 3 * MAXT])
        gidx = [sb("gidx0", [P, MAXT], I32), sb("gidx1", [P, MAXT], I32)]
        sidx = sb("sidx", [P, MAXT], I32)

        idx_ring = sb("idx_ring", [P, BLOCK], I32)
        idx2_ring = sb("idx2_ring", [P, BLOCK], I32)
        rows = sb("rows", [P, BLOCK * 2 * DIM])
        slotsT = sb("slotsT", [P, 2 * P])
        sig, hid, hidT = shifted, probs, probsT
        yout = xb

        psA = ctx.enter_context(nc.psum_tensor("psA", [P, 4 * 512], F32))
        psB = ctx.enter_context(nc.psum_tensor("psB", [P, 2 * 512], F32))
        psX = ctx.enter_context(nc.psum_tensor("psX", [P, 512], F32))
        psL = ctx.enter_context(nc.psum_tensor("psL", [P, 512], F32))

        def ps_scores(r):
            return psA[:, r * 512:r * 512 + HK]

        def ps_probsT(r):
            return psA[:, (2 + r) * 512:(2 + r) * 512 + HK]

        ps_out = psB[:, 0:CH * VW]
        ps_oT, ps_y = psB[:, 512:512 + P], psB[:, 512 + P:512 + P + DIM]
        ps_xT, ps_q = psX[:, 0:P], psX[:, P:2 * P]
        ps_xT2 = psL[:, 384:512]
        setup_banks = [psA[:, k * 512:k * 512 + P] for k in range(4)] + [psB[:, 0:P], psB[:, 512:512 + P],
                                                                         psX[:, 0:P], psL[:, 0:P]]


        in_x0, in_x1, in_ctx, in_w0, in_w1, in_small = map(sem, (
            "in_x0", "in_x1", "in_ctx", "in_w0", "in_w1", "in_small"))
        in_e0, in_e1, in_bias, parts_out, parts_in = map(sem, (
            "in_e0", "in_e1", "in_bias", "parts_out", "parts_in"))
        consts, zeroed = sem("consts"), sem("zeroed")
        ps_set, sb_set = sem("ps_set"), sem("sb_set")
        mask_ready, kbd_ready = sem("mask_ready"), [sem("kbd0_ready"), sem("kbd1_ready")]
        vaug_ready = [sem("vaug0_ready"), sem("vaug1_ready")]
        parts_ready, mrow_ready = sem("parts_ready"), sem("mrow_ready")
        vchain = sem("vchain")
        names = ["stat", "mv", "veps", "rstd", "xn", "xT_ps", "xT", "q_ps", "qT", "s_ps", "mx", "sh",
                 "p", "pT_ps", "pT", "o_ps", "rs", "o", "oT_ps", "oT", "y_ps", "x1", "xb",
                 "stat2", "mv2", "veps2", "rstd2", "xn2", "xT2_ps", "xT2", "logit"]
        A = {n: sem(n) for n in names}
        stored = [[sem(f"stored{L}_{u}") for u in range(BLOCK)] for L in range(2)]
        gathered_y = [sem(f"gathered_y{u}") for u in range(BLOCK)]
        combined, half_combined = sem("combined"), sem("half_combined")
        landed = sem("landed")
        yidx, idx2_ready = sem("yidx"), sem("idx2_ready")
        fnames = ["idx", "T_ps", "xT", "h_ps", "act", "hid", "hT_ps", "hT", "y_ps", "y"]
        F = [{n: sem(f"f_{n}_{L}") for n in fnames} for L in range(2)]
        gathered = [[sem(f"gathered{L}_{u}") for u in range(BLOCK)] for L in range(2)]
        written = [[sem(f"written{L}_{u}") for u in range(BLOCK)] for L in range(2)]
        R = [{n: sem(f"r_{n}_{L}") for n in ("shift", "exp", "onehot", "prefix", "hots", "chot", "table",
                                             "index")} for L in range(2)]

        waited = {n: sem(f"waited_{n}") for n in ("gpsimd", "tensor", "vector")}
        A["combined"] = combined
        makers = {
            "gpsimd": ("veps", "rstd", "xb", "veps2", "rstd2"),
            "scalar": ("xT", "qT", "p", "pT", "oT", "xT2"),
            "tensor": ("xT_ps", "q_ps", "s_ps", "pT_ps", "o_ps", "oT_ps", "y_ps", "xT2_ps", "logit"),
            "vector": ("stat", "mv", "xn", "mx", "sh", "rs", "o", "x1", "stat2", "mv2", "xn2", "combined"),
        }
        expert_makers = {
            "gpsimd": (("idx",), ("idx",)), "tensor": (("T_ps", "h_ps", "hT_ps", "y_ps"),) * 2,
            "scalar": (("xT", "hid", "y"), ("xT", "act", "hT")), "vector": (("hT",), ("hid", "y")),
        }

        def give_credit(eng, name):
            for n in makers[name]:
                eng.sem_inc(A[n], CREDIT)
            for L in range(2):
                for n in expert_makers[name][L]:
                    eng.sem_inc(F[L][n], CREDIT)

        block = ctx.enter_context(nc.Block())
        rows_per_place = [len(range(u, SLOT_TILES[0], BLOCK)) for u in range(BLOCK)]

        @block.sync
        def _(sp):
            sp.sem_inc(landed, CREDIT)
            for q in (*stored[0], *stored[1], *written[0]):
                sp.sem_inc(q, DMA)
            xr = a["x"].rearrange("b (t p) d -> p (b t) d", p=P)
            xv = x[:, :].rearrange("p (t d) -> p t d", d=DIM)
            sp.dma_start(xv[:, 0:TPB, :], xr[:, 0:TPB, :]).then_inc(in_x0, 16)
            sp.dma_start(ctx_sb[:, :], a["ctx_1024"].rearrange("b s d -> (b s) d")).then_inc(in_ctx, 16)
            for t, n in ((wq, "Wq"), (wk, "Wk"), (wv, "Wv"), (wo, "Wo")):
                sp.dma_start(t[0][:, :], a[f"L0_xattn_{n}"]).then_inc(in_w0, 16)
            sp.dma_start(xv[:, TPB:, :], xr[:, TPB:, :]).then_inc(in_x1, 16)
            for k, n in enumerate(("Wq", "Wk", "Wv", "Wo")):
                sp.dma_start(wload[:, k * DIM:(k + 1) * DIM], a[f"L1_xattn_{n}"]).then_inc(in_w1, 16)
            sp.dma_start(rw_in[:, :], a["L0_ffn_router_w"]).then_inc(in_w1, 16)
            sp.dma_start(bias_in[:, 0:NB1], a["L1_ffn_b1"].rearrange("e (q n) -> (e q) n", n=NB1)).then_inc(in_bias, 16)
            sp.dma_start(bias_in[:, NB1:], a["L1_ffn_b2"].rearrange("e (q n) -> (e q) n", n=NB2)).then_inc(in_bias, 16)
            for L, s_in in ((0, in_e0), (1, in_e1)):
                n1 = HID * (L + 1)
                sp.dma_start(w1[L][:, :].rearrange("p (e n) -> p e n", n=n1),
                             a[f"L{L}_ffn_w1"].rearrange("e c n -> c e n")).then_inc(s_in, 16)
                sp.dma_start(w2[L][:, :].rearrange("p (k d) -> p k d", d=DIM),
                             a[f"L{L}_ffn_w2"].rearrange("e (c p) d -> p (e c) d", p=P)).then_inc(s_in, 16)
            sp.wait_ge(parts_ready, 1)
            sp.dma_start(b1_dram.rearrange("k (p n) -> p k n", p=P), bias_parts[:, :, 0:NB1]).then_inc(parts_out, 16)
            sp.dma_start(b2_dram.rearrange("k (p n) -> p k n", p=P), bias_parts[:, :, NB1:]).then_inc(parts_out, 16)
            sp.wait_ge(parts_out, 32)
            sp.dma_start(b1[:, :], b1_dram).then_inc(parts_in, 16)
            sp.dma_start(b2[:, :], b2_dram).then_inc(parts_in, 16)

            for L in range(2):
                def store(i, u, g, L=L):
                    ready(sp, A["xn2"], L * TILES + i + 1)
                    if L == 0:
                        sp.dma_start(xn_dram[bass.ds(i * P, P), :], xn2[:, u * DIM:(u + 1) * DIM]).then_inc(stored[L][u], 16)
                    else:
                        sp.dma_start(xx_dram[bass.ds(i * P, P), 0:DIM], xn2[:, u * DIM:(u + 1) * DIM]).then_inc(stored[L][u], 16)
                        sp.dma_start(xx_dram[bass.ds(i * P, P), DIM:], cols(x, i)).then_inc(stored[L][u], 16)
                pipelined(sp, TILES, [(0, store)])
                if L == 0:
                    def store_y(j, u, g):
                        ready(sp, F[0]["y"], j + 1)
                        sp.dma_start(y_dram[bass.ds(j * P, P), :], yout[:, u * DIM:(u + 1) * DIM]).then_inc(written[0][u], 16)
                    pipelined(sp, SLOT_TILES[0], [(0, store_y)])
            def landed_rows(j, u, g):
                sp.wait_ge(written[1][u], 16 * (g + 1))
                sp.sem_inc(landed, 1)
            pipelined(sp, SLOT_TILES[1], [(0, landed_rows)])

        @block.gpsimd
        def _(pool):
            give_credit(pool, "gpsimd")
            pool.memset(ident[:, :], 0.0).then_inc(zeroed, 1)
            pool.memset(headmask[:, :], 1.0).then_inc(zeroed, 1)
            pool.memset(groupmask[:, :], 1.0).then_inc(zeroed, 1)
            pool.memset(before[:, :], 1.0).then_inc(zeroed, 1)
            pool.memset(carry[:, :], 1.0).then_inc(zeroed, 1)
            pool.memset(ones16[:, :], 1.0).then_inc(consts, 1)
            pool.memset(onesb[:, :], 1.0).then_inc(consts, 1)
            pool.memset(ones8[:, :], 1.0).then_inc(consts, 1)
            pool.memset(minus_half[:, :], -0.5).then_inc(consts, 1)
            pool.memset(eps[:, :], EPS).then_inc(consts, 1)
            pool.wait_ge(zeroed, 5)
            pool.affine_select(out=ident[:, :], in_=ident[:, :], compare_op=ALU.not_equal, fill=1.0, base=0,
                               pattern=[[-1, P]], channel_multiplier=1).then_inc(consts, 1)
            for m, n, w in ((headmask, HEADS, HD), (groupmask, HPC, KEYS)):
                pool.affine_select(out=m[:, :], in_=m[:, :], compare_op=ALU.is_ge, fill=0.0, base=0,
                                   pattern=[[-w, n]], channel_multiplier=1).then_inc(zeroed, 1)
            pool.wait_ge(zeroed, 7)
            for m, n, w in ((headmask, HEADS, HD), (groupmask, HPC, KEYS)):
                pool.affine_select(out=m[:, :], in_=m[:, :], compare_op=ALU.is_ge, fill=0.0, base=w - 1,
                                   pattern=[[w, n]], channel_multiplier=-1).then_inc(consts, 1)
            pool.affine_select(out=before[:, :], in_=before[:, :], compare_op=ALU.is_gt, fill=0.0, base=0,
                               pattern=[[1, P]], channel_multiplier=-1).then_inc(consts, 1)
            pool.affine_select(out=carry[:, :], in_=carry[:, :], compare_op=ALU.not_equal, fill=0.0, base=0,
                               pattern=[[0, EXPERTS], [1, TILES]], channel_multiplier=0).then_inc(consts, 1)
            for t, pat, base, cm in (
                    (iota_row, [[1, P]], 0, 0), (iota_tiles, [[1, MAXT]], 0, 0), (tile_no, [[1, MAXT]], 0, 0),
                    (prefer, [[-1, EXPERTS]], EXPERTS, 0), (steps128, [[P, TILES]], 0, 0),
                    (token1, [[P, TILES]], 1, 1)):
                pool.iota(t[:, :], pat, base=base, channel_multiplier=cm,
                          allow_small_or_imprecise_dtypes=True).then_inc(consts, 1)
            pool.wait_ge(in_small, 16 * 11)
            pool.tensor_copy(maskf[:, :], mask8[:, :]).then_inc(mask_ready, 1)
            pool.wait_ge(mask_ready, 1)
            pool.tensor_scalar(maskrow[0:1, :].rearrange("p (b h k) -> p b h k", b=BATCH, h=HEADS),
                               maskf[0:1, :].rearrange("p (b k) -> p b k", b=BATCH).unsqueeze(2)
                               .to_broadcast([1, BATCH, HEADS, KEYS]),
                               -1.0, -FILL, ALU.add, ALU.mult).then_inc(mrow_ready, 1)

            for L in range(2):
                D, N0 = A, L * TILES

                def pick(i, u, g):
                    if L == 1:
                        free(pool, combined, i + 1 - BLOCK)
                        pool.tensor_copy(idx_ring[:, u:u + 1], slot[0][:, bass.ds(i, 1)]).then_inc(yidx, 1)
                        pool.tensor_copy(idx2_ring[:, u:u + 1], slot[0][:, bass.ds(i + TILES, 1)]).then_inc(yidx, 1)
                        pool.wait_ge(yidx, i * 2 + 2)
                        for dst, ix in ((y1g, idx_ring), (y2g, idx2_ring)):
                            settle(pool, waited["gpsimd"])
                            pool.indirect_dma_start(dst[:, u * DIM:(u + 1) * DIM], None, y_dram,
                                                    bass.IndirectOffsetOnAxis(ap=ix[:, u:u + 1], axis=0)
                                                    ).then_inc(gathered_y[u], 16)

                def rstd1(i, u, g):
                    ready(pool, D["mv"], N0 + i + 1)
                    pool.tensor_tensor(vareps[:, u:u + 1], mv[:, 2 * u + 1:2 * u + 2], eps[:, :], ALU.add
                                       ).then_inc(D["veps"], 1)
                    ready(pool, D["veps"], N0 + i + 1)
                    free(pool, D["xn"], N0 + i + 1 - BLOCK)
                    pool.tensor_tensor(rstd[:, u:u + 1], vareps[:, u:u + 1], minus_half[:, :], ALU.pow
                                       ).then_inc(D["rstd"], 1)

                def residual(i, u, g):
                    ready(pool, D["mv"], N0 + i + 1)
                    free(pool, D["x1"], N0 + i + 1 - BLOCK)
                    pool.tensor_tensor(xb[:, u * DIM:(u + 1) * DIM], cols(x, i), bo[L][:, :], ALU.add
                                       ).then_inc(D["xb"], 1)

                def rstd_2(i, u, g):
                    ready(pool, D["mv2"], N0 + i + 1)
                    pool.tensor_tensor(vareps2[:, u:u + 1], mv2[:, 2 * u + 1:2 * u + 2], eps[:, :], ALU.add
                                       ).then_inc(D["veps2"], 1)
                    ready(pool, D["veps2"], N0 + i + 1)
                    free(pool, D["xn2"], N0 + i + 1 - BLOCK)
                    pool.tensor_tensor(rstd2[:, u:u + 1], vareps2[:, u:u + 1], minus_half[:, :], ALU.pow
                                       ).then_inc(D["rstd2"], 1)

                if L == 1:
                    for u in range(BLOCK):
                        pool.wait_ge(written[0][u], DMA + 16 * rows_per_place[u])
                pipelined(pool, TILES, [(0, pick), (0, rstd1), (1, residual), (4, rstd_2)])

                K = TOPK[L] * TILES
                NT = SLOT_TILES[L]
                pool.wait_ge(R[L]["index"], 1)
                for u in range(BLOCK):
                    pool.wait_ge(stored[L][u], DMA + 16 * (L + 1) * (TILES // BLOCK))
                W = (L + 1) * DIM
                src = xn_dram if L == 0 else xx_dram

                def gather(j, u, g):
                    free(pool, F[L]["T_ps" if L == 0 else "y"], j + 1 - BLOCK)
                    pool.tensor_copy(idx_ring[:, u:u + 1], gidx[L][:, bass.ds(j, 1)]).then_inc(F[L]["idx"], 1)
                    ready(pool, F[L]["idx"], j + 1)
                    settle(pool, waited["gpsimd"])
                    pool.indirect_dma_start(rows[:, u * W:(u + 1) * W], None, src,
                                            bass.IndirectOffsetOnAxis(ap=idx_ring[:, u:u + 1], axis=0)
                                            ).then_inc(gathered[L][u], 16)

                last_row = pool.to_reg(TOKENS - 1)

                def scatter(j, u, g):
                    ready(pool, F[L]["y"], j + 1)
                    pool.tensor_copy(idx2_ring[:, u:u + 1], sidx[:, bass.ds(j, 1)]).then_inc(idx2_ready, 1)
                    pool.wait_ge(idx2_ready, j + 1)
                    settle(pool, waited["gpsimd"])
                    pool.indirect_dma_start(out_rows, bass.IndirectOffsetOnAxis(ap=idx2_ring[:, u:u + 1], axis=0),
                                            yout[:, u * DIM:(u + 1) * DIM], None,
                                            bounds_check=last_row, oob_is_err=False
                                            ).then_inc(written[L][u], 16)

                pipelined(pool, NT, [(0, gather)] + ([(4, scatter)] if L else []))

        @block.scalar
        def _(act):
            def row(ap):
                return ap.rearrange("(a n) -> a n", a=1).partition_broadcast(P).rearrange("p a n -> p (a n)")

            def column(ap):
                return ap.rearrange("(p a) -> p a", a=1)

            for L in range(2):
                act.dma_start(bq[L][:, :], column(a[f"L{L}_xattn_bq"])).then_inc(in_small, 16)
                act.dma_start(bk[L][:, :], column(a[f"L{L}_xattn_bk"])).then_inc(in_small, 16)
                act.dma_start(bv[L][:, :], row(a[f"L{L}_xattn_bv"])).then_inc(in_small, 16)
                act.dma_start(bo[L][:, :], row(a[f"L{L}_xattn_bo"])).then_inc(in_small, 16)
            act.dma_start(rb[:, :], row(a["L1_ffn_router_b"])).then_inc(in_small, 16)
            act.dma_start(rw[1][:, :], a["L1_ffn_router_w"]).then_inc(in_small, 16)
            act.dma_start(mask8[:, :], row(a["mask_BxS2_bf1"].rearrange("b k -> (b k)"))).then_inc(in_small, 16)
            give_credit(act, "scalar")

            for L in range(2):
                D, N0 = A, L * TILES

                def evac_x(i, u, g):
                    r = u % 2
                    ready(act, D["xT_ps"], N0 + i + 1)
                    free(act, D["q_ps"], N0 + i - 1)
                    act.activation(xT[:, r * P:(r + 1) * P], ps_xT, ACT.Copy).then_inc(D["xT"], 1)

                def evac_q(i, u, g):
                    r = u % 2
                    ready(act, D["q_ps"], N0 + i + 1)
                    free(act, D["s_ps"], N0 + i - 1)
                    act.activation(qT[:, r * P:(r + 1) * P], ps_q, ACT.Identity, bias=bq[L][:, 0:1]).then_inc(D["qT"], 1)

                def exp(i, u, g):
                    r = u % 2
                    ready(act, D["sh"], N0 + i + 1)
                    free(act, D["pT_ps"], N0 + i - 1)
                    act.activation(probs[:, r * HK:(r + 1) * HK], shifted[:, r * HK:(r + 1) * HK], ACT.Exp,
                                   scale=SCALE).then_inc(D["p"], 1)

                def evac_p(i, u, g):
                    r = u % 2
                    ready(act, D["pT_ps"], N0 + i + 1)
                    free(act, D["o_ps"], N0 + i - 1)
                    act.activation(probsT[:, r * HK:(r + 1) * HK], ps_probsT(r), ACT.Copy
                                   ).then_inc(D["pT"], 1)

                def evac_o(i, u, g):
                    r = u % 2
                    ready(act, D["oT_ps"], N0 + i + 1)
                    free(act, D["y_ps"], N0 + i - 1)
                    act.activation(headsT[:, r * P:(r + 1) * P], ps_oT, ACT.Copy).then_inc(D["oT"], 1)

                def evac_x2(i, u, g):
                    r = u % 2
                    ready(act, D["xT2_ps"], N0 + i + 1)
                    free(act, D["logit"], N0 + i - 1)
                    act.activation(xT2[:, r * P:(r + 1) * P], ps_xT2, ACT.Copy).then_inc(D["xT2"], 1)

                if L == 0:
                    act.wait_ge(in_small, 16 * 11)
                pipelined(act, TILES, [(2, exp), (3, evac_p), (1, evac_x), (1, evac_q), (3, evac_o), (4, evac_x2)])

                act.wait_ge(R[L]["shift"], 1)
                act.activation(pr[:, :], tmp[:, :], ACT.Exp).then_inc(R[L]["exp"], 1)

                NT = SLOT_TILES[L]
                E = F[L]

                def gelu(j, u, g):
                    r = u % 2
                    ready(act, E["h_ps"], j + 1)
                    free(act, E["hT_ps"], j - 1)
                    act.activation(hid[:, r * HID:(r + 1) * HID], psA[:, r * 512:r * 512 + HID], ACT.Gelu
                                   ).then_inc(E["hid"], 1)

                def sigmoid(j, u, g):
                    r = u % 2
                    ready(act, E["h_ps"], j + 1)
                    free(act, E["hid"], j - 1)
                    act.activation(sig[:, r * HID:(r + 1) * HID], psA[:, (2 * r + 1) * 512:(2 * r + 2) * 512],
                                   ACT.Sigmoid).then_inc(E["act"], 1)

                def evac_slots(j, u, g):
                    r = u % 2
                    ready(act, E["T_ps"], j + 1)
                    free(act, E["h_ps"], j - 1)
                    act.activation(slotsT[:, r * P:(r + 1) * P], ps_xT, ACT.Copy).then_inc(E["xT"], 1)

                def evac_y(j, u, g):
                    r = u % 2
                    ready(act, E["y_ps"], j + 1)
                    need_written(act, j, u, g)
                    act.activation(yout[:, u * DIM:(u + 1) * DIM], psL[:, 0:DIM], ACT.Copy
                                   ).then_inc(E["y"], 1)

                def need_written(eng, j, u, g):
                    eng.wait_ge(written[L][u], DMA + 16 * g)

                def evac_h(j, u, g):
                    r = u % 2
                    ready(act, E["hT_ps"], j + 1)
                    free(act, E["y_ps"], j - 1)
                    act.activation(hidT[:, r * HID:(r + 1) * HID], psB[:, r * 512:r * 512 + HID], ACT.Copy
                                   ).then_inc(E["hT"], 1)

                if L == 0:
                    pipelined(act, NT, [(0, evac_slots), (1, gelu), (3, evac_y)])
                else:
                    pipelined(act, NT, [(0, evac_slots), (1, sigmoid), (2, evac_h)])

        @block.vector
        def _(dve):
            give_credit(dve, "vector")
            links = [0]

            def link(ins):
                links[0] += 1
                ins.then_inc(vchain, 1)
                dve.wait_ge(vchain, links[0])

            V = nc.vector

            evac = [0]

            def setup_evac(make):
                evac[0] += 1
                dve.wait_ge(ps_set, evac[0])
                make().then_inc(sb_set, 1)

            setup_evac(lambda: V.tensor_copy(ctxT[:, :], setup_banks[0]))
            dve.wait_ge(sb_set, 1)
            link(V.tensor_copy(ctxrep[:, :].rearrange("p (b r k) -> p b r k", b=BATCH, r=HPC),
                               ctxT[:, :].rearrange("p (b k) -> p b k", b=BATCH).unsqueeze(2)
                               .to_broadcast([P, BATCH, HPC, KEYS])))
            setup_evac(lambda: V.tensor_copy(rw[0][:, :], setup_banks[1][:, 0:EXPERTS]))
            for k, t in enumerate((wq, wk, wv, wo)):
                setup_evac(lambda: V.tensor_copy(t[1][:, :], setup_banks[(2 + k) % 8]))
            dve.wait_ge(in_small, 16 * 11)
            for L in range(2):
                setup_evac(lambda: V.tensor_scalar(kT[L][:, :], setup_banks[(6 + L * 5) % 8], bk[L][:, 0:1], None, ALU.add))
                for b in range(BATCH):
                    setup_evac(lambda: V.tensor_tensor(vrows[:, (L * BATCH + b) * DIM:(L * BATCH + b + 1) * DIM],
                                                       setup_banks[(7 + L * 5 + b) % 8], bv[L][:, :], ALU.add))
            dve.wait_ge(sb_set, evac[0])
            dve.wait_ge(mask_ready, 1)
            link(V.tensor_tensor(kT[1][:, :], kT[1][:, :], maskf[:, :], ALU.mult))
            for L in range(2):
                for b in range(BATCH):
                    V.tensor_tensor(kbd[L][:, b * HK:(b + 1) * HK].rearrange("p (h k) -> p h k", h=HEADS),
                                    kT[L][:, b * KEYS:(b + 1) * KEYS].unsqueeze(1).to_broadcast([P, HEADS, KEYS]),
                                    headmask[:, :].unsqueeze(2).to_broadcast([P, HEADS, KEYS]),
                                    ALU.mult).then_inc(kbd_ready[L], 1)
                    va = vaug[L][:, b * CH * VW:(b + 1) * CH * VW].rearrange("p (c h d) -> p c h d", c=CH, h=HPC)
                    vr = vrows[:, (L * BATCH + b) * DIM:(L * BATCH + b + 1) * DIM].rearrange(
                        "p (c h d) -> p c h d", c=CH, h=HPC)
                    V.tensor_tensor(va[:, :, :, 0:HD], vr,
                                    groupmask[:, :].unsqueeze(1).unsqueeze(3).to_broadcast([P, CH, HPC, HD]),
                                    ALU.mult).then_inc(vaug_ready[L], 1)
                    V.tensor_copy(va[:, :, :, HD], groupmask[:, :].unsqueeze(1).to_broadcast([P, CH, HPC])
                                  ).then_inc(vaug_ready[L], 1)
            dve.wait_ge(in_bias, 32)
            left = bias_in[:, :]
            for k in range(3):
                link(V.tensor_copy(bias_parts[:, k, :], left))
                if k < 2:
                    link(V.tensor_tensor(bias_left[:, k, :], left, bias_parts[:, k, :], ALU.subtract))
                    left = bias_left[:, k, :]
            dve.sem_inc(parts_ready, 1)

            for L in range(2):
                D, N0 = A, L * TILES

                def combine(i, u, g):
                    if L == 1:
                        dve.wait_ge(gathered_y[u], 32 * (g + 1))
                        V.scalar_tensor_tensor(xpart[:, u * DIM:(u + 1) * DIM], y1g[:, u * DIM:(u + 1) * DIM],
                                               gate[0][:, bass.ds(i, 1)], cols(x, i), ALU.mult, ALU.add
                                               ).then_inc(half_combined, 1)
                        dve.wait_ge(half_combined, i + 1)
                        V.scalar_tensor_tensor(cols(x, i), y2g[:, u * DIM:(u + 1) * DIM],
                                               gate[1][:, bass.ds(i, 1)], xpart[:, u * DIM:(u + 1) * DIM],
                                               ALU.mult, ALU.add).then_inc(combined, 1)
                        ready(dve, combined, i + 1)
                    elif isinstance(i, int) and i == 0:
                        dve.wait_ge(in_x0, 16)
                    elif isinstance(g, int):
                        pass
                    elif u == 0:
                        dve.wait_ge(in_x1, 16)

                def stat(i, u, g):
                    settle(dve, waited["vector"])
                    V.bn_stats(bst[:, 6 * u:6 * u + 6], cols(x, i)).then_inc(D["stat"], 1)
                    ready(dve, D["stat"], N0 + i + 1)
                    settle(dve, waited["vector"])
                    V.bn_aggr(mv[:, 2 * u:2 * u + 2], bst[:, 6 * u:6 * u + 6]).then_inc(D["mv"], 1)

                def norm(i, u, g):
                    ready(dve, D["rstd"], N0 + i + 1)
                    free(dve, D["xT_ps"], N0 + i + 1 - BLOCK)
                    V.tensor_scalar(xn[:, u * DIM:(u + 1) * DIM], cols(x, i), mv[:, 2 * u:2 * u + 1],
                                    rstd[:, u:u + 1], ALU.subtract, ALU.mult).then_inc(D["xn"], 1)

                def shift(i, u, g):
                    r = u % 2
                    sc = ps_scores(r).rearrange("p (h k) -> p h k", h=HEADS)
                    ready(dve, D["s_ps"], N0 + i + 1)
                    V.tensor_reduce(mx[:, r * HEADS:(r + 1) * HEADS], sc, axis=AX, op=ALU.max).then_inc(D["mx"], 1)
                    ready(dve, D["mx"], N0 + i + 1)
                    free(dve, D["p"], N0 + i - 1)
                    V.tensor_tensor(shifted[:, r * HK:(r + 1) * HK].rearrange("p (h k) -> p h k", h=HEADS), sc,
                                    mx[:, r * HEADS:(r + 1) * HEADS].unsqueeze(2).to_broadcast([P, HEADS, KEYS]),
                                    ALU.subtract).then_inc(D["sh"], 1)

                def normalise(i, u, g):
                    r = u % 2
                    po = ps_out.rearrange("p (h d) -> p h d", h=HEADS)
                    ready(dve, D["o_ps"], N0 + i + 1)
                    V.reciprocal(rsum[:, r * HEADS:(r + 1) * HEADS], po[:, :, HD]).then_inc(D["rs"], 1)
                    ready(dve, D["rs"], N0 + i + 1)
                    free(dve, D["oT_ps"], N0 + i - 1)
                    V.tensor_tensor(heads_out[:, r * DIM:(r + 1) * DIM].rearrange("p (h d) -> p h d", h=HEADS),
                                    po[:, :, 0:HD],
                                    rsum[:, r * HEADS:(r + 1) * HEADS].unsqueeze(2).to_broadcast([P, HEADS, HD]),
                                    ALU.mult).then_inc(D["o"], 1)

                def add(i, u, g):
                    ready(dve, D["y_ps"], N0 + i + 1)
                    ready(dve, D["xb"], N0 + i + 1)
                    V.tensor_tensor(cols(x, i), ps_y, xb[:, u * DIM:(u + 1) * DIM], ALU.add).then_inc(D["x1"], 1)
                    ready(dve, D["x1"], N0 + i + 1)
                    settle(dve, waited["vector"])
                    V.bn_stats(bst2[:, 6 * u:6 * u + 6], cols(x, i)).then_inc(D["stat2"], 1)
                    ready(dve, D["stat2"], N0 + i + 1)
                    settle(dve, waited["vector"])
                    V.bn_aggr(mv2[:, 2 * u:2 * u + 2], bst2[:, 6 * u:6 * u + 6]).then_inc(D["mv2"], 1)

                def norm2(i, u, g):
                    ready(dve, D["rstd2"], N0 + i + 1)
                    free(dve, D["xT2_ps"], N0 + i + 1 - BLOCK)
                    dve.wait_ge(stored[L][u], DMA + 16 * (L + 1) * g)
                    V.tensor_scalar(xn2[:, u * DIM:(u + 1) * DIM], cols(x, i), mv2[:, 2 * u:2 * u + 1],
                                    rstd2[:, u:u + 1], ALU.subtract, ALU.mult).then_inc(D["xn2"], 1)

                pipelined(dve, TILES, [(0, combine), (0, stat), (4, add), (2, shift), (0, norm), (3, normalise), (4, norm2)])

                K = TOPK[L]
                NT = SLOT_TILES[L]

                def te(t):
                    return t.rearrange("p (t e) -> p t e", e=EXPERTS)

                def et(t):
                    return t.rearrange("p (e t) -> p e t", t=TILES)

                def over_e(t):
                    return t.unsqueeze(2).to_broadcast([P, TILES, EXPERTS])

                M, SUM, RM, M2 = (red[:, k, :] for k in range(4))
                ready(dve, D["logit"], N0 + TILES)
                if L == 0:
                    link(V.tensor_copy(lg[:, :], psL[:, 0:TE]))
                else:
                    link(V.tensor_tensor(te(lg[:, :]), te(psL[:, 0:TE]),
                                         rb[:, :].unsqueeze(1).to_broadcast([P, TILES, EXPERTS]), ALU.add))
                link(V.tensor_reduce(M, te(lg[:, :]), axis=AX, op=ALU.max))
                V.tensor_tensor(te(tmp[:, :]), te(lg[:, :]), over_e(M), ALU.subtract).then_inc(R[L]["shift"], 1)
                dve.wait_ge(R[L]["exp"], 1)
                link(V.tensor_reduce(SUM, te(pr[:, :]), axis=AX, op=ALU.add))
                link(V.reciprocal(RM, SUM))
                link(V.tensor_tensor(te(pr[:, :]), te(pr[:, :]), over_e(RM), ALU.mult))
                tops = [red[:, 4, :], red[:, 5, :]]
                for k in range(K):
                    link(V.tensor_reduce(tops[k], te(pr[:, :]), axis=AX, op=ALU.max))
                    link(V.tensor_tensor(te(tmp[:, :]), te(pr[:, :]), over_e(tops[k]), ALU.is_equal))
                    link(V.tensor_tensor(te(tmp2[:, :]), te(tmp[:, :]),
                                         prefer[:, :].unsqueeze(1).to_broadcast([P, TILES, EXPERTS]), ALU.mult))
                    link(V.tensor_reduce(RM, te(tmp2[:, :]), axis=AX, op=ALU.max))
                    link(V.tensor_tensor(te(oh[k][:, :]), te(tmp2[:, :]), over_e(RM), ALU.is_equal))
                    if k + 1 < K:
                        link(V.scalar_tensor_tensor(pr[:, :], oh[k][:, :], -2.0, pr[:, :], ALU.mult, ALU.add))
                if K == 2:
                    link(V.tensor_tensor(oh16[:, :], oh[0][:, :], oh[1][:, :], ALU.add))
                else:
                    link(V.tensor_copy(oh16[:, :], oh[0][:, :]))
                dve.sem_inc(R[L]["onehot"], 1)
                if K == 2:
                    link(V.tensor_tensor(SUM, tops[0], tops[1], ALU.add))
                    link(V.reciprocal(M2, SUM))
                    V.tensor_tensor(gate[0][:, :], tops[0], M2, ALU.mult)
                    link(V.tensor_tensor(gate[1][:, :], tops[1], M2, ALU.mult))
                dve.wait_ge(R[L]["prefix"], 1)
                link(V.tensor_copy(et(tot[:, :]), psL[:, 256:256 + TE].rearrange("p (t e) -> p e t", e=EXPERTS)))
                link(V.tensor_tensor_scan(incl[:, :], carry[:, :], tot[:, :], 0.0, ALU.mult, ALU.add))
                count = et(incl[:, :])[:, :, TILES - 1]
                link(V.tensor_tensor(et(cmp[:, :]), count.unsqueeze(2).to_broadcast([P, EXPERTS, TILES]),
                                     steps128[:, :].unsqueeze(1).to_broadcast([P, EXPERTS, TILES]), ALU.is_gt))
                ntile, upto, base = (etile[:, k, :] for k in range(3))
                link(V.tensor_reduce(ntile, et(cmp[:, :]), axis=AX, op=ALU.add))
                link(V.tensor_tensor_scan(upto, ones8[:, :], ntile, 0.0, ALU.mult, ALU.add))
                link(V.tensor_tensor(base, upto, ntile, ALU.subtract))
                link(V.tensor_tensor(tot[:, :], incl[:, :], tot[:, :], ALU.subtract))
                link(V.scalar_tensor_tensor(et(incl[:, :]), base.unsqueeze(2).to_broadcast([P, EXPERTS, TILES]),
                                            float(P), et(tot[:, :]), ALU.mult, ALU.add))
                link(V.tensor_tensor(te(slotmat[:, :]), te(psL[:, 128:128 + TE]),
                                     incl[:, :].rearrange("p (e t) -> p t e", t=TILES), ALU.add))
                for k in range(K):
                    link(V.tensor_tensor(tmp[:, :], slotmat[:, :], oh[k][:, :], ALU.mult))
                    link(V.tensor_reduce(slotf[:, k * TILES:(k + 1) * TILES], te(tmp[:, :]), axis=AX, op=ALU.add))
                KT = K * TILES
                link(V.tensor_copy(slot[L][:, 0:KT], slotf[:, 0:KT]))
                V.tensor_scalar(slot_r[:, 0:KT], slot[L][:, 0:KT], P - 1, None, ALU.bitwise_and)
                link(V.tensor_scalar(slot_j[:, 0:KT], slot[L][:, 0:KT], 7, None, ALU.logical_shift_right))
                V.tensor_copy(rowf[:, 0:KT], slot_r[:, 0:KT])
                link(V.tensor_copy(colf[:, 0:KT], slot_j[:, 0:KT]))
                for q in range(KT):
                    V.tensor_scalar(rowhot[:, q * P:(q + 1) * P], iota_row[:, :], rowf[:, q:q + 1], None,
                                    ALU.is_equal)
                    V.tensor_scalar(colhot[:, q * MAXT:q * MAXT + NT], iota_tiles[:, 0:NT], colf[:, q:q + 1],
                                    token1[:, q % TILES:q % TILES + 1], ALU.is_equal, ALU.mult
                                    ).then_inc(R[L]["hots"], 1)
                cj = cmpj[:, 0:NT * EXPERTS].rearrange("p (j e) -> p j e", e=EXPERTS)
                link(V.tensor_tensor(cj, upto.unsqueeze(1).to_broadcast([P, NT, EXPERTS]),
                                     tile_no[:, 0:NT].unsqueeze(2).to_broadcast([P, NT, EXPERTS]), ALU.is_le))
                link(V.tensor_reduce(etabf[:, 0:NT], cj, axis=AX, op=ALU.add))
                link(V.tensor_scalar(etab[L][:, 0:NT], etabf[:, 0:NT], float(EXPERTS - 1), None, ALU.min))
                dve.wait_ge(R[L]["table"], 1)
                table = psL[:, 384:384 + NT]
                link(V.tensor_scalar(gidx[L][:, 0:NT], table, -1.0, 0.0, ALU.add, ALU.max))
                if L == 1:
                    link(V.tensor_scalar(tabf[:, 0:NT], table, 0.0, 2.0 * TOKENS, ALU.is_equal, ALU.mult))
                    link(V.scalar_tensor_tensor(sidx[:, 0:NT], tabf[:, 0:NT], -1.0, table, ALU.add, ALU.add))
                dve.sem_inc(R[L]["index"], 1)

                E = F[L]

                def evac_h(j, u, g):
                    r = u % 2
                    ready(dve, E["hT_ps"], j + 1)
                    free(dve, E["y_ps"], j - 1)
                    V.tensor_copy(hidT[:, r * HID:(r + 1) * HID], psB[:, r * 512:r * 512 + HID]
                                  ).then_inc(E["hT"], 1)

                def glu(j, u, g):
                    r = u % 2
                    ready(dve, E["act"], j + 1)
                    free(dve, E["hT_ps"], j - 1)
                    V.tensor_tensor(hid[:, r * HID:(r + 1) * HID], psA[:, 2 * r * 512:2 * r * 512 + HID],
                                    sig[:, r * HID:(r + 1) * HID], ALU.mult).then_inc(E["hid"], 1)

                def residual(j, u, g):
                    r = u % 2
                    ready(dve, E["y_ps"], j + 1)
                    free(dve, landed, j + 1 - BLOCK)
                    V.tensor_tensor(yout[:, u * DIM:(u + 1) * DIM], psL[:, 0:DIM],
                                    rows[:, (2 * u + 1) * DIM:(2 * u + 2) * DIM], ALU.add).then_inc(E["y"], 1)

                if L == 0:
                    pipelined(dve, NT, [(2, evac_h)])
                else:
                    pipelined(dve, NT, [(1, glu), (3, residual)])

        @block.tensor
        def _(pe):
            give_credit(pe, "tensor")
            T = nc.tensor
            done = [0]

            def setup(emit):
                n = done[0]
                if n > 7:
                    pe.wait_ge(sb_set, n - 7)
                emit(setup_banks[n % 8]).then_inc(ps_set, 1)
                done[0] += 1

            pe.wait_ge(consts, CONSTS)
            pe.wait_ge(in_ctx, 16)
            setup(lambda d: T.transpose(d, ctx_sb[:, :], ident[:, :]))
            pe.wait_ge(in_w1, 16 * 5)
            setup(lambda d: T.transpose(d[:, 0:EXPERTS], rw_in[:, :], ident[0:EXPERTS, 0:EXPERTS]))
            for k in range(4):
                setup(lambda d: T.transpose(d, wload[:, k * DIM:(k + 1) * DIM], ident[:, :]))
            pe.wait_ge(in_w0, 16 * 4)
            pe.wait_ge(sb_set, 6)
            pe.wait_ge(vchain, 1)
            for L in range(2):
                setup(lambda d: T.matmul(d, wk[L][:, :], ctxT[:, :], start=True, stop=True))
                for b in range(BATCH):
                    setup(lambda d: T.matmul(d, ctxrep[:, b * P:(b + 1) * P], wv[L][:, :], start=True, stop=True))
            pe.wait_ge(sb_set, done[0])

            for L in range(2):
                D, N0 = A, L * TILES
                pe.wait_ge(kbd_ready[L], BATCH)
                pe.wait_ge(vaug_ready[L], 2 * BATCH)
                if L == 1:
                    pe.wait_ge(mrow_ready, 1)

                def transpose_x(i, u, g):
                    ready(pe, D["xn"], N0 + i + 1)
                    free(pe, D["qT"], N0 + i)
                    T.transpose(ps_xT, xn[:, u * DIM:(u + 1) * DIM], ident[:, :]).then_inc(D["xT_ps"], 1)

                def queries(i, u, g):
                    r = u % 2
                    ready(pe, D["xT"], N0 + i + 1)
                    T.matmul(ps_q, wq[L][:, :], xT[:, r * P:(r + 1) * P], start=True, stop=True).then_inc(D["q_ps"], 1)

                def scores(i, u, g):
                    r = u % 2
                    ready(pe, D["qT"], N0 + i + 1)
                    free(pe, D["sh"], N0 + i - 1)
                    last = T.matmul(ps_scores(r), qT[:, r * P:(r + 1) * P], cols(kbd[L], g, HK), start=True, stop=L == 0)
                    if L == 1:
                        last = T.matmul(ps_scores(r), onesb[0:1, :], cols(maskrow, g, HK), start=False, stop=True)
                    last.then_inc(D["s_ps"], 1)

                def transpose_p(i, u, g):
                    r = u % 2
                    ready(pe, D["p"], N0 + i + 1)
                    free(pe, D["pT"], N0 + i - 1)
                    for c in range(CH):
                        last = T.transpose(ps_probsT(r)[:, c * P:(c + 1) * P],
                                           probs[:, r * HK + c * P:r * HK + (c + 1) * P], ident[:, :])
                    last.then_inc(D["pT_ps"], 1)

                def values(i, u, g):
                    r = u % 2
                    ready(pe, D["pT"], N0 + i + 1)
                    free(pe, D["o"], N0 + i)
                    for c in range(CH):
                        last = T.matmul(ps_out[:, c * VW:(c + 1) * VW],
                                        probsT[:, r * HK + c * P:r * HK + (c + 1) * P],
                                        vaug[L][:, bass.ds(g * CH * VW + c * VW, VW)], start=True, stop=True)
                    last.then_inc(D["o_ps"], 1)

                def transpose_o(i, u, g):
                    r = u % 2
                    ready(pe, D["o"], N0 + i + 1)
                    free(pe, D["x1"], N0 + i)
                    T.transpose(ps_oT, heads_out[:, r * DIM:(r + 1) * DIM], ident[:, :]).then_inc(D["oT_ps"], 1)

                def project(i, u, g):
                    r = u % 2
                    ready(pe, D["oT"], N0 + i + 1)
                    T.matmul(ps_y, headsT[:, r * P:(r + 1) * P], wo[L][:, :], start=True, stop=True).then_inc(D["y_ps"], 1)

                def transpose_x2(i, u, g):
                    ready(pe, D["xn2"], N0 + i + 1)
                    free(pe, D["xT2"], N0 + i)
                    T.transpose(ps_xT2, xn2[:, u * DIM:(u + 1) * DIM], ident[:, :]).then_inc(D["xT2_ps"], 1)

                def logits(i, u, g):
                    r = u % 2
                    ready(pe, D["xT2"], N0 + i + 1)
                    T.matmul(psL[:, bass.ds(i * EXPERTS, EXPERTS)], xT2[:, r * P:(r + 1) * P], rw[L][:, :],
                             start=True, stop=True).then_inc(D["logit"], 1)

                pipelined(pe, TILES, [(4, project), (2, scores), (1, transpose_x), (3, transpose_p), (1, queries),
                                      (3, values), (3, transpose_o), (4, transpose_x2), (4, logits)])

                NT = SLOT_TILES[L]
                pe.wait_ge(R[L]["onehot"], 1)
                T.matmul(psL[:, 128:128 + TE], before[:, :], oh16[:, :], start=True, stop=True)
                T.matmul(psL[:, 256:256 + TE], ones16[:, :], oh16[:, :], start=True, stop=True
                         ).then_inc(R[L]["prefix"], 1)
                KT = TOPK[L] * TILES
                for q in range(KT):
                    pe.wait_ge(R[L]["hots"], q + 1)
                    last = T.matmul(psL[:, 384:384 + NT], rowhot[:, q * P:(q + 1) * P],
                                    colhot[:, q * MAXT:q * MAXT + NT], start=q == 0, stop=q == KT - 1)
                last.then_inc(R[L]["table"], 1)

                E = F[L]
                H = (L + 1) * HID
                pe.wait_ge(R[L]["index"], 1)
                pe.wait_ge((in_e0, in_e1)[L], 32)
                if L == 1:
                    pe.wait_ge(parts_in, 32)
                W = (L + 1) * DIM

                def transpose_rows(j, u, g):
                    r = u % 2
                    pe.wait_ge(gathered[L][u], 16 * (g + 1))
                    free(pe, E["xT"], j)
                    T.transpose(ps_xT, rows[:, u * W:u * W + DIM], ident[:, :]).then_inc(E["T_ps"], 1)

                def up(j, u, g):
                    r = u % 2
                    ready(pe, E["xT"], j + 1)
                    free(pe, E["hid"], j - 1)
                    settle(pe, waited["tensor"])
                    e = pe.value_load(etab[L][0:1, bass.ds(j, 1)], min_val=0, max_val=EXPERTS - 1)
                    for k in range(L + 1):
                        dst = psA[:, ((L + 1) * r + k) * 512:((L + 1) * r + k) * 512 + HID]
                        last = T.matmul(dst, slotsT[:, r * P:(r + 1) * P], w1[L][:, bass.ds(e * H + k * HID, HID)],
                                        start=True, stop=L == 0)
                        if L == 1:
                            last = T.matmul(dst, onesb[0:3, :], b1[:, bass.ds(e * H + k * HID, HID)],
                                            start=False, stop=True)
                    last.then_inc(E["h_ps"], 1)

                def transpose_h(j, u, g):
                    r = u % 2
                    ready(pe, E["hid"], j + 1)
                    free(pe, E["hT"], j - 1)
                    for c in range(CH):
                        last = T.transpose(psB[:, r * 512 + c * P:r * 512 + (c + 1) * P],
                                           hid[:, r * HID + c * P:r * HID + (c + 1) * P], ident[:, :])
                    last.then_inc(E["hT_ps"], 1)

                def down(j, u, g):
                    r = u % 2
                    ready(pe, E["hT"], j + 1)
                    free(pe, E["y"], j)
                    settle(pe, waited["tensor"])
                    e = pe.value_load(etab[L][0:1, bass.ds(j, 1)], min_val=0, max_val=EXPERTS - 1)
                    dst = psL[:, 0:DIM]
                    for c in range(CH):
                        last = T.matmul(dst, hidT[:, r * HID + c * P:r * HID + (c + 1) * P],
                                        w2[L][:, bass.ds(e * HID + c * DIM, DIM)], start=c == 0,
                                        stop=c == CH - 1 and L == 0)
                    if L == 1:
                        last = T.matmul(dst, onesb[0:3, :], b2[:, bass.ds(e * DIM, DIM)], start=False, stop=True)
                    last.then_inc(E["y_ps"], 1)

                pipelined(pe, NT, [(0, transpose_rows), (1, up), (2, transpose_h), (3, down)])


_INS = ['x', 'ctx_1024', 'mask_BxS2_bf1'] + [
    f'L{L}_xattn_{n}' for L in range(2) for n in ('Wq', 'bq', 'Wk', 'bk', 'Wv', 'bv', 'Wo', 'bo')] + [
    'L0_ffn_router_w', 'L0_ffn_w1', 'L0_ffn_w2', 'L1_ffn_router_w', 'L1_ffn_router_b',
    'L1_ffn_w1', 'L1_ffn_b1', 'L1_ffn_w2', 'L1_ffn_b2']


def kernel(**inputs):
    import concourse.bacc as bacc
    from concourse.bass_utils import run_bass_kernel_spmd

    nc = bacc.Bacc("TRN2", target_bir_lowering=False, num_devices=1)
    arrays, aps = {}, {}
    for name in _INS:
        v = np.ascontiguousarray(inputs[name])
        if v.dtype == np.bool_:
            v = v.view(np.uint8)
        arrays[f"in_{name}"] = v
        aps[name] = nc.dram_tensor(f"in_{name}", v.shape, mybir.dt.from_np(v.dtype), kind="ExternalInput").ap()
    out = nc.dram_tensor("out", (BATCH, SEQ, DIM), F32, kind="ExternalOutput").ap()
    build(nc, aps, out)
    r = run_bass_kernel_spmd(nc, [arrays], core_ids=[0])
    return r.results[0]["out"]
```

```python
from contextlib import ExitStack

import numpy as np
import concourse.bass as bass
from concourse import mybir
from concourse.alu_op_type import AluOpType as ALU

ACT = mybir.ActivationFunctionType
F32 = mybir.dt.float32
F16 = mybir.dt.float16
BF16 = mybir.dt.bfloat16
I32 = mybir.dt.int32
U8 = mybir.dt.uint8
AX = mybir.AxisListType.X

P = 128
BATCH, SEQ, DIM = 4, 512, 128
KEYS, HEADS = 32, 16
HD = DIM // HEADS
TOKENS = BATCH * SEQ
TILES = TOKENS // P
GROUP = SEQ // P
GROUPS = TILES // GROUP
GW = GROUP * P
EXPERTS = 8
HID = 512
CH = HID // P
HK = HEADS * KEYS
HPC = P // KEYS
VW = HPC * (HD + 1)
BLOCK = 4
EPS = 1e-5
SCALE = float(HD) ** -0.5
FILL = -1e8 / SCALE
TOPK = (2, 1)
CONSTS = 22
SLOT_TILES = tuple(k * TILES + EXPERTS - 1 for k in TOPK)
MAXT = max(SLOT_TILES)
MAXI = -(-MAXT // 4) * 4


DMA = 16
CREDIT = BLOCK


def ready(eng, sem, count):
    eng.wait_ge(sem, count + CREDIT)


def free(eng, sem, count):
    eng.wait_ge(sem, count + CREDIT)


def settle(eng, sem):
    eng.sem_inc(sem, 1)


def pipelined(eng, n, stages, block=BLOCK, tail=None):
    most = max(lag for lag, _ in stages)
    assert most <= block

    def steps(b, count):
        for s in range(count):
            for lag, emit in stages:
                item = b * block + (s - lag)
                if isinstance(item, int) and not 0 <= item < n:
                    continue
                emit(item, (s - lag) % block, b + (s - lag) // block)
            if tail and isinstance(b, int) and b * block + s >= n:
                tail(b * block + s - n)

    steps(0, block)
    full = n // block
    with eng.Fori(1, full) as b:
        steps(b, block)
    steps(full, n - full * block + most)


def skewed(n, stages):
    for step in range(n + max(lag for lag, _ in stages)):
        for lag, emit in stages:
            if 0 <= step - lag < n:
                emit(step - lag)


def positive(eng, sem, count):
    if count > 0:
        eng.wait_ge(sem, count)


def build(nc, a, out):
    ctx = ExitStack()
    with ctx:
        def sb(name, shape, dt=F32):
            return ctx.enter_context(nc.sbuf_tensor(name, shape, dt))

        def sem(name):
            return ctx.enter_context(nc.semaphore(name))

        def cols(t, i, w=P):
            return t[:, bass.ds(i * w, w)]

        xn_dram = nc.dram_tensor("xn_rows", [TOKENS, DIM], F32, kind="Internal").ap()
        xx_dram = nc.dram_tensor("xn_x_rows", [TOKENS, 2 * DIM], F32, kind="Internal").ap()
        y_dram = nc.dram_tensor("expert_rows", [2 * TOKENS, DIM], F32, kind="Internal").ap()
        b1_dram = nc.dram_tensor("b1_parts", [3, EXPERTS * 2 * HID], BF16, kind="Internal").ap()
        b2_dram = nc.dram_tensor("b2_parts", [3, EXPERTS * DIM], BF16, kind="Internal").ap()
        out_rows = out.rearrange("b s d -> (b s) d")

        x = sb("x", [P, TILES * DIM])
        ident = sb("ident", [P, P])
        headmask = sb("headmask", [P, HEADS])
        groupmask = sb("groupmask", [P, HPC])
        before = sb("before", [P, P], F16)
        ones16 = sb("ones16", [P, P], F16)
        onesb = sb("onesb", [P, P], BF16)
        iota_row = sb("iota_row", [P, P], F16)
        iota_tiles = sb("iota_tiles", [P, MAXT], F16)
        tile_no = sb("tile_no", [P, MAXT])
        prefer = sb("prefer", [P, EXPERTS])
        steps128 = sb("steps128", [P, TILES])
        token1 = sb("token1", [P, 2 * TILES])
        carry = sb("carry", [P, EXPERTS * TILES])
        ones8 = sb("ones8", [P, EXPERTS])
        eps = sb("eps", [P, 1])
        minus_half = sb("minus_half", [P, 1])
        minus_one = sb("minus_one", [P, 1])

        ctx_sb = sb("ctx_sb", [P, DIM])
        ctxT = sb("ctxT", [P, P])
        ybuf = sb("ybuf", [P, 2 * 2 * GW])
        wload, ctxrep, vrows = (ybuf[:, k * GW:(k + 1) * GW] for k in range(3))
        wq, wk, wv, wo, kT = [], [], [], [], []
        bq, bk, bv, bo, kbd, vaug = [], [], [], [], [], []
        for L in range(2):
            wq.append(sb(f"wq{L}", [P, DIM]))
            wk.append(sb(f"wk{L}", [P, DIM]))
            wv.append(sb(f"wv{L}", [P, DIM]))
            wo.append(sb(f"wo{L}", [P, DIM]))
            kT.append(sb(f"kT{L}", [P, P]))
            bq.append(sb(f"bq{L}", [P, 1]))
            bk.append(sb(f"bk{L}", [P, 1]))
            bv.append(sb(f"bv{L}", [P, DIM]))
            bo.append(sb(f"bo{L}", [P, DIM]))
            kbd.append(sb(f"kbd{L}", [P, BATCH * HK]))
            vaug.append(sb(f"vaug{L}", [P, BATCH * CH * VW]))
        mask8 = sb("mask8", [P, P], U8)
        maskf = sb("maskf", [P, P])
        maskrow = sb("maskrow", [1, BATCH * HK], BF16)
        rw_in = sb("rw_in", [EXPERTS, DIM])
        rw = [sb("rw0", [P, EXPERTS]), sb("rw1", [P, EXPERTS])]
        rb = sb("rb", [P, EXPERTS])
        w1 = [sb("w1_0", [P, EXPERTS * HID]), sb("w1_1", [P, EXPERTS * 2 * HID])]
        w2 = [sb("w2_0", [P, EXPERTS * HID]), sb("w2_1", [P, EXPERTS * HID])]
        NB1, NB2 = EXPERTS * 2 * HID // P, EXPERTS * DIM // P
        bias_in = sb("bias_in", [P, NB1 + NB2])
        bias_left = sb("bias_left", [P, 2, NB1 + NB2])
        bias_parts = sb("bias_parts", [P, 3, NB1 + NB2], BF16)
        b1 = sb("b1", [3, EXPERTS * 2 * HID], BF16)
        b2 = sb("b2", [3, EXPERTS * DIM], BF16)

        bst = sb("bst", [P, TILES * 6])
        mv = sb("mv", [P, TILES * 2])
        bst2 = sb("bst2", [P, GROUP * 6])
        mv2 = sb("mv2", [P, GROUP * 2])
        vareps, rstd, mr, nbias = (sb(n, [P, TILES]) for n in ("vareps", "rstd", "mr", "nbias"))
        vareps2, rstd2, mr2, nbias2 = (sb(n, [P, TILES]) for n in ("vareps2", "rstd2", "mr2", "nbias2"))
        xn = sb("xn", [P, 2 * GW])
        xT = sb("xT", [P, TOKENS])

        xb = sb("xb", [P, BLOCK * DIM])
        qT = sb("qT", [P, 2 * P])
        mx = sb("mx", [P, 2 * HEADS])
        shifted = sb("shifted", [P, 2 * HK])
        probs = sb("probs", [P, 2 * HK])
        probsT = sb("probsT", [P, 2 * HK])
        rsum = sb("rsum", [P, 2 * HEADS])
        heads_out = sb("heads_out", [P, 2 * DIM])
        headsT = sb("headsT", [P, 2 * P])

        TE = TILES * EXPERTS
        lg = sb("lg", [P, TE])
        gexp = sb("gexp", [P, TILES])
        red = sb("red", [P, 8, TILES])
        tmp = sb("tmp", [P, TE])
        tmp2 = sb("tmp2", [P, TE])
        oh = [sb("oh0", [P, TE]), sb("oh1", [P, TE])]
        oh16 = sb("oh16", [P, TE], F16)
        tot = sb("tot", [P, TE])
        incl = sb("incl", [P, TE])
        slotmat = sb("slotmat", [P, TE])
        cmp = sb("cmp", [P, EXPERTS * TILES])
        etile = sb("etile", [P, 4, EXPERTS])
        cmpj = sb("cmpj", [P, MAXT * EXPERTS])
        etabf = sb("etabf", [P, MAXT])
        etab = [sb("etab0", [P, MAXT], I32), sb("etab1", [P, MAXT], I32)]
        gate = [sb("gate0", [P, TILES]), sb("gate1", [P, TILES])]
        slotf = sb("slotf", [P, 2 * TILES])
        slot = [sb("slots_0", [P, 2 * TILES], I32), sb("slots_1", [P, 2 * TILES], I32)]
        slot_r = sb("slot_r", [P, 2 * TILES], I32)
        slot_j = sb("slot_j", [P, 2 * TILES], I32)
        rowf = sb("rowf", [P, 2 * TILES])
        colf = sb("colf", [P, 2 * TILES])
        rowhot = xT[:, :].bitcast(F16)
        colhot = sb("colhot", [P, 2 * TILES * MAXT], F16)
        tabf = sb("tabf", [P, 3 * MAXT])
        gidx = [sb("gidx0", [P, MAXI], I32), sb("gidx1", [P, MAXI], I32)]
        sidx = [sb("sidx0", [P, MAXI], I32), sb("sidx1", [P, MAXI], I32)]

        idx_ring = sb("idx_ring", [P, 2 * BLOCK], I32)
        idx2_ring = sb("idx2_ring", [P, 2 * BLOCK], I32)
        rows = sb("rows", [P, BLOCK * 2 * DIM])
        slotsT = sb("slotsT", [P, 2 * P])
        sig, hid, hidT = shifted, probs, probsT
        xkeep = sb("xkeep", [P, BLOCK * DIM])
        yout = xb

        psA = ctx.enter_context(nc.psum_tensor("psA", [P, 4 * 512], F32))
        psB = ctx.enter_context(nc.psum_tensor("psB", [P, 2 * 512], F32))
        psX = ctx.enter_context(nc.psum_tensor("psX", [P, 512], F32))
        psL = ctx.enter_context(nc.psum_tensor("psL", [P, 512], F32))

        def ps_scores(r):
            return psA[:, r * 512:r * 512 + HK]

        def ps_probsT(r):
            return psA[:, (2 + r) * 512:(2 + r) * 512 + HK]

        ps_out = psB[:, 0:CH * VW]
        ps_oT, ps_y = psB[:, 512:512 + P], psB[:, 512 + P:512 + P + DIM]
        ps_xT, ps_q = psX[:, 0:P], psX[:, 0:P]
        ps_group = [psA[:, 0:512], psA[:, 512:2 * 512]]
        setup_banks = [psA[:, k * 512:k * 512 + P] for k in range(4)] + [psB[:, 0:P], psB[:, 512:512 + P],
                                                                         psX[:, 0:P], psL[:, 0:P]]


        in_x0, in_x1, in_ctx, in_w0, in_w1, in_b0, in_small = map(sem, (
            "in_x0", "in_x1", "in_ctx", "in_w0", "in_w1", "in_b0", "in_small"))
        in_e0, in_e1, in_bias, parts_out, parts_in = map(sem, (
            "in_e0", "in_e1", "in_bias", "parts_out", "parts_in"))
        consts, zeroed = sem("consts"), sem("zeroed")
        ps_set, sb_set = sem("ps_set"), sem("sb_set")
        kT_ready, rep_ready = sem("kT_ready"), sem("rep_ready")
        mask_ready, kbd_ready = sem("mask_ready"), [sem("kbd0_ready"), sem("kbd1_ready")]
        vaug_ready = [sem("vaug0_ready"), sem("vaug1_ready")]
        parts_ready, mrow_ready = sem("parts_ready"), sem("mrow_ready")
        vchain = sem("vchain")
        stat, mv_ready, pchain = sem("stat"), sem("mv_ready"), sem("pchain")
        nb_ready, xT_ps, xT_ready = sem("nb_ready"), sem("xT_ps"), sem("xT_ready")
        xn_ready = [sem("xn_ready_act"), sem("xn_ready_dve")]
        logit, x_mixed, x_half = sem("logit"), sem("x_mixed"), sem("x_half")
        y_in = [sem("y_in0"), sem("y_in1")]
        stored, stored_x = [sem("stored0"), sem("stored1")], sem("stored_x")
        names = ["q_ps", "qT", "s_ps", "mx", "sh", "p", "pT_ps", "pT", "o_ps", "rs", "o", "oT_ps", "oT", "y_ps",
                 "x1", "xb", "stat2", "mv2", "veps2", "rstd2", "mr2", "nb2"]
        A = {n: sem(n) for n in names}
        landed = sem("landed")
        fnames = ["idx", "idx2", "keep", "T_ps", "xT", "h_ps", "act", "hid", "hT_ps", "hT", "y_ps", "y"]
        F = [{n: sem(f"f_{n}_{L}") for n in fnames} for L in range(2)]
        gathered = [[sem(f"gathered{L}_{u}") for u in range(BLOCK)] for L in range(2)]
        written = [[sem(f"written{L}_{u}") for u in range(BLOCK)] for L in range(2)]
        R = [{n: sem(f"r_{n}_{L}") for n in ("gap", "exp", "onehot", "prefix", "hots", "table", "index", "experts", "sindex")}
             for L in range(2)]

        waited = {n: sem(f"waited_{n}") for n in ("gpsimd", "vector")}
        makers = {
            "gpsimd": ("xb", "veps2", "rstd2", "mr2", "nb2"),
            "scalar": ("qT", "p", "pT", "oT"),
            "tensor": ("q_ps", "s_ps", "pT_ps", "o_ps", "oT_ps", "y_ps"),
            "vector": ("mx", "sh", "rs", "o", "x1", "stat2", "mv2"),
        }
        expert_makers = {
            "gpsimd": (("idx", "idx2"), ("idx", "idx2")), "tensor": (("T_ps", "h_ps", "hT_ps", "y_ps"),) * 2,
            "scalar": (("xT", "hid", "y"), ("xT", "act", "hT", "keep")), "vector": (("hT",), ("hid", "y")),
        }

        def give_credit(eng, name):
            for n in makers[name]:
                eng.sem_inc(A[n], CREDIT)
            for L in range(2):
                for n in expert_makers[name][L]:
                    eng.sem_inc(F[L][n], CREDIT)

        block = ctx.enter_context(nc.Block())

        @block.sync
        def _(sp):
            sp.sem_inc(landed, CREDIT)
            xr = a["x"].rearrange("b (t p) d -> p (b t) d", p=P)
            xv = x[:, :].rearrange("p (t d) -> p t d", d=DIM)
            sp.dma_start(ctx_sb[:, :], a["ctx_1024"].rearrange("b s d -> (b s) d")).then_inc(in_ctx, 16)
            sp.dma_start(xv[:, 0:GROUP, :], xr[:, 0:GROUP, :]).then_inc(in_x0, 16)
            for t, n in ((wk, "Wk"), (wv, "Wv"), (wq, "Wq"), (wo, "Wo")):
                sp.dma_start(t[0][:, :], a[f"L0_xattn_{n}"]).then_inc(in_w0, 16)
            sp.dma_start(xv[:, GROUP:, :], xr[:, GROUP:, :]).then_inc(in_x1, 16)
            for k, n in enumerate(("Wq", "Wk", "Wv", "Wo")):
                sp.dma_start(wload[:, k * DIM:(k + 1) * DIM], a[f"L1_xattn_{n}"]).then_inc(in_w1, 16)
            sp.dma_start(rw_in[:, :], a["L0_ffn_router_w"]).then_inc(in_w1, 16)
            sp.dma_start(bias_in[:, 0:NB1], a["L1_ffn_b1"].rearrange("e (q n) -> (e q) n", n=NB1)).then_inc(in_bias, 16)
            sp.dma_start(bias_in[:, NB1:], a["L1_ffn_b2"].rearrange("e (q n) -> (e q) n", n=NB2)).then_inc(in_bias, 16)
            for L, s_in in ((0, in_e0), (1, in_e1)):
                n1 = HID * (L + 1)
                sp.dma_start(w1[L][:, :].rearrange("p (e n) -> p e n", n=n1),
                             a[f"L{L}_ffn_w1"].rearrange("e c n -> c e n")).then_inc(s_in, 16)
                sp.dma_start(w2[L][:, :].rearrange("p (k d) -> p k d", d=DIM),
                             a[f"L{L}_ffn_w2"].rearrange("e (c p) d -> p (e c) d", p=P)).then_inc(s_in, 16)
            y_rows = y_dram.rearrange("(k g t p) d -> p k g t d", p=P, t=GROUP, g=GROUPS)
            for L in range(2):
                if L == 1:
                    sp.wait_ge(vaug_ready[1], 2 * BATCH)
                    for g in range(GROUPS):
                        positive(sp, x_mixed, GROUP * (g - 1))
                        for k in range(2):
                            sp.dma_start(ybuf[:, ((g % 2) * 2 + k) * GW:((g % 2) * 2 + k + 1) * GW]
                                         .rearrange("p (t d) -> p t d", d=DIM), y_rows[:, k, g]).then_inc(y_in[g % 2], 16)
                    sp.wait_ge(parts_ready, 1)
                    sp.dma_start(b1_dram.rearrange("k (p n) -> p k n", p=P), bias_parts[:, :, 0:NB1]).then_inc(parts_out, 16)
                    sp.dma_start(b2_dram.rearrange("k (p n) -> p k n", p=P), bias_parts[:, :, NB1:]).then_inc(parts_out, 16)
                    sp.wait_ge(parts_out, 32)
                    sp.dma_start(b1[:, :], b1_dram).then_inc(parts_in, 16)
                    sp.dma_start(b2[:, :], b2_dram).then_inc(parts_in, 16)
                dst = xn_dram if L == 0 else xx_dram[:, 0:DIM]
                for g in range(GROUPS):
                    if L == 1:
                        ready(sp, A["x1"], TILES + GROUP * (g + 1))
                        sp.dma_start(xx_dram[g * GW:(g + 1) * GW, DIM:].rearrange("(t p) d -> p t d", p=P),
                                     xv[:, g * GROUP:(g + 1) * GROUP, :]).then_inc(stored_x, 16)
                    for h in range(2):
                        sp.wait_ge(xn_ready[h], (TILES * (2 * L + 1) + GROUP * (g + 1)) // 2)
                    sp.dma_start(dst[g * GW:(g + 1) * GW, :].rearrange("(t p) d -> p t d", p=P),
                                 xn[:, (g % 2) * GW:(g % 2 + 1) * GW].rearrange("p (t d) -> p t d", d=DIM)
                                 ).then_inc(stored[g % 2], 16)
                def landed_rows(j, u, g):
                    sp.wait_ge(written[L][u], 16 * (g + 1))
                    sp.sem_inc(landed, 1)
                pipelined(sp, SLOT_TILES[L], [(0, landed_rows)])

        @block.gpsimd
        def _(pool):
            give_credit(pool, "gpsimd")
            pool.memset(ident[:, :], 0.0).then_inc(zeroed, 1)
            pool.memset(headmask[:, :], 1.0).then_inc(zeroed, 1)
            pool.memset(groupmask[:, :], 1.0).then_inc(zeroed, 1)
            pool.memset(before[:, :], 1.0).then_inc(zeroed, 1)
            pool.memset(carry[:, :], 1.0).then_inc(zeroed, 1)
            pool.memset(ones16[:, :], 1.0).then_inc(consts, 1)
            pool.memset(onesb[:, :], 1.0).then_inc(consts, 1)
            pool.memset(ones8[:, :], 1.0).then_inc(consts, 1)
            pool.memset(minus_half[:, :], -0.5).then_inc(consts, 1)
            pool.memset(eps[:, :], EPS).then_inc(consts, 1)
            pool.memset(minus_one[:, :], -1.0).then_inc(consts, 1)
            for t in (*gidx, *sidx):
                pool.memset(t[:, :], 0).then_inc(consts, 1)
            pool.wait_ge(zeroed, 5)
            pool.affine_select(out=ident[:, :], in_=ident[:, :], compare_op=ALU.not_equal, fill=1.0, base=0,
                               pattern=[[-1, P]], channel_multiplier=1).then_inc(consts, 1)
            for m, n, w in ((headmask, HEADS, HD), (groupmask, HPC, KEYS)):
                pool.affine_select(out=m[:, :], in_=m[:, :], compare_op=ALU.is_ge, fill=0.0, base=0,
                                   pattern=[[-w, n]], channel_multiplier=1).then_inc(zeroed, 1)
            pool.wait_ge(zeroed, 7)
            for m, n, w in ((headmask, HEADS, HD), (groupmask, HPC, KEYS)):
                pool.affine_select(out=m[:, :], in_=m[:, :], compare_op=ALU.is_ge, fill=0.0, base=w - 1,
                                   pattern=[[w, n]], channel_multiplier=-1).then_inc(consts, 1)
            pool.affine_select(out=before[:, :], in_=before[:, :], compare_op=ALU.is_gt, fill=0.0, base=0,
                               pattern=[[1, P]], channel_multiplier=-1).then_inc(consts, 1)
            pool.affine_select(out=carry[:, :], in_=carry[:, :], compare_op=ALU.not_equal, fill=0.0, base=0,
                               pattern=[[0, EXPERTS], [1, TILES]], channel_multiplier=0).then_inc(consts, 1)
            for t, pat, base, cm in (
                    (iota_row, [[1, P]], 0, 0), (iota_tiles, [[1, MAXT]], 0, 0), (tile_no, [[1, MAXT]], 0, 0),
                    (prefer, [[-1, EXPERTS]], EXPERTS, 0), (steps128, [[P, TILES]], 0, 0),
                    (token1[:, 0:TILES], [[P, TILES]], 1, 1), (token1[:, TILES:], [[-P, TILES]], -1, -1)):
                pool.iota(t[:, :], pat, base=base, channel_multiplier=cm,
                          allow_small_or_imprecise_dtypes=True).then_inc(consts, 1)
            def spread_keys(L, first):
                for b in range(first, BATCH):
                    pool.tensor_tensor(kbd[L][:, b * HK:(b + 1) * HK].rearrange("p (h k) -> p h k", h=HEADS),
                                       kT[L][:, b * KEYS:(b + 1) * KEYS].unsqueeze(1).to_broadcast([P, HEADS, KEYS]),
                                       headmask[:, :].unsqueeze(2).to_broadcast([P, HEADS, KEYS]),
                                       ALU.mult).then_inc(kbd_ready[L], 1)

            links = [0]

            def link(ins):
                links[0] += 1
                ins.then_inc(pchain, 1)
                pool.wait_ge(pchain, links[0])

            for L in range(2):
                D, N0 = A, L * TILES

                def norm_terms(g):
                    c = slice(g * GROUP, (g + 1) * GROUP)
                    m = mv[:, :].rearrange("p (t k) -> p k t", k=2)
                    pool.wait_ge(mv_ready, N0 + GROUP * (g + 1))
                    link(pool.tensor_tensor(vareps[:, c], m[:, 1, c], eps[:, :].to_broadcast([P, GROUP]), ALU.add))
                    link(pool.tensor_tensor(rstd[:, c], vareps[:, c], minus_half[:, :].to_broadcast([P, GROUP]), ALU.pow))
                    link(pool.tensor_tensor(mr[:, c], m[:, 0, c], rstd[:, c], ALU.mult))
                    pool.tensor_tensor(nbias[:, c], mr[:, c], minus_one[:, :].to_broadcast([P, GROUP]), ALU.mult
                                       ).then_inc(nb_ready, 1)

                def residual(i, u, g):
                    free(pool, D["x1"], N0 + i + 1 - BLOCK)
                    pool.tensor_tensor(xb[:, u * DIM:(u + 1) * DIM], cols(x, i), bo[L][:, :], ALU.add
                                       ).then_inc(D["xb"], 1)

                def norm_terms2(i, u, g):
                    if u != GROUP - 1:
                        return
                    G0 = L * GROUPS
                    c = bass.ds(g * GROUP, GROUP)
                    m = mv2[:, :].rearrange("p (t k) -> p k t", k=2)
                    ready(pool, D["mv2"], N0 + i + 1)
                    pool.tensor_tensor(vareps2[:, c], m[:, 1, :], eps[:, :].to_broadcast([P, GROUP]), ALU.add
                                       ).then_inc(D["veps2"], 1)
                    ready(pool, D["veps2"], G0 + g + 1)
                    pool.tensor_tensor(rstd2[:, c], vareps2[:, c], minus_half[:, :].to_broadcast([P, GROUP]), ALU.pow
                                       ).then_inc(D["rstd2"], 1)
                    ready(pool, D["rstd2"], G0 + g + 1)
                    pool.tensor_tensor(mr2[:, c], m[:, 0, :], rstd2[:, c], ALU.mult).then_inc(D["mr2"], 1)
                    ready(pool, D["mr2"], G0 + g + 1)
                    pool.tensor_tensor(nbias2[:, c], mr2[:, c], minus_one[:, :].to_broadcast([P, GROUP]), ALU.mult
                                       ).then_inc(D["nb2"], 1)

                if L == 0:
                    pool.wait_ge(kT_ready, 1)
                    spread_keys(0, 1)
                for g in range(GROUPS):
                    norm_terms(g)
                pool.wait_ge(mv_ready, N0 + TILES)
                if L == 0:
                    pool.wait_ge(in_b0, 16 * 4)
                pipelined(pool, TILES, [(1, residual), (4, norm_terms2)])
                if L == 0:
                    pool.wait_ge(in_small, 16 * 7)
                    pool.tensor_copy(maskf[:, :], mask8[:, :]).then_inc(mask_ready, 1)
                    pool.wait_ge(mask_ready, 1)
                    pool.tensor_scalar(maskrow[0:1, :].rearrange("p (b h k) -> p b h k", b=BATCH, h=HEADS),
                                       maskf[0:1, :].rearrange("p (b k) -> p b k", b=BATCH).unsqueeze(2)
                                       .to_broadcast([1, BATCH, HEADS, KEYS]),
                                       -1.0, -FILL, ALU.add, ALU.mult).then_inc(mrow_ready, 1)

                NT = SLOT_TILES[L]
                pool.wait_ge(R[L]["index"], 1)
                for u in range(2):
                    pool.wait_ge(stored[u], 16 * 2 * (L + 1))
                if L == 1:
                    pool.wait_ge(stored_x, 16 * GROUPS)
                W = (L + 1) * DIM
                src = xn_dram if L == 0 else xx_dram

                def fetch(name, ring, table, j, u, g):
                    if u % 4 == 0:
                        pool.tensor_copy(ring[:, u:u + 4], table[:, bass.ds(j, 4)]).then_inc(F[L][name], 1)
                    return 2 * g + u // 4 + 1

                def gather(j, u, g):
                    v = u % BLOCK
                    free(pool, F[L]["T_ps"], j + 1 - BLOCK)
                    if L == 1:
                        free(pool, F[L]["keep"], j + 1 - BLOCK)
                    fetched = fetch("idx", idx_ring, gidx[L], j, u, g)
                    ready(pool, F[L]["idx"], fetched)
                    settle(pool, waited["gpsimd"])
                    pool.indirect_dma_start(rows[:, v * W:(v + 1) * W], None, src,
                                            bass.IndirectOffsetOnAxis(ap=idx_ring[:, u:u + 1], axis=0)
                                            ).then_inc(gathered[L][v], 16)

                dst, rows_out = (y_dram, 2 * TOKENS) if L == 0 else (out_rows, TOKENS)
                last_row = pool.to_reg(rows_out - 1)

                def scatter(j, u, g):
                    v = u % BLOCK
                    if isinstance(j, int) and j == 0:
                        pool.wait_ge(R[L]["sindex"], 1)
                    ready(pool, F[L]["y"], j + 1)
                    fetched = fetch("idx2", idx2_ring, sidx[L], j, u, g)
                    ready(pool, F[L]["idx2"], fetched)
                    settle(pool, waited["gpsimd"])
                    pool.indirect_dma_start(dst, bass.IndirectOffsetOnAxis(ap=idx2_ring[:, u:u + 1], axis=0),
                                            yout[:, v * DIM:(v + 1) * DIM], None,
                                            bounds_check=last_row, oob_is_err=False
                                            ).then_inc(written[L][v], 16)

                pipelined(pool, NT, [(0, gather), (6, scatter)], block=2 * BLOCK)
                if L == 0:
                    pool.wait_ge(kT_ready, 2)
                    spread_keys(1, 0)

        @block.scalar
        def _(act):
            def row(ap):
                return ap.rearrange("(a n) -> a n", a=1).partition_broadcast(P).rearrange("p a n -> p (a n)")

            def column(ap):
                return ap.rearrange("(p a) -> p a", a=1)

            for L, s_in in ((0, in_b0), (1, in_small)):
                act.dma_start(bk[L][:, :], column(a[f"L{L}_xattn_bk"])).then_inc(s_in, 16)
                act.dma_start(bv[L][:, :], row(a[f"L{L}_xattn_bv"])).then_inc(s_in, 16)
                act.dma_start(bq[L][:, :], column(a[f"L{L}_xattn_bq"])).then_inc(s_in, 16)
                act.dma_start(bo[L][:, :], row(a[f"L{L}_xattn_bo"])).then_inc(s_in, 16)
            act.dma_start(rb[:, :], row(a["L1_ffn_router_b"])).then_inc(in_small, 16)
            act.dma_start(rw[1][:, :], a["L1_ffn_router_w"]).then_inc(in_small, 16)
            act.dma_start(mask8[:, :], row(a["mask_BxS2_bf1"].rearrange("b k -> (b k)"))).then_inc(in_small, 16)
            give_credit(act, "scalar")

            for L in range(2):
                D, N0 = A, L * TILES

                def normalise(n, rs, nb):
                    def emit(g):
                        if n % 2 == 0:
                            act.wait_ge(nb_ready, L * GROUPS + g + 1)
                        else:
                            ready(act, D["nb2"], L * GROUPS + g + 1)
                        positive(act, xT_ps, GROUPS * n + g - 1)
                        if g >= 2 and n % 2:
                            act.wait_ge(stored[g % 2], 16 * (2 * L + g // 2))
                        for t in range(GROUP // 2):
                            i = g * GROUP + t
                            act.activation(xn[:, ((g % 2) * GROUP + t) * P:((g % 2) * GROUP + t + 1) * P],
                                           x[:, i * DIM:(i + 1) * DIM], ACT.Identity, bias=nb[:, i:i + 1],
                                           scale=rs[:, i:i + 1]).then_inc(xn_ready[0], 1)
                    return emit

                def evac_x(n):
                    def emit(g):
                        act.wait_ge(xT_ps, GROUPS * n + g + 1)
                        act.activation(xT[:, g * GW:(g + 1) * GW], ps_group[g % 2], ACT.Copy).then_inc(xT_ready, 1)
                    return emit

                def evac_q(i, u, g):
                    r = u % 2
                    ready(act, D["q_ps"], N0 + i + 1)
                    free(act, D["s_ps"], N0 + i - 1)
                    act.activation(qT[:, r * P:(r + 1) * P], ps_q, ACT.Identity, bias=bq[L][:, 0:1]).then_inc(D["qT"], 1)

                def exp(i, u, g):
                    r = u % 2
                    ready(act, D["sh"], N0 + i + 1)
                    free(act, D["pT_ps"], N0 + i - 1)
                    act.activation(probs[:, r * HK:(r + 1) * HK], shifted[:, r * HK:(r + 1) * HK], ACT.Exp,
                                   scale=SCALE).then_inc(D["p"], 1)

                def evac_p(i, u, g):
                    r = u % 2
                    ready(act, D["pT_ps"], N0 + i + 1)
                    free(act, D["o_ps"], N0 + i - 1)
                    act.activation(probsT[:, r * HK:(r + 1) * HK], ps_probsT(r), ACT.Copy
                                   ).then_inc(D["pT"], 1)

                def evac_o(i, u, g):
                    r = u % 2
                    ready(act, D["oT_ps"], N0 + i + 1)
                    free(act, D["y_ps"], N0 + i - 1)
                    act.activation(headsT[:, r * P:(r + 1) * P], ps_oT, ACT.Copy).then_inc(D["oT"], 1)

                skewed(GROUPS, [(0, normalise(2 * L, rstd, nbias)), (1, evac_x(2 * L))])
                if L == 0:
                    act.wait_ge(in_b0, 16 * 4)
                norm, evac = normalise(2 * L + 1, rstd2, nbias2), evac_x(2 * L + 1)

                def normalise_rest(k):
                    norm(k)
                    if k:
                        evac(k - 1)
                pipelined(act, TILES, [(4, evac_o), (0, evac_q), (1, exp), (2, evac_p)], tail=normalise_rest)
                evac(GROUPS - 1)

                if L == 0:
                    act.wait_ge(R[L]["gap"], 1)
                    act.activation(gexp[:, :], tmp[:, 0:TILES], ACT.Exp).then_inc(R[L]["exp"], 1)

                NT = SLOT_TILES[L]
                E = F[L]

                def gelu(j, u, g):
                    r = u % 2
                    ready(act, E["h_ps"], j + 1)
                    free(act, E["hT_ps"], j - 1)
                    act.activation(hid[:, r * HID:(r + 1) * HID], psA[:, r * 512:r * 512 + HID], ACT.Gelu
                                   ).then_inc(E["hid"], 1)

                def sigmoid(j, u, g):
                    r = u % 2
                    ready(act, E["h_ps"], j + 1)
                    free(act, E["hid"], j - 1)
                    act.activation(sig[:, r * HID:(r + 1) * HID], psA[:, (2 * r + 1) * 512:(2 * r + 2) * 512],
                                   ACT.Sigmoid).then_inc(E["act"], 1)

                def evac_slots(j, u, g):
                    r = u % 2
                    ready(act, E["T_ps"], j + 1)
                    free(act, E["h_ps"], j - 1)
                    act.activation(slotsT[:, r * P:(r + 1) * P], ps_xT, ACT.Copy).then_inc(E["xT"], 1)

                def evac_y(j, u, g):
                    r = u % 2
                    ready(act, E["y_ps"], j + 1)
                    free(act, landed, j + 1 - BLOCK)
                    act.activation(yout[:, u * DIM:(u + 1) * DIM], psL[:, 0:DIM], ACT.Copy
                                   ).then_inc(E["y"], 1)

                def keep_x(j, u, g):
                    act.wait_ge(gathered[L][u], 16 * (g + 1))
                    free(act, E["y"], j + 1 - BLOCK)
                    act.activation(xkeep[:, u * DIM:(u + 1) * DIM], rows[:, (2 * u + 1) * DIM:(2 * u + 2) * DIM],
                                   ACT.Copy).then_inc(E["keep"], 1)

                def evac_h(j, u, g):
                    r = u % 2
                    ready(act, E["hT_ps"], j + 1)
                    free(act, E["y_ps"], j - 1)
                    act.activation(hidT[:, r * HID:(r + 1) * HID], psB[:, r * 512:r * 512 + HID], ACT.Copy
                                   ).then_inc(E["hT"], 1)

                if L == 0:
                    pipelined(act, NT, [(0, evac_slots), (1, gelu), (3, evac_y)])
                else:
                    pipelined(act, NT, [(0, evac_slots), (1, sigmoid), (1, keep_x), (2, evac_h)])

        @block.vector
        def _(dve):
            give_credit(dve, "vector")
            links = [0]

            def link(ins):
                links[0] += 1
                ins.then_inc(vchain, 1)
                dve.wait_ge(vchain, links[0])

            V = nc.vector

            evac = [0]

            def setup_evac(make):
                bank = setup_banks[evac[0] % 8]
                evac[0] += 1
                dve.wait_ge(ps_set, evac[0])
                make(bank).then_inc(sb_set, 1)

            def setup_keys_values(L):
                setup_evac(lambda ps: V.tensor_scalar(kT[L][:, :], ps, bk[L][:, 0:1], None, ALU.add))
                if L == 1:
                    dve.wait_ge(sb_set, evac[0])
                    dve.wait_ge(mask_ready, 1)
                    link(V.tensor_tensor(kT[1][:, :], kT[1][:, :], maskf[:, :], ALU.mult))
                    dve.sem_inc(kT_ready, 1)
                else:
                    dve.wait_ge(sb_set, evac[0])
                    dve.sem_inc(kT_ready, 1)
                    V.tensor_tensor(kbd[L][:, 0:HK].rearrange("p (h k) -> p h k", h=HEADS),
                                    kT[L][:, 0:KEYS].unsqueeze(1).to_broadcast([P, HEADS, KEYS]),
                                    headmask[:, :].unsqueeze(2).to_broadcast([P, HEADS, KEYS]),
                                    ALU.mult).then_inc(kbd_ready[L], 1)
                for b in range(BATCH):
                    setup_evac(lambda ps: V.tensor_tensor(vrows[:, b * DIM:(b + 1) * DIM], ps, bv[L][:, :], ALU.add))
                dve.wait_ge(sb_set, evac[0])
                va = vaug[L][:, :].rearrange("p (b h d) -> p b h d", b=BATCH, h=HEADS)
                for b in range(BATCH):
                    vc = va[:, b].rearrange("p (c h) d -> p c h d", c=CH)
                    vr = vrows[:, b * DIM:(b + 1) * DIM].rearrange("p (c h d) -> p c h d", c=CH, h=HPC)
                    V.tensor_tensor(vc[:, :, :, 0:HD], vr,
                                    groupmask[:, :].unsqueeze(1).unsqueeze(3).to_broadcast([P, CH, HPC, HD]),
                                    ALU.mult).then_inc(vaug_ready[L], 1)
                    V.tensor_copy(vc[:, :, :, HD], groupmask[:, :].unsqueeze(1).to_broadcast([P, CH, HPC])
                                  ).then_inc(vaug_ready[L], 1)

            def setup_layer1():
                dve.wait_ge(in_small, 16 * 7)
                for k, t in enumerate((wq, wk, wv, wo)):
                    setup_evac(lambda ps: V.tensor_copy(t[1][:, :], ps))
                setup_keys_values(1)
                dve.wait_ge(in_bias, 32)
                left = bias_in[:, :]
                for k in range(3):
                    link(V.tensor_copy(bias_parts[:, k, :], left))
                    if k < 2:
                        link(V.tensor_tensor(bias_left[:, k, :], left, bias_parts[:, k, :], ALU.subtract))
                        left = bias_left[:, k, :]
                dve.sem_inc(parts_ready, 1)

            def stats(L, g):
                tiles = range(g * GROUP, (g + 1) * GROUP)
                if L == 1:
                    dve.wait_ge(y_in[g % 2], 32 * (g // 2 + 1))
                    for k in range(2):
                        for t, i in enumerate(tiles):
                            xi = x[:, i * DIM:(i + 1) * DIM]
                            if k == 1:
                                dve.wait_ge(x_half, i + 1)
                            V.scalar_tensor_tensor(xi, ybuf[:, (((g % 2) * 2 + k) * GROUP + t) * DIM:
                                                            (((g % 2) * 2 + k) * GROUP + t + 1) * DIM],
                                                   gate[k][:, i:i + 1], xi, ALU.mult, ALU.add
                                                   ).then_inc((x_half, x_mixed)[k], 1)
                    dve.wait_ge(x_mixed, (g + 1) * GROUP)
                else:
                    dve.wait_ge(in_x0 if g == 0 else in_x1, 16)
                for i in tiles:
                    V.bn_stats(bst[:, 6 * i:6 * i + 6], x[:, i * DIM:(i + 1) * DIM]).then_inc(stat, 1)
                dve.wait_ge(stat, L * TILES + (g + 1) * GROUP)
                for i in tiles:
                    V.bn_aggr(mv[:, 2 * i:2 * i + 2], bst[:, 6 * i:6 * i + 6]).then_inc(mv_ready, 1)

            def normalise_half(n, rs, nb):
                def emit(g):
                    L = n // 2
                    if n % 2 == 0:
                        dve.wait_ge(nb_ready, L * GROUPS + g + 1)
                    else:
                        ready(dve, A["nb2"], L * GROUPS + g + 1)
                    positive(dve, xT_ps, GROUPS * n + g - 1)
                    if g >= 2 and n % 2:
                        dve.wait_ge(stored[g % 2], 16 * (2 * L + g // 2))
                    for t in range(GROUP // 2, GROUP):
                        i = g * GROUP + t
                        V.tensor_scalar(xn[:, ((g % 2) * GROUP + t) * P:((g % 2) * GROUP + t + 1) * P],
                                        x[:, i * DIM:(i + 1) * DIM], rs[:, i:i + 1], nb[:, i:i + 1],
                                        ALU.mult, ALU.add).then_inc(xn_ready[1], 1)
                return emit

            setup_evac(lambda ps: V.tensor_copy(ctxT[:, :], ps))
            dve.wait_ge(sb_set, 1)
            V.tensor_copy(ctxrep[:, :].rearrange("p (b r k) -> p b r k", b=BATCH, r=HPC),
                          ctxT[:, :].rearrange("p (b k) -> p b k", b=BATCH).unsqueeze(2)
                          .to_broadcast([P, BATCH, HPC, KEYS])).then_inc(rep_ready, 1)
            stats(0, 0)
            dve.wait_ge(in_b0, 16 * 4)
            setup_keys_values(0)
            setup_evac(lambda ps: V.tensor_copy(rw[0][:, :], ps[:, 0:EXPERTS]))

            for L in range(2):
                D, N0 = A, L * TILES
                if L == 1:
                    setup_layer1()
                half = normalise_half(2 * L, rstd, nbias)
                for g in range(GROUPS):
                    if L or g:
                        stats(L, g)
                    if g:
                        half(g - 1)
                half(GROUPS - 1)
                def shift(i, u, g):
                    r = u % 2
                    sc = ps_scores(r).rearrange("p (h k) -> p h k", h=HEADS)
                    ready(dve, D["s_ps"], N0 + i + 1)
                    V.tensor_reduce(mx[:, r * HEADS:(r + 1) * HEADS], sc, axis=AX, op=ALU.max).then_inc(D["mx"], 1)
                    ready(dve, D["mx"], N0 + i + 1)
                    free(dve, D["p"], N0 + i - 1)
                    V.tensor_tensor(shifted[:, r * HK:(r + 1) * HK].rearrange("p (h k) -> p h k", h=HEADS), sc,
                                    mx[:, r * HEADS:(r + 1) * HEADS].unsqueeze(2).to_broadcast([P, HEADS, KEYS]),
                                    ALU.subtract).then_inc(D["sh"], 1)

                def normalise(i, u, g):
                    r = u % 2
                    po = ps_out.rearrange("p (h d) -> p h d", h=HEADS)
                    ready(dve, D["o_ps"], N0 + i + 1)
                    V.reciprocal(rsum[:, r * HEADS:(r + 1) * HEADS], po[:, :, HD]).then_inc(D["rs"], 1)
                    ready(dve, D["rs"], N0 + i + 1)
                    free(dve, D["oT_ps"], N0 + i - 1)
                    V.tensor_tensor(heads_out[:, r * DIM:(r + 1) * DIM].rearrange("p (h d) -> p h d", h=HEADS),
                                    po[:, :, 0:HD],
                                    rsum[:, r * HEADS:(r + 1) * HEADS].unsqueeze(2).to_broadcast([P, HEADS, HD]),
                                    ALU.mult).then_inc(D["o"], 1)

                def add(i, u, g):
                    ready(dve, D["y_ps"], N0 + i + 1)
                    ready(dve, D["xb"], N0 + i + 1)
                    V.tensor_tensor(cols(x, i), ps_y, xb[:, u * DIM:(u + 1) * DIM], ALU.add).then_inc(D["x1"], 1)
                    ready(dve, D["x1"], N0 + i + 1)
                    if u == 0:
                        free(dve, D["mr2"], L * GROUPS + g)
                    settle(dve, waited["vector"])
                    V.bn_stats(bst2[:, 6 * u:6 * u + 6], cols(x, i)).then_inc(D["stat2"], 1)
                    ready(dve, D["stat2"], N0 + i + 1)
                    settle(dve, waited["vector"])
                    V.bn_aggr(mv2[:, 2 * u:2 * u + 2], bst2[:, 6 * u:6 * u + 6]).then_inc(D["mv2"], 1)

                pipelined(dve, TILES, [(1, shift), (3, normalise), (4, add)],
                          tail=normalise_half(2 * L + 1, rstd2, nbias2))

                K = TOPK[L]
                NT = SLOT_TILES[L]

                def te(t):
                    return t.rearrange("p (t e) -> p t e", e=EXPERTS)

                def et(t):
                    return t.rearrange("p (e t) -> p e t", t=TILES)

                def over_e(t):
                    return t.unsqueeze(2).to_broadcast([P, TILES, EXPERTS])

                SUM, RM = red[:, 0, :], red[:, 1, :]
                dve.wait_ge(logit, N0 + TILES)
                if L == 0:
                    link(V.tensor_copy(lg[:, :], psL[:, 0:TE]))
                else:
                    link(V.tensor_tensor(te(lg[:, :]), te(psL[:, 0:TE]),
                                         rb[:, :].unsqueeze(1).to_broadcast([P, TILES, EXPERTS]), ALU.add))
                tops = [red[:, 4, :], red[:, 5, :]]
                for k in range(K):
                    link(V.tensor_reduce(tops[k], te(lg[:, :]), axis=AX, op=ALU.max))
                    link(V.tensor_tensor(te(tmp[:, :]), te(lg[:, :]), over_e(tops[k]), ALU.is_equal))
                    link(V.tensor_tensor(te(tmp2[:, :]), te(tmp[:, :]),
                                         prefer[:, :].unsqueeze(1).to_broadcast([P, TILES, EXPERTS]), ALU.mult))
                    link(V.tensor_reduce(RM, te(tmp2[:, :]), axis=AX, op=ALU.max))
                    link(V.tensor_tensor(te(oh[k][:, :]), te(tmp2[:, :]), over_e(RM), ALU.is_equal))
                    if k + 1 < K:
                        link(V.scalar_tensor_tensor(lg[:, :], oh[k][:, :], -3e38, lg[:, :], ALU.mult, ALU.add))
                if K == 2:
                    link(V.tensor_tensor(oh16[:, :], oh[0][:, :], oh[1][:, :], ALU.add))
                else:
                    link(V.tensor_copy(oh16[:, :], oh[0][:, :]))
                dve.sem_inc(R[L]["onehot"], 1)
                if K == 2:
                    V.tensor_tensor(tmp[:, 0:TILES], tops[1], tops[0], ALU.subtract).then_inc(R[L]["gap"], 1)
                    dve.wait_ge(R[L]["exp"], 1)
                    link(V.tensor_scalar(SUM, gexp[:, :], 1.0, None, ALU.add))
                    link(V.reciprocal(gate[0][:, :], SUM))
                    link(V.tensor_tensor(gate[1][:, :], gexp[:, :], gate[0][:, :], ALU.mult))
                dve.wait_ge(R[L]["prefix"], 1)
                link(V.tensor_copy(et(tot[:, :]), psL[:, 256:256 + TE].rearrange("p (t e) -> p e t", e=EXPERTS)))
                link(V.tensor_tensor_scan(incl[:, :], carry[:, :], tot[:, :], 0.0, ALU.mult, ALU.add))
                count = et(incl[:, :])[:, :, TILES - 1]
                link(V.tensor_tensor(et(cmp[:, :]), count.unsqueeze(2).to_broadcast([P, EXPERTS, TILES]),
                                     steps128[:, :].unsqueeze(1).to_broadcast([P, EXPERTS, TILES]), ALU.is_gt))
                ntile, upto, base = (etile[:, k, :] for k in range(3))
                link(V.tensor_reduce(ntile, et(cmp[:, :]), axis=AX, op=ALU.add))
                link(V.tensor_tensor_scan(upto, ones8[:, :], ntile, 0.0, ALU.mult, ALU.add))
                link(V.tensor_tensor(base, upto, ntile, ALU.subtract))
                link(V.tensor_tensor(tot[:, :], incl[:, :], tot[:, :], ALU.subtract))
                link(V.scalar_tensor_tensor(et(incl[:, :]), base.unsqueeze(2).to_broadcast([P, EXPERTS, TILES]),
                                            float(P), et(tot[:, :]), ALU.mult, ALU.add))
                link(V.tensor_tensor(te(slotmat[:, :]), te(psL[:, 128:128 + TE]),
                                     incl[:, :].rearrange("p (e t) -> p t e", t=TILES), ALU.add))
                for k in range(K):
                    link(V.tensor_tensor(tmp[:, :], slotmat[:, :], oh[k][:, :], ALU.mult))
                    link(V.tensor_reduce(slotf[:, k * TILES:(k + 1) * TILES], te(tmp[:, :]), axis=AX, op=ALU.add))
                KT = K * TILES
                link(V.tensor_copy(slot[L][:, 0:KT], slotf[:, 0:KT]))
                V.tensor_scalar(slot_r[:, 0:KT], slot[L][:, 0:KT], P - 1, None, ALU.bitwise_and)
                link(V.tensor_scalar(slot_j[:, 0:KT], slot[L][:, 0:KT], 7, None, ALU.logical_shift_right))
                V.tensor_copy(rowf[:, 0:KT], slot_r[:, 0:KT])
                link(V.tensor_copy(colf[:, 0:KT], slot_j[:, 0:KT]))
                col3 = colhot[:, 0:KT * NT].rearrange("p (q j) -> p q j", j=NT)
                link(V.tensor_tensor(col3, iota_tiles[:, 0:NT].unsqueeze(1).to_broadcast([P, KT, NT]),
                                     colf[:, 0:KT].unsqueeze(2).to_broadcast([P, KT, NT]), ALU.is_equal))
                link(V.tensor_tensor(col3, col3, token1[:, 0:KT].unsqueeze(2).to_broadcast([P, KT, NT]), ALU.mult))
                for q in range(KT):
                    V.tensor_scalar(rowhot[:, q * P:(q + 1) * P], iota_row[:, :], rowf[:, q:q + 1], None,
                                    ALU.is_equal).then_inc(R[L]["hots"], 1)
                rows_out = K * TOKENS
                dve.wait_ge(R[L]["table"], 1)
                tab, mag, pad = (tabf[:, k * MAXT:k * MAXT + NT] for k in range(3))
                link(V.tensor_copy(tab, psL[:, 384:384 + NT]))
                link(V.scalar_tensor_tensor(mag, tab, -1.0, tab, ALU.mult, ALU.max))
                link(V.tensor_scalar(gidx[L][:, 0:NT], mag, -1.0, 0.0, ALU.add, ALU.max))
                dve.sem_inc(R[L]["index"], 1)
                cj = cmpj[:, 0:NT * EXPERTS].rearrange("p (j e) -> p j e", e=EXPERTS)
                link(V.tensor_tensor(cj, upto.unsqueeze(1).to_broadcast([P, NT, EXPERTS]),
                                     tile_no[:, 0:NT].unsqueeze(2).to_broadcast([P, NT, EXPERTS]), ALU.is_le))
                link(V.tensor_reduce(etabf[:, 0:NT], cj, axis=AX, op=ALU.add))
                link(V.tensor_scalar(etab[L][:, 0:NT], etabf[:, 0:NT], float(EXPERTS - 1), None, ALU.min))
                dve.sem_inc(R[L]["experts"], 1)
                link(V.tensor_scalar(pad, tab, 0.0, 2.0 * rows_out, ALU.is_equal, ALU.mult))
                link(V.scalar_tensor_tensor(pad, mag, -1.0, pad, ALU.add, ALU.add))
                link(V.tensor_scalar(tab, tab, 0.0, float(TOKENS), ALU.is_lt, ALU.mult))
                link(V.tensor_tensor(sidx[L][:, 0:NT], tab, pad, ALU.add))
                dve.sem_inc(R[L]["sindex"], 1)

                E = F[L]

                def evac_h(j, u, g):
                    r = u % 2
                    ready(dve, E["hT_ps"], j + 1)
                    free(dve, E["y_ps"], j - 1)
                    V.tensor_copy(hidT[:, r * HID:(r + 1) * HID], psB[:, r * 512:r * 512 + HID]
                                  ).then_inc(E["hT"], 1)

                def glu(j, u, g):
                    r = u % 2
                    ready(dve, E["act"], j + 1)
                    free(dve, E["hT_ps"], j - 1)
                    V.tensor_tensor(hid[:, r * HID:(r + 1) * HID], psA[:, 2 * r * 512:2 * r * 512 + HID],
                                    sig[:, r * HID:(r + 1) * HID], ALU.mult).then_inc(E["hid"], 1)

                def residual(j, u, g):
                    r = u % 2
                    ready(dve, E["y_ps"], j + 1)
                    ready(dve, E["keep"], j + 1)
                    free(dve, landed, SLOT_TILES[0] + j + 1 - BLOCK)
                    V.tensor_tensor(yout[:, u * DIM:(u + 1) * DIM], psL[:, 0:DIM],
                                    xkeep[:, u * DIM:(u + 1) * DIM], ALU.add).then_inc(E["y"], 1)

                if L == 0:
                    pipelined(dve, NT, [(2, evac_h)])
                else:
                    pipelined(dve, NT, [(1, glu), (3, residual)])

        @block.tensor
        def _(pe):
            give_credit(pe, "tensor")
            T = nc.tensor
            done = [0]

            def setup(emit):
                n = done[0]
                if n > 7:
                    pe.wait_ge(sb_set, n - 7)
                emit(setup_banks[n % 8]).then_inc(ps_set, 1)
                done[0] += 1

            def setup_keys_values(L):
                setup(lambda d: T.matmul(d, wk[L][:, :], ctxT[:, :], start=True, stop=True))
                for b in range(BATCH):
                    setup(lambda d: T.matmul(d, ctxrep[:, b * P:(b + 1) * P], wv[L][:, :], start=True, stop=True))

            def setup_layer1():
                ready(pe, F[0]["y"], SLOT_TILES[0])
                for k in range(4):
                    setup(lambda d: T.transpose(d, wload[:, k * DIM:(k + 1) * DIM], ident[:, :]))
                pe.wait_ge(sb_set, done[0])
                setup_keys_values(1)
                pe.wait_ge(sb_set, done[0])

            pe.wait_ge(consts, CONSTS)
            pe.wait_ge(in_ctx, 16)
            setup(lambda d: T.transpose(d, ctx_sb[:, :], ident[:, :]))
            pe.wait_ge(in_w0, 16 * 4)
            pe.wait_ge(sb_set, 1)
            pe.wait_ge(rep_ready, 1)
            setup_keys_values(0)
            pe.wait_ge(in_w1, 16 * 5)
            setup(lambda d: T.transpose(d[:, 0:EXPERTS], rw_in[:, :], ident[0:EXPERTS, 0:EXPERTS]))
            pe.wait_ge(sb_set, done[0])

            for L in range(2):
                D, N0 = A, L * TILES

                def transpose_x(n):
                    def emit(g):
                        positive(pe, xT_ready, GROUPS * n + g - 1)
                        for t in range(GROUP):
                            pe.wait_ge(xn_ready[t // 2], (TILES * n + GROUP * g) // 2 + t % 2 + 1)
                            last = T.transpose(ps_group[g % 2][:, t * P:(t + 1) * P],
                                               xn[:, ((g % 2) * GROUP + t) * P:((g % 2) * GROUP + t + 1) * P],
                                               ident[:, :])
                        last.then_inc(xT_ps, 1)
                    return emit

                def logits(g):
                    pe.wait_ge(xT_ready, GROUPS * (2 * L + 1) + g + 1)
                    for i in range(g * GROUP, (g + 1) * GROUP):
                        T.matmul(psL[:, i * EXPERTS:(i + 1) * EXPERTS], xT[:, i * P:(i + 1) * P], rw[L][:, :],
                                 start=True, stop=True).then_inc(logit, 1)

                def queries(i, u, g):
                    free(pe, D["qT"], N0 + i)
                    T.matmul(ps_q, wq[L][:, :], cols(xT, i), start=True, stop=True).then_inc(D["q_ps"], 1)

                def scores(i, u, g):
                    r = u % 2
                    ready(pe, D["qT"], N0 + i + 1)
                    free(pe, D["sh"], N0 + i - 1)
                    last = T.matmul(ps_scores(r), qT[:, r * P:(r + 1) * P], cols(kbd[L], g, HK), start=True, stop=L == 0)
                    if L == 1:
                        last = T.matmul(ps_scores(r), onesb[0:1, :], cols(maskrow, g, HK), start=False, stop=True)
                    last.then_inc(D["s_ps"], 1)

                def transpose_p(i, u, g):
                    r = u % 2
                    ready(pe, D["p"], N0 + i + 1)
                    free(pe, D["pT"], N0 + i - 1)
                    for c in range(CH):
                        last = T.transpose(ps_probsT(r)[:, c * P:(c + 1) * P],
                                           probs[:, r * HK + c * P:r * HK + (c + 1) * P], ident[:, :])
                    last.then_inc(D["pT_ps"], 1)

                def values(i, u, g):
                    r = u % 2
                    ready(pe, D["pT"], N0 + i + 1)
                    free(pe, D["o"], N0 + i)
                    for c in range(CH):
                        last = T.matmul(ps_out[:, c * VW:(c + 1) * VW],
                                        probsT[:, r * HK + c * P:r * HK + (c + 1) * P],
                                        vaug[L][:, bass.ds(g * CH * VW + c * VW, VW)], start=True, stop=True)
                    last.then_inc(D["o_ps"], 1)

                def transpose_o(i, u, g):
                    r = u % 2
                    ready(pe, D["o"], N0 + i + 1)
                    free(pe, D["x1"], N0 + i)
                    T.transpose(ps_oT, heads_out[:, r * DIM:(r + 1) * DIM], ident[:, :]).then_inc(D["oT_ps"], 1)

                def project(i, u, g):
                    r = u % 2
                    ready(pe, D["oT"], N0 + i + 1)
                    T.matmul(ps_y, headsT[:, r * P:(r + 1) * P], wo[L][:, :], start=True, stop=True).then_inc(D["y_ps"], 1)

                if L == 1:
                    setup_layer1()
                skewed(GROUPS, [(0, transpose_x(2 * L))])
                pe.wait_ge(xT_ready, GROUPS * (2 * L + 1))
                pe.wait_ge(kbd_ready[L], BATCH)
                pe.wait_ge(vaug_ready[L], 2 * BATCH)
                if L == 1:
                    pe.wait_ge(mrow_ready, 1)
                transpose = transpose_x(2 * L + 1)

                def transpose_rest(k):
                    if k == 1:
                        ready(pe, D["sh"], N0 + TILES)
                    if k >= 1:
                        transpose(k - 1)
                    if k >= 2:
                        logits(k - 2)
                pipelined(pe, TILES, [(1, scores), (4, transpose_o), (3, values), (0, queries), (2, transpose_p),
                                      (4, project)], tail=transpose_rest)
                transpose_rest(GROUPS)
                logits(GROUPS - 1)

                NT = SLOT_TILES[L]
                pe.wait_ge(R[L]["onehot"], 1)
                T.matmul(psL[:, 128:128 + TE], before[:, :], oh16[:, :], start=True, stop=True)
                T.matmul(psL[:, 256:256 + TE], ones16[:, :], oh16[:, :], start=True, stop=True
                         ).then_inc(R[L]["prefix"], 1)
                KT = TOPK[L] * TILES
                for q in range(KT):
                    pe.wait_ge(R[L]["hots"], q + 1)
                    last = T.matmul(psL[:, 384:384 + NT], rowhot[:, q * P:(q + 1) * P],
                                    colhot[:, q * NT:(q + 1) * NT], start=q == 0, stop=q == KT - 1)
                last.then_inc(R[L]["table"], 1)

                E = F[L]
                H = (L + 1) * HID
                pe.wait_ge(R[L]["experts"], 1)
                pe.wait_ge((in_e0, in_e1)[L], 32)
                if L == 1:
                    pe.wait_ge(parts_in, 32)
                W = (L + 1) * DIM

                def transpose_rows(j, u, g):
                    r = u % 2
                    pe.wait_ge(gathered[L][u], 16 * (g + 1))
                    free(pe, E["xT"], j)
                    T.transpose(ps_xT, rows[:, u * W:u * W + DIM], ident[:, :]).then_inc(E["T_ps"], 1)

                def up(j, u, g):
                    r = u % 2
                    e = pe.value_load(etab[L][0:1, bass.ds(j, 1)], min_val=0, max_val=EXPERTS - 1)
                    ready(pe, E["xT"], j + 1)
                    free(pe, E["hid"], j - 1)
                    for k in range(L + 1):
                        dst = psA[:, ((L + 1) * r + k) * 512:((L + 1) * r + k) * 512 + HID]
                        last = T.matmul(dst, slotsT[:, r * P:(r + 1) * P], w1[L][:, bass.ds(e * H + k * HID, HID)],
                                        start=True, stop=L == 0)
                        if L == 1:
                            last = T.matmul(dst, onesb[0:3, :], b1[:, bass.ds(e * H + k * HID, HID)],
                                            start=False, stop=True)
                    last.then_inc(E["h_ps"], 1)

                def transpose_h(j, u, g):
                    r = u % 2
                    ready(pe, E["hid"], j + 1)
                    free(pe, E["hT"], j - 1)
                    for c in range(CH):
                        last = T.transpose(psB[:, r * 512 + c * P:r * 512 + (c + 1) * P],
                                           hid[:, r * HID + c * P:r * HID + (c + 1) * P], ident[:, :])
                    last.then_inc(E["hT_ps"], 1)

                def down(j, u, g):
                    r = u % 2
                    e = pe.value_load(etab[L][0:1, bass.ds(j, 1)], min_val=0, max_val=EXPERTS - 1)
                    ready(pe, E["hT"], j + 1)
                    free(pe, E["y"], j)
                    dst = psL[:, 0:DIM]
                    for c in range(CH):
                        last = T.matmul(dst, hidT[:, r * HID + c * P:r * HID + (c + 1) * P],
                                        w2[L][:, bass.ds(e * HID + c * DIM, DIM)], start=c == 0,
                                        stop=c == CH - 1 and L == 0)
                    if L == 1:
                        last = T.matmul(dst, onesb[0:3, :], b2[:, bass.ds(e * DIM, DIM)], start=False, stop=True)
                    last.then_inc(E["y_ps"], 1)

                pipelined(pe, NT, [(0, transpose_rows), (1, up), (2, transpose_h), (3, down)])


_INS = ['x', 'ctx_1024', 'mask_BxS2_bf1'] + [
    f'L{L}_xattn_{n}' for L in range(2) for n in ('Wq', 'bq', 'Wk', 'bk', 'Wv', 'bv', 'Wo', 'bo')] + [
    'L0_ffn_router_w', 'L0_ffn_w1', 'L0_ffn_w2', 'L1_ffn_router_w', 'L1_ffn_router_b',
    'L1_ffn_w1', 'L1_ffn_b1', 'L1_ffn_w2', 'L1_ffn_b2']


def kernel(**inputs):
    import concourse.bacc as bacc
    from concourse.bass_utils import run_bass_kernel_spmd

    nc = bacc.Bacc("TRN2", target_bir_lowering=False, num_devices=1)
    arrays, aps = {}, {}
    for name in _INS:
        v = np.ascontiguousarray(inputs[name])
        if v.dtype == np.bool_:
            v = v.view(np.uint8)
        arrays[f"in_{name}"] = v
        aps[name] = nc.dram_tensor(f"in_{name}", v.shape, mybir.dt.from_np(v.dtype), kind="ExternalInput").ap()
    out = nc.dram_tensor("out", (BATCH, SEQ, DIM), F32, kind="ExternalOutput").ap()
    build(nc, aps, out)
    r = run_bass_kernel_spmd(nc, [arrays], core_ids=[0])
    return r.results[0]["out"]
```

```python
from contextlib import ExitStack

import numpy as np
import concourse.bass as bass
from concourse import mybir
from concourse.alu_op_type import AluOpType as ALU

ACT = mybir.ActivationFunctionType
F32 = mybir.dt.float32
F16 = mybir.dt.float16
BF16 = mybir.dt.bfloat16
I32 = mybir.dt.int32
U8 = mybir.dt.uint8
AX = mybir.AxisListType.X

P = 128
BATCH, SEQ, DIM = 4, 512, 128
KEYS, HEADS = 32, 16
HD = DIM // HEADS
TOKENS = BATCH * SEQ
TILES = TOKENS // P
GROUP = SEQ // P
GROUPS = TILES // GROUP
GW = GROUP * P
EXPERTS = 8
HID = 512
CH = HID // P
HK = HEADS * KEYS
HPC = P // KEYS
VW = HPC * (HD + 1)
BLOCK = 4
EPS = 1e-5
SCALE = float(HD) ** -0.5
FILL = -1e8 / SCALE
TOPK = (2, 1)
HOTS_ACT = (8, 4)
HOTS_CHUNK = 4
CONSTS = 21
SLOT_TILES = tuple(k * TILES + EXPERTS - 1 for k in TOPK)
MAXT = max(SLOT_TILES)
FBLOCK = 2 * BLOCK
RING = (2 * BLOCK, BLOCK)
MAXI = -(-MAXT // FBLOCK) * FBLOCK + BLOCK


CREDIT = BLOCK


def ready(eng, sem, count):
    eng.wait_ge(sem, count + CREDIT)


def free(eng, sem, count):
    eng.wait_ge(sem, count + CREDIT)


def settle(eng, sem):
    eng.sem_inc(sem, 1)


def pipelined(eng, n, stages, block=BLOCK, head=None, tail=None):
    most = max(lag for lag, _ in stages)
    lead = -(-most // block)

    def steps(b, count):
        for s in range(count):
            for lag, emit in stages:
                item = b * block + (s - lag)
                if isinstance(item, int) and not 0 <= item < n:
                    continue
                emit(item, (s - lag) % block, b + (s - lag) // block)
            if head and isinstance(b, int) and b == 0:
                head(s)
            if tail and isinstance(b, int) and b * block + s >= n:
                tail(b * block + s - n)

    for b in range(lead):
        steps(b, block)
    full = n // block
    with eng.Fori(lead, full) as b:
        steps(b, block)
    steps(full, n - full * block + most)


def landed_in_ring(L, u, g):
    return g * (FBLOCK // RING[L]) + u // RING[L] + 1


def hot_order(L):
    chunks = [range(q, q + HOTS_CHUNK) for q in range(0, TOPK[L] * TILES, HOTS_CHUNK)]
    n = HOTS_ACT[L] // HOTS_CHUNK
    order = []
    for k in range(n):
        order += chunks[n + 3 * k:n + 3 * (k + 1)] + [chunks[k]]
    return [q for chunk in order for q in chunk]


def positive(eng, sem, count):
    if count > 0:
        eng.wait_ge(sem, count)


def build(nc, a, out):
    ctx = ExitStack()
    with ctx:
        def sb(name, shape, dt=F32):
            return ctx.enter_context(nc.sbuf_tensor(name, shape, dt))

        def sem(name):
            return ctx.enter_context(nc.semaphore(name))

        def cols(t, i, w=P):
            return t[:, bass.ds(i * w, w)]

        xn_dram = nc.dram_tensor("xn_rows", [TOKENS, DIM], F32, kind="Internal").ap()
        xx_dram = nc.dram_tensor("xn_x_rows", [TOKENS, 2 * DIM], F32, kind="Internal").ap()
        y_dram = nc.dram_tensor("expert_rows", [2 * TOKENS, DIM], F32, kind="Internal").ap()
        out_rows = out.rearrange("b s d -> (b s) d")

        x = sb("x", [P, TILES * DIM])
        ident = sb("ident", [P, P])
        headmask = sb("headmask", [P, HEADS])
        groupmask = sb("groupmask", [P, HPC])
        before = sb("before", [P, P], F16)
        ones16 = sb("ones16", [P, P], F16)
        onesb = sb("onesb", [P, P], BF16)
        iota_row = sb("iota_row", [P, P], F16)
        iota_tiles = sb("iota_tiles", [P, MAXT], F16)
        tile_no = sb("tile_no", [P, MAXT])
        prefer = sb("prefer", [P, EXPERTS])
        steps128 = sb("steps128", [P, TILES])
        token1 = sb("token1", [P, 2 * TILES])
        carry = sb("carry", [P, EXPERTS * TILES])
        ones8 = sb("ones8", [P, EXPERTS])
        eps = sb("eps", [P, 1])
        minus_half = sb("minus_half", [P, 1])
        minus_one = sb("minus_one", [P, 1])
        table_use = sb("table_use", [P, 1])

        ctx_sb = sb("ctx_sb", [P, DIM])
        ctxT = sb("ctxT", [P, P])
        ybuf = sb("ybuf", [P, 2 * 2 * GW])
        wload, ctxrep, vrows = (ybuf[:, k * GW:(k + 1) * GW] for k in range(3))
        wq, wk, wv, wo, kT = [], [], [], [], []
        bq, bk, bv, bo, kbd, vaug = [], [], [], [], [], []
        for L in range(2):
            wq.append(sb(f"wq{L}", [P, DIM]))
            wk.append(sb(f"wk{L}", [P, DIM]))
            wv.append(sb(f"wv{L}", [P, DIM]))
            wo.append(sb(f"wo{L}", [P, DIM]))
            kT.append(sb(f"kT{L}", [P, P]))
            bq.append(sb(f"bq{L}", [P, 1]))
            bk.append(sb(f"bk{L}", [P, 1]))
            bv.append(sb(f"bv{L}", [P, DIM]))
            bo.append(sb(f"bo{L}", [P, DIM]))
            kbd.append(sb(f"kbd{L}", [P, BATCH * HK]))
            vaug.append(sb(f"vaug{L}", [P, BATCH * CH * VW]))
        mask8 = sb("mask8", [P, P], U8)
        maskf = sb("maskf", [P, P])
        maskrow = sb("maskrow", [1, BATCH * HK], BF16)
        rw_in = sb("rw_in", [EXPERTS, DIM])
        rw = [sb("rw0", [P, EXPERTS]), sb("rw1", [P, EXPERTS])]
        rb = sb("rb", [P, EXPERTS])
        WC = (HID, 2 * HID + 2 * CH)
        w1 = [sb("w1_0", [P, EXPERTS * WC[0]]), sb("w1_1", [P, EXPERTS * WC[1]])]
        w_ring = sb("w_ring", [P, 2 * WC[1]])
        w2 = [sb("w2_0", [P, EXPERTS * HID]), sb("w2_1", [P, EXPERTS * HID])]
        b1_in = sb("b1_in", [EXPERTS * 2 * CH, P])
        b2 = sb("b2", [P, EXPERTS * DIM])

        bst = sb("bst", [P, TILES * 6])
        mv = sb("mv", [P, TILES * 2])
        bst2 = sb("bst2", [P, GROUP * 6])
        mv2 = sb("mv2", [P, GROUP * 2])
        vareps, rstd, minus_mean, nbias = (sb(n, [P, TILES]) for n in ("vareps", "rstd", "minus_mean", "nbias"))
        vareps2, rstd2, mr2, nbias2 = (sb(n, [P, TILES]) for n in ("vareps2", "rstd2", "mr2", "nbias2"))
        xn = sb("xn", [P, 2 * GW])
        xT = sb("xT", [P, TOKENS])

        xb = sb("xb", [P, BLOCK * DIM])
        qT = sb("qT", [P, 2 * P])
        mx = sb("mx", [P, 2 * HEADS])
        shifted = sb("shifted", [P, 2 * HK])
        probs = sb("probs", [P, 2 * HK])
        probsT = sb("probsT", [P, 2 * HK])
        rsum = sb("rsum", [P, 2 * HEADS])
        heads_out = sb("heads_out", [P, 2 * DIM])
        headsT = sb("headsT", [P, 2 * P])

        TE = TILES * EXPERTS
        lg = sb("lg", [P, TE])
        gexp = sb("gexp", [P, TILES])
        red = sb("red", [P, 8, TILES])
        tmp = sb("tmp", [P, TE])
        tmp2 = sb("tmp2", [P, TE])
        oh = [sb("oh0", [P, TE]), sb("oh1", [P, TE])]
        oh16 = sb("oh16", [P, TE], F16)
        tot = sb("tot", [P, TE])
        incl = sb("incl", [P, TE])
        slotmat = sb("slotmat", [P, TE])
        cmp = sb("cmp", [P, EXPERTS * TILES])
        etile = sb("etile", [P, 4, EXPERTS])
        cmpj = sb("cmpj", [P, MAXT * EXPERTS])
        etabf = sb("etabf", [P, MAXT])
        etab = [sb("etab0", [P, MAXT], I32), sb("etab1", [P, MAXT], I32)]
        gate = [sb("gate0", [P, TILES]), sb("gate1", [P, TILES])]
        slotf = sb("slotf", [P, 2 * TILES])
        slot = [sb("slots_0", [P, 2 * TILES], I32), sb("slots_1", [P, 2 * TILES], I32)]
        slot_r = sb("slot_r", [P, 2 * TILES], I32)
        slot_j = sb("slot_j", [P, 2 * TILES], I32)
        rowf = sb("rowf", [P, 2 * TILES])
        rowhot = xT[:, :].bitcast(F16)
        away = sb("away", [P, 4 * P], F16)
        colhot = sb("colhot", [P, 2 * TILES * MAXT], F16)
        tabf = sb("tabf", [P, 3 * MAXT])
        gidx = [sb("gidx0", [P, MAXI], I32), sb("gidx1", [P, MAXI], I32)]
        sidx = [sb("sidx0", [P, MAXI], I32), sb("sidx1", [P, MAXI], I32)]

        idx_ring = sb("idx_ring", [P, 2 * BLOCK], I32)
        idx2_ring = sb("idx2_ring", [P, 2 * BLOCK], I32)
        rows = sb("rows", [P, BLOCK * 2 * DIM])
        slotsT = sb("slotsT", [P, 2 * P])
        sig, hidT = shifted, probsT
        xkeep = sb("xkeep", [P, BLOCK * DIM])
        yout = xb

        psA = ctx.enter_context(nc.psum_tensor("psA", [P, 4 * 512], F32))
        psB = ctx.enter_context(nc.psum_tensor("psB", [P, 2 * 512], F32))
        psX = ctx.enter_context(nc.psum_tensor("psX", [P, 512], F32))
        psL = ctx.enter_context(nc.psum_tensor("psL", [P, 512], F32))

        def b1_column(r, c):
            return w_ring[:, r * WC[1] + 2 * HID + c:r * WC[1] + 2 * HID + c + 1]

        def ps_scores(r):
            return psA[:, r * 512:r * 512 + HK]

        def ps_logits(g):
            return psX if g == GROUPS - 1 else psL

        def ps_probsT(r):
            return psA[:, (2 + r) * 512:(2 + r) * 512 + HK]

        ps_out = psB[:, 0:CH * VW]
        ps_oT, ps_y = psB[:, 512:512 + P], psB[:, 512 + P:512 + P + DIM]
        ps_slots, ps_rows = [psX[:, 0:P], psL[:, 0:P]], [psB[:, 0:DIM], psB[:, 512:512 + DIM]]
        ps_q = psX[:, 0:P]
        ps_group = [[psA[:, 0:512]] + [psL[:, :]] * (GROUPS - 1), [psA[:, 0:512], psA[:, 512:2 * 512]] * 2]
        setup_banks = [psA[:, k * 512:k * 512 + P] for k in range(4)] + [psB[:, 0:P], psB[:, 512:512 + P],
                                                                         psX[:, 0:P], psL[:, 0:P]]


        in_x = [sem(f"in_x{g}") for g in range(GROUPS)]
        in_ctx, in_wk, in_wv, in_w0, in_w1, in_b0, in_bo, in_small, in_router = map(sem, (
            "in_ctx", "in_wk", "in_wv", "in_w0", "in_w1", "in_b0", "in_bo", "in_small", "in_router"))
        in_e0, in_e1, in_bias = map(sem, ("in_e0", "in_e1", "in_bias"))
        consts, zeroed, ident_ready = sem("consts"), sem("zeroed"), sem("ident_ready")
        ps_set, sb_set = sem("ps_set"), sem("sb_set")
        gates_ready, terms = sem("gates_ready"), sem("terms")
        rw_ps, rw_ready = sem("rw_ps"), sem("rw_ready")
        kT_ready, keys_ready, rep_ready = sem("kT_ready"), sem("keys_ready"), sem("rep_ready")
        mask_ready, kbd_ready = sem("mask_ready"), [sem("kbd0_ready"), sem("kbd1_ready")]
        vaug_ready = [sem("vaug0_ready"), sem("vaug1_ready")]
        mrow_ready = sem("mrow_ready")
        vchain = sem("vchain")
        stat, mv_ready, pchain = sem("stat"), sem("mv_ready"), sem("pchain")
        nb_ready, xT_ps, xT_ready = sem("nb_ready"), sem("xT_ps"), sem("xT_ready")
        xn_ready = [sem("xn_ready_act"), sem("xn_ready_dve")]
        logit, x_mixed, x_half = sem("logit"), sem("x_mixed"), sem("x_half")
        y_in, y_scaled = [sem("y_in0"), sem("y_in1")], sem("y_scaled")
        stored, stored_x = [sem("stored0"), sem("stored1")], sem("stored_x")
        names = ["q_ps", "qT", "s_ps", "mx", "sh", "p", "pT_ps", "pT", "o_ps", "rs", "o", "oT_ps", "oT", "y_ps",
                 "x1", "xb", "stat2", "mv2", "veps2", "rstd2", "mr2", "nb2"]
        A = {n: sem(n) for n in names}
        landed = sem("landed")
        fnames = ["idx", "idx2", "keep", "w", "T_ps", "xT", "h_ps", "act", "hid", "y_ps", "y"]
        F = [{n: sem(f"f_{n}_{L}") for n in fnames} for L in range(2)]
        gathered = [[sem(f"gathered{L}_{u}") for u in range(RING[L])] for L in range(2)]
        written = [[sem(f"written{L}_{u}") for u in range(BLOCK)] for L in range(2)]
        R = [{n: sem(f"r_{n}_{L}") for n in ("gap", "exp", "onehot", "prefix", "hots", "table", "experts",
                                     "slots", "away", "hots_act", "columns", "tokens")}
             for L in range(2)]

        waited = {n: sem(f"waited_{n}") for n in ("gpsimd", "vector")}
        makers = {
            "gpsimd": ("xb", "veps2", "rstd2", "mr2", "nb2"),
            "scalar": ("qT", "p", "pT", "oT"),
            "tensor": ("q_ps", "s_ps", "pT_ps", "o_ps", "oT_ps", "y_ps"),
            "vector": ("mx", "sh", "rs", "o", "x1", "stat2", "mv2"),
        }
        expert_makers = {
            "gpsimd": ((), ()), "tensor": (("T_ps", "h_ps", "y_ps"),) * 2,
            "scalar": (("xT", "hid", "y"), ("xT", "act")), "vector": (("idx", "idx2", "w"), ("idx", "idx2", "w", "keep", "hid", "y")),
        }

        def give_credit(eng, name):
            for n in makers[name]:
                eng.sem_inc(A[n], CREDIT)
            for L in range(2):
                for n in expert_makers[name][L]:
                    eng.sem_inc(F[L][n], CREDIT)

        def row(ap):
            return ap.rearrange("(a n) -> a n", a=1).partition_broadcast(P).rearrange("p a n -> p (a n)")

        def column(ap):
            return ap.rearrange("(p a) -> p a", a=1)

        block = ctx.enter_context(nc.Block())

        @block.sync
        def _(sp):
            sp.sem_inc(landed, CREDIT)
            xr = a["x"].rearrange("b (t p) d -> p (b t) d", p=P)
            xv = x[:, :].rearrange("p (t d) -> p t d", d=DIM)
            sp.dma_start(ctx_sb[:, :], a["ctx_1024"].rearrange("b s d -> (b s) d")).then_inc(in_ctx, 16)
            sp.dma_start(xv[:, 0:GROUP, :], xr[:, 0:GROUP, :]).then_inc(in_x[0], 16)
            sp.dma_start(wk[0][:, :], a["L0_xattn_Wk"]).then_inc(in_wk, 16)
            sp.dma_start(wv[0][:, :], a["L0_xattn_Wv"]).then_inc(in_wv, 16)
            for g in range(1, GROUPS):
                sp.dma_start(xv[:, g * GROUP:(g + 1) * GROUP, :], xr[:, g * GROUP:(g + 1) * GROUP, :]).then_inc(in_x[g], 16)
            sp.dma_start(wq[0][:, :], a["L0_xattn_Wq"]).then_inc(in_w0, 16)
            sp.dma_start(wo[0][:, :], a["L0_xattn_Wo"]).then_inc(in_w0, 16)
            sp.dma_start(bo[0][:, :], row(a["L0_xattn_bo"])).then_inc(in_bo, 16)
            sp.dma_start(mask8[:, :], row(a["mask_BxS2_bf1"].rearrange("b k -> (b k)"))).then_inc(in_small, 16)
            sp.dma_start(rw_in[:, :], a["L0_ffn_router_w"]).then_inc(in_router, 16)
            sp.dma_start(rw[1][:, :], a["L1_ffn_router_w"]).then_inc(in_router, 16)
            sp.dma_start(rb[:, :], row(a["L1_ffn_router_b"])).then_inc(in_router, 16)
            for k, n in enumerate(("Wq", "Wk", "Wv", "Wo")):
                sp.dma_start(wload[:, k * DIM:(k + 1) * DIM], a[f"L1_xattn_{n}"]).then_inc(in_w1, 16)
            sp.dma_start(bk[1][:, :], column(a["L1_xattn_bk"])).then_inc(in_small, 16)
            sp.dma_start(bv[1][:, :], row(a["L1_xattn_bv"])).then_inc(in_small, 16)
            sp.dma_start(bq[1][:, :], column(a["L1_xattn_bq"])).then_inc(in_small, 16)
            sp.dma_start(bo[1][:, :], row(a["L1_xattn_bo"])).then_inc(in_small, 16)
            sp.dma_start(b2[:, :], row(a["L1_ffn_b2"].rearrange("e d -> (e d)"))).then_inc(in_bias, 16)
            sp.dma_start(b1_in[:, :], a["L1_ffn_b1"].rearrange("e (c p) -> (e c) p", p=P)).then_inc(in_bias, 16)
            for L, s_in in ((0, in_e0), (1, in_e1)):
                n1 = HID * (L + 1)
                sp.dma_start(w1[L][:, :].rearrange("p (e n) -> p e n", n=WC[L])[:, :, 0:n1],
                             a[f"L{L}_ffn_w1"].rearrange("e c n -> c e n")).then_inc(s_in, 16)
                sp.dma_start(w2[L][:, :].rearrange("p (k d) -> p k d", d=DIM),
                             a[f"L{L}_ffn_w2"].rearrange("e (c p) d -> p (e c) d", p=P)).then_inc(s_in, 16)
            y_rows = y_dram.rearrange("(k g t p) d -> p k g t d", p=P, t=GROUP, g=GROUPS)
            for L in range(2):
                if L == 1:
                    sp.wait_ge(vaug_ready[1], 2 * BATCH)
                    for g in range(GROUPS):
                        positive(sp, x_mixed, GROUP * (g - 1))
                        for k in range(2):
                            sp.dma_start(ybuf[:, ((g % 2) * 2 + k) * GW:((g % 2) * 2 + k + 1) * GW]
                                         .rearrange("p (t d) -> p t d", d=DIM), y_rows[:, k, g]).then_inc(y_in[g % 2], 16)
                dst = xn_dram if L == 0 else xx_dram[:, 0:DIM]
                for g in range(GROUPS):
                    if L == 1:
                        ready(sp, A["x1"], TILES + GROUP * (g + 1))
                        sp.dma_start(xx_dram[g * GW:(g + 1) * GW, DIM:].rearrange("(t p) d -> p t d", p=P),
                                     xv[:, g * GROUP:(g + 1) * GROUP, :]).then_inc(stored_x, 16)
                    for h in range(2):
                        sp.wait_ge(xn_ready[h], (TILES * (2 * L + 1) + GROUP * (g + 1)) // 2)
                    sp.dma_start(dst[g * GW:(g + 1) * GW, :].rearrange("(t p) d -> p t d", p=P),
                                 xn[:, (g % 2) * GW:(g % 2 + 1) * GW].rearrange("p (t d) -> p t d", d=DIM)
                                 ).then_inc(stored[g % 2], 16)
                def landed_rows(j, u, g):
                    sp.wait_ge(written[L][u], 16 * (g + 1))
                    sp.sem_inc(landed, 1)
                pipelined(sp, SLOT_TILES[L], [(0, landed_rows)])

        @block.gpsimd
        def _(pool):
            give_credit(pool, "gpsimd")
            pool.memset(ident[:, :], 0.0).then_inc(zeroed, 1)
            pool.wait_ge(zeroed, 1)
            pool.affine_select(out=ident[:, :], in_=ident[:, :], compare_op=ALU.not_equal, fill=1.0, base=0,
                               pattern=[[-1, P]], channel_multiplier=1).then_inc(ident_ready, 1)
            pool.memset(headmask[:, :], 1.0).then_inc(zeroed, 1)
            pool.memset(groupmask[:, :], 1.0).then_inc(zeroed, 1)
            pool.memset(before[:, :], 1.0).then_inc(zeroed, 1)
            pool.memset(carry[:, :], 1.0).then_inc(zeroed, 1)
            pool.memset(ones16[:, :], 1.0).then_inc(consts, 1)
            pool.memset(onesb[:, :], 1.0).then_inc(consts, 1)
            pool.memset(ones8[:, :], 1.0).then_inc(consts, 1)
            pool.memset(minus_half[:, :], -0.5).then_inc(consts, 1)
            pool.memset(eps[:, :], EPS).then_inc(consts, 1)
            pool.memset(minus_one[:, :], -1.0).then_inc(consts, 1)
            for t in (*gidx, *sidx):
                pool.memset(t[:, :], 0).then_inc(consts, 1)
            pool.wait_ge(zeroed, 5)
            for m, n, w in ((headmask, HEADS, HD), (groupmask, HPC, KEYS)):
                pool.affine_select(out=m[:, :], in_=m[:, :], compare_op=ALU.is_ge, fill=0.0, base=0,
                                   pattern=[[-w, n]], channel_multiplier=1).then_inc(zeroed, 1)
            pool.wait_ge(zeroed, 7)
            for m, n, w in ((headmask, HEADS, HD), (groupmask, HPC, KEYS)):
                pool.affine_select(out=m[:, :], in_=m[:, :], compare_op=ALU.is_ge, fill=0.0, base=w - 1,
                                   pattern=[[w, n]], channel_multiplier=-1).then_inc(consts, 1)
            pool.affine_select(out=before[:, :], in_=before[:, :], compare_op=ALU.is_gt, fill=0.0, base=0,
                               pattern=[[1, P]], channel_multiplier=-1).then_inc(consts, 1)
            pool.affine_select(out=carry[:, :], in_=carry[:, :], compare_op=ALU.not_equal, fill=0.0, base=0,
                               pattern=[[0, EXPERTS], [1, TILES]], channel_multiplier=0).then_inc(consts, 1)
            for t, pat, base, cm in (
                    (iota_row, [[1, P]], 0, 0), (iota_tiles, [[1, MAXT]], 0, 0), (tile_no, [[1, MAXT]], 0, 0),
                    (prefer, [[-1, EXPERTS]], EXPERTS, 0), (steps128, [[P, TILES]], 0, 0),
                    (token1[:, 0:TILES], [[P, TILES]], 1, 1), (token1[:, TILES:], [[-P, TILES]], -1, -1)):
                pool.iota(t[:, :], pat, base=base, channel_multiplier=cm,
                          allow_small_or_imprecise_dtypes=True).then_inc(consts, 1)
            def spread_keys(L):
                for b in range(BATCH // 2, BATCH):
                    pool.tensor_tensor(kbd[L][:, b * HK:(b + 1) * HK].rearrange("p (h k) -> p h k", h=HEADS),
                                       kT[L][:, b * KEYS:(b + 1) * KEYS].unsqueeze(1).to_broadcast([P, HEADS, KEYS]),
                                       headmask[:, :].unsqueeze(2).to_broadcast([P, HEADS, KEYS]),
                                       ALU.mult).then_inc(kbd_ready[L], 1)

            links = [0]

            def link(ins):
                links[0] += 1
                ins.then_inc(pchain, 1)
                pool.wait_ge(pchain, links[0])

            for L in range(2):
                D, N0 = A, L * TILES

                def norm_terms(g):
                    c = slice(g * GROUP, (g + 1) * GROUP)
                    pool.wait_ge(terms, 2 * (L * GROUPS + g + 1))
                    link(pool.tensor_tensor(rstd[:, c], vareps[:, c], minus_half[:, :].to_broadcast([P, GROUP]), ALU.pow))
                    pool.tensor_tensor(nbias[:, c], minus_mean[:, c], rstd[:, c], ALU.mult).then_inc(nb_ready, 1)

                def residual(i, u, g):
                    free(pool, D["x1"], N0 + i + 1 - BLOCK)
                    pool.tensor_tensor(xb[:, u * DIM:(u + 1) * DIM], cols(x, i), bo[L][:, :], ALU.add
                                       ).then_inc(D["xb"], 1)

                def norm_terms2(i, u, g):
                    if u != GROUP - 1:
                        return
                    G0 = L * GROUPS
                    c = bass.ds(g * GROUP, GROUP)
                    m = mv2[:, :].rearrange("p (t k) -> p k t", k=2)
                    ready(pool, D["mv2"], N0 + i + 1)
                    pool.tensor_tensor(vareps2[:, c], m[:, 1, :], eps[:, :].to_broadcast([P, GROUP]), ALU.add
                                       ).then_inc(D["veps2"], 1)
                    ready(pool, D["veps2"], G0 + g + 1)
                    pool.tensor_tensor(rstd2[:, c], vareps2[:, c], minus_half[:, :].to_broadcast([P, GROUP]), ALU.pow
                                       ).then_inc(D["rstd2"], 1)
                    ready(pool, D["rstd2"], G0 + g + 1)
                    pool.tensor_tensor(mr2[:, c], m[:, 0, :], rstd2[:, c], ALU.mult).then_inc(D["mr2"], 1)
                    ready(pool, D["mr2"], G0 + g + 1)
                    pool.tensor_tensor(nbias2[:, c], mr2[:, c], minus_one[:, :].to_broadcast([P, GROUP]), ALU.mult
                                       ).then_inc(D["nb2"], 1)

                for g in range(GROUPS):
                    norm_terms(g)
                    if g == 0:
                        pool.wait_ge(kT_ready, L + 1)
                        spread_keys(L)
                pool.wait_ge(mv_ready, N0 + TILES)
                if L == 0:
                    pool.wait_ge(in_bo, 16)
                pipelined(pool, TILES, [(1, residual), (4, norm_terms2)])
                if L == 0:
                    pool.wait_ge(in_small, 16 * 5)
                    pool.tensor_copy(maskf[:, :], mask8[:, :]).then_inc(mask_ready, 1)
                    pool.wait_ge(mask_ready, 1)
                    pool.tensor_scalar(maskrow[0:1, :].rearrange("p (b h k) -> p b h k", b=BATCH, h=HEADS),
                                       maskf[0:1, :].rearrange("p (b k) -> p b k", b=BATCH).unsqueeze(2)
                                       .to_broadcast([1, BATCH, HEADS, KEYS]),
                                       -1.0, -FILL, ALU.add, ALU.mult).then_inc(mrow_ready, 1)

                NT = SLOT_TILES[L]
                pool.wait_ge(R[L]["columns"], 1)
                for c in hot_order(L)[::HOTS_CHUNK]:
                    col3 = colhot[:, c * NT:(c + HOTS_CHUNK) * NT].rearrange("p (q j) -> p q j", j=NT)
                    pool.tensor_tensor(col3, col3, token1[:, c:c + HOTS_CHUNK].unsqueeze(2)
                                       .to_broadcast([P, HOTS_CHUNK, NT]), ALU.mult).then_inc(R[L]["tokens"], 1)
                for u in range(2):
                    pool.wait_ge(stored[u], 16 * 2 * (L + 1))
                if L == 1:
                    pool.wait_ge(stored_x, 16 * GROUPS)
                W = (L + 1) * DIM
                src = xn_dram if L == 0 else xx_dram

                def gather(j, u, g):
                    v = u % RING[L]
                    if not (isinstance(j, int) and j < RING[L]):
                        free(pool, F[L]["T_ps"], j + 1 - RING[L])
                        if L == 1:
                            free(pool, F[L]["keep"], j + 1 - RING[L])
                    ready(pool, F[L]["idx"], 2 * g + u // BLOCK + 1)
                    settle(pool, waited["gpsimd"])
                    pool.indirect_dma_start(rows[:, v * W:(v + 1) * W], None, src,
                                            bass.IndirectOffsetOnAxis(ap=idx_ring[:, u:u + 1], axis=0)
                                            ).then_inc(gathered[L][v], 16)

                dst, rows_out = (y_dram, 2 * TOKENS) if L == 0 else (out_rows, TOKENS)
                last_row = pool.to_reg(rows_out - 1)

                def scatter(j, u, g):
                    v = u % BLOCK
                    ready(pool, F[L]["y"], j + 1)
                    ready(pool, F[L]["idx2"], 2 * g + u // BLOCK + 1)
                    settle(pool, waited["gpsimd"])
                    pool.indirect_dma_start(dst, bass.IndirectOffsetOnAxis(ap=idx2_ring[:, u:u + 1], axis=0),
                                            yout[:, v * DIM:(v + 1) * DIM], None,
                                            bounds_check=last_row, oob_is_err=False
                                            ).then_inc(written[L][v], 16)

                LAG = (7, 6)[L]
                pipelined(pool, NT, [(0, gather), (LAG, scatter)], block=FBLOCK)

        @block.scalar
        def _(act):
            act.dma_start(bk[0][:, :], column(a["L0_xattn_bk"])).then_inc(in_b0, 16)
            act.dma_start(bv[0][:, :], row(a["L0_xattn_bv"])).then_inc(in_b0, 16)
            act.dma_start(bq[0][:, :], column(a["L0_xattn_bq"])).then_inc(in_b0, 16)
            give_credit(act, "scalar")

            def load_table(function):
                act.activation(table_use[:, :], eps[:, :], function)
            act.wait_ge(consts, CONSTS)
            load_table(ACT.Exp)

            for L in range(2):
                D, N0 = A, L * TILES

                def normalise(n, rs, nb):
                    def emit(g):
                        if n % 2 == 0:
                            act.wait_ge(nb_ready, L * GROUPS + g + 1)
                        else:
                            ready(act, D["nb2"], L * GROUPS + g + 1)
                        positive(act, xT_ps, GROUPS * n + g - 1)
                        if g >= 2 and n % 2:
                            act.wait_ge(stored[g % 2], 16 * (2 * L + g // 2))
                        for t in range(GROUP // 2):
                            i = g * GROUP + t
                            act.activation(xn[:, ((g % 2) * GROUP + t) * P:((g % 2) * GROUP + t + 1) * P],
                                           x[:, i * DIM:(i + 1) * DIM], ACT.Identity, bias=nb[:, i:i + 1],
                                           scale=rs[:, i:i + 1]).then_inc(xn_ready[0], 1)
                    return emit

                def evac_x(n):
                    def emit(g):
                        act.wait_ge(xT_ps, GROUPS * n + g + 1)
                        act.activation(xT[:, g * GW:(g + 1) * GW], ps_group[n % 2][g], ACT.Copy).then_inc(xT_ready, 1)
                    return emit

                def evac_q(i, u, g):
                    r = u % 2
                    ready(act, D["q_ps"], N0 + i + 1)
                    free(act, D["s_ps"], N0 + i - 1)
                    act.activation(qT[:, r * P:(r + 1) * P], ps_q, ACT.Identity, bias=bq[L][:, 0:1]).then_inc(D["qT"], 1)

                def exp(i, u, g):
                    r = u % 2
                    ready(act, D["sh"], N0 + i + 1)
                    free(act, D["pT_ps"], N0 + i - 1)
                    act.activation(probs[:, r * HK:(r + 1) * HK], shifted[:, r * HK:(r + 1) * HK], ACT.Exp,
                                   scale=SCALE).then_inc(D["p"], 1)

                def evac_p(i, u, g):
                    r = u % 2
                    ready(act, D["pT_ps"], N0 + i + 1)
                    free(act, D["o_ps"], N0 + i - 1)
                    act.activation(probsT[:, r * HK:(r + 1) * HK], ps_probsT(r), ACT.Copy
                                   ).then_inc(D["pT"], 1)

                def evac_o(i, u, g):
                    r = u % 2
                    ready(act, D["oT_ps"], N0 + i + 1)
                    free(act, D["y_ps"], N0 + i - 1)
                    act.activation(headsT[:, r * P:(r + 1) * P], ps_oT, ACT.Copy).then_inc(D["oT"], 1)

                if L == 1:
                    load_table(ACT.Exp)
                norm1, evac1 = normalise(2 * L, rstd, nbias), evac_x(2 * L)

                def scale_rows(g):
                    if L == 0:
                        return
                    act.wait_ge(gates_ready, 1)
                    act.wait_ge(y_in[g % 2], 32 * (g // 2 + 1))
                    for t in range(GROUP):
                        at = ((g % 2) * 2 * GROUP + t) * DIM
                        i = g * GROUP + t
                        last = act.activation(ybuf[:, at:at + DIM], ybuf[:, at:at + DIM], ACT.Copy, scale=gate[0][:, i:i + 1])
                    last.then_inc(y_scaled, 1)

                scale_rows(1)
                norm1(0)
                evac1(0)
                scale_rows(2)
                norm1(1)

                def normalise_next(k):
                    if k + 1 < GROUPS:
                        evac1(k + 1)
                    if k == 0:
                        scale_rows(3)
                    if k + 2 < GROUPS:
                        norm1(k + 2)
                if L == 0:
                    act.wait_ge(in_b0, 16 * 3)
                norm, evac = normalise(2 * L + 1, rstd2, nbias2), evac_x(2 * L + 1)

                rest = [[(norm, 0), (norm, 1)], [(evac, 0), (norm, 2)], [(evac, 1)], [(evac, 2), (norm, 3)]]

                def normalise_rest(k):
                    for stage, g in rest[k]:
                        stage(g)
                pipelined(act, TILES, [(4, evac_o), (0, evac_q), (2, evac_p), (1, exp)],
                          head=normalise_next, tail=normalise_rest)
                evac(GROUPS - 1)

                act.wait_ge(R[L]["slots"], 1)
                def distance(q):
                    positive(act, R[L]["hots_act"], q - 3)
                    act.activation(away[:, q % 4 * P:(q % 4 + 1) * P], iota_row[:, :], ACT.Abs, scale=-1.0,
                                   bias=rowf[:, q:q + 1]).then_inc(R[L]["away"], 1)
                distance(0)
                for q in range(HOTS_ACT[L]):
                    if q + 1 < HOTS_ACT[L]:
                        distance(q + 1)
                    act.wait_ge(R[L]["away"], q + 1)
                    act.activation(rowhot[:, q * P:(q + 1) * P], away[:, q % 4 * P:(q % 4 + 1) * P], ACT.Relu,
                                   scale=-1.0, bias=ones8[:, 0:1]).then_inc(R[L]["hots_act"], 1)
                if L == 0:
                    act.wait_ge(R[L]["gap"], 1)
                    act.activation(gexp[:, :], red[:, 2, :], ACT.Exp).then_inc(R[L]["exp"], 1)
                load_table((ACT.Gelu, ACT.Sigmoid)[L])

                NT = SLOT_TILES[L]
                E = F[L]

                def gelu(j, u, g):
                    r = u % 2
                    ready(act, E["h_ps"], j + 1)
                    free(act, E["y_ps"], j - 1)
                    act.activation(hidT[:, r * HID:(r + 1) * HID], psA[:, r * 512:r * 512 + HID], ACT.Gelu
                                   ).then_inc(E["hid"], 1)

                def sigmoid(j, u, g):
                    r = u % 2
                    ready(act, E["h_ps"], j + 1)
                    free(act, E["hid"], j - 1)
                    for c in range(CH):
                        last = act.activation(sig[:, r * HID + c * P:r * HID + (c + 1) * P],
                                              psA[:, (2 * r + 1) * 512 + c * P:(2 * r + 1) * 512 + (c + 1) * P],
                                              ACT.Sigmoid, bias=b1_column(r, CH + c))
                    last.then_inc(E["act"], 1)

                def evac_slots(j, u, g):
                    r = u % 2
                    ready(act, E["T_ps"], j + 1)
                    free(act, E["h_ps"], j - 1)
                    act.activation(slotsT[:, r * P:(r + 1) * P], ps_slots[r], ACT.Copy).then_inc(E["xT"], 1)

                def evac_y(j, u, g):
                    ready(act, E["y_ps"], j + 1)
                    free(act, landed, j + 1 - BLOCK)
                    act.activation(yout[:, u % BLOCK * DIM:(u % BLOCK + 1) * DIM], ps_rows[u % 2], ACT.Copy
                                   ).then_inc(E["y"], 1)

                if L == 0:
                    pipelined(act, NT, [(0, evac_slots), (1, gelu), (2, evac_y)], block=FBLOCK)
                else:
                    pipelined(act, NT, [(0, evac_slots), (1, sigmoid)], block=FBLOCK)

        @block.vector
        def _(dve):
            give_credit(dve, "vector")
            links = [0]

            def chain(ins):
                links[0] += 1
                ins.then_inc(vchain, 1)

            def link(ins=None):
                if ins is not None:
                    chain(ins)
                dve.wait_ge(vchain, links[0])

            V = nc.vector

            evac = [0]

            def setup_evac(make):
                bank = setup_banks[evac[0] % 8]
                evac[0] += 1
                dve.wait_ge(ps_set, evac[0])
                make(bank).then_inc(sb_set, 1)

            def setup_keys(L):
                setup_evac(lambda ps: V.tensor_scalar(kT[L][:, :], ps, bk[L][:, 0:1], None, ALU.add))
                dve.wait_ge(sb_set, evac[0])
                if L == 1:
                    dve.wait_ge(mask_ready, 1)
                    link(V.tensor_tensor(kT[1][:, :], kT[1][:, :], maskf[:, :], ALU.mult))
                dve.sem_inc(kT_ready, 1)
                def spread_keys():
                    for b in range(BATCH // 2):
                        V.tensor_tensor(kbd[L][:, b * HK:(b + 1) * HK].rearrange("p (h k) -> p h k", h=HEADS),
                                        kT[L][:, b * KEYS:(b + 1) * KEYS].unsqueeze(1).to_broadcast([P, HEADS, KEYS]),
                                        headmask[:, :].unsqueeze(2).to_broadcast([P, HEADS, KEYS]),
                                        ALU.mult).then_inc(*((kbd_ready[L], 1) if b else (keys_ready, 1)))

                if L == 0:
                    spread_keys()
                return spread_keys

            def setup_values(L, spread_keys):
                for b in range(BATCH):
                    setup_evac(lambda ps: V.tensor_tensor(vrows[:, b * DIM:(b + 1) * DIM], ps, bv[L][:, :], ALU.add))
                dve.wait_ge(sb_set, evac[0])
                va = vaug[L][:, :].rearrange("p (b h d) -> p b h d", b=BATCH, h=HEADS)
                for b in range(BATCH):
                    vc = va[:, b].rearrange("p (c h) d -> p c h d", c=CH)
                    vr = vrows[:, b * DIM:(b + 1) * DIM].rearrange("p (c h d) -> p c h d", c=CH, h=HPC)
                    V.tensor_tensor(vc[:, :, :, 0:HD], vr,
                                    groupmask[:, :].unsqueeze(1).unsqueeze(3).to_broadcast([P, CH, HPC, HD]),
                                    ALU.mult).then_inc(vaug_ready[L], 1)
                    V.tensor_copy(vc[:, :, :, HD], groupmask[:, :].unsqueeze(1).to_broadcast([P, CH, HPC])
                                  ).then_inc(vaug_ready[L], 1)
                if L == 1:
                    spread_keys()

            def setup_layer1():
                dve.wait_ge(in_small, 16 * 5)
                for k, t in enumerate((wq, wk, wv, wo)):
                    setup_evac(lambda ps: V.tensor_copy(t[1][:, :], ps))
                setup_values(1, setup_keys(1))
                setup_evac(lambda ps: V.tensor_copy(
                    w1[1][:, :].rearrange("p (e n) -> p e n", n=WC[1])[:, :, 2 * HID:],
                    ps[:, 0:EXPERTS * 2 * CH].rearrange("p (e c) -> p e c", e=EXPERTS)))
                dve.wait_ge(sb_set, evac[0])

            def mix(L, g):
                tiles = range(g * GROUP, (g + 1) * GROUP)
                if L == 1:
                    dve.wait_ge(y_in[g % 2], 32 * (g // 2 + 1))
                    def rows(k, t):
                        at = (((g % 2) * 2 + k) * GROUP + t) * DIM
                        return ybuf[:, at:at + DIM]

                    for k in range(2) if g == 0 else (1,):
                        for t, i in enumerate(tiles):
                            xi = x[:, i * DIM:(i + 1) * DIM]
                            if g == 0 and k == 1:
                                dve.wait_ge(x_half, i + 1)
                            V.scalar_tensor_tensor(xi, rows(k, t), gate[k][:, i:i + 1], xi, ALU.mult, ALU.add
                                                   ).then_inc(x_mixed if g == 0 and k == 1 else x_half, 1)
                    if g:
                        dve.wait_ge(x_half, (g + 1) * GROUP)
                        dve.wait_ge(y_scaled, g)
                        xg = x[:, g * GW:(g + 1) * GW]
                        V.tensor_tensor(xg, xg, ybuf[:, (g % 2) * 2 * GW:((g % 2) * 2 + 1) * GW], ALU.add
                                        ).then_inc(x_mixed, GROUP)

            def stats(L, g):
                tiles = range(g * GROUP, (g + 1) * GROUP)
                if L == 1:
                    dve.wait_ge(x_mixed, (g + 1) * GROUP)
                else:
                    dve.wait_ge(in_x[g], 16)
                for i in tiles:
                    V.bn_stats(bst[:, 6 * i:6 * i + 6], x[:, i * DIM:(i + 1) * DIM]).then_inc(stat, 1)
                dve.wait_ge(stat, L * TILES + (g + 1) * GROUP)
                for i in tiles:
                    V.bn_aggr(mv[:, 2 * i:2 * i + 2], bst[:, 6 * i:6 * i + 6]).then_inc(mv_ready, 1)
                dve.wait_ge(mv_ready, L * TILES + (g + 1) * GROUP)
                c = slice(g * GROUP, (g + 1) * GROUP)
                m = mv[:, :].rearrange("p (t k) -> p k t", k=2)
                V.tensor_scalar(vareps[:, c], m[:, 1, c], EPS, None, ALU.add).then_inc(terms, 1)
                V.tensor_scalar(minus_mean[:, c], m[:, 0, c], -1.0, None, ALU.mult).then_inc(terms, 1)

            def normalise_half(n, rs, nb):
                def emit(g):
                    L = n // 2
                    if n % 2 == 0:
                        dve.wait_ge(nb_ready, L * GROUPS + g + 1)
                    else:
                        ready(dve, A["nb2"], L * GROUPS + g + 1)
                    positive(dve, xT_ps, GROUPS * n + g - 1)
                    if g >= 2 and n % 2:
                        dve.wait_ge(stored[g % 2], 16 * (2 * L + g // 2))
                    for t in range(GROUP // 2, GROUP):
                        i = g * GROUP + t
                        V.tensor_scalar(xn[:, ((g % 2) * GROUP + t) * P:((g % 2) * GROUP + t + 1) * P],
                                        x[:, i * DIM:(i + 1) * DIM], rs[:, i:i + 1], nb[:, i:i + 1],
                                        ALU.mult, ALU.add).then_inc(xn_ready[1], 1)
                return emit

            setup_evac(lambda ps: V.tensor_copy(ctxT[:, :], ps))
            dve.wait_ge(sb_set, 1)
            V.tensor_copy(ctxrep[:, :].rearrange("p (b r k) -> p b r k", b=BATCH, r=HPC),
                          ctxT[:, :].rearrange("p (b k) -> p b k", b=BATCH).unsqueeze(2)
                          .to_broadcast([P, BATCH, HPC, KEYS])).then_inc(rep_ready, 1)
            stats(0, 0)
            dve.wait_ge(in_b0, 16 * 3)
            dve.wait_ge(consts, CONSTS)
            spread = setup_keys(0)

            for L in range(2):
                D, N0 = A, L * TILES
                if L == 1:
                    setup_layer1()
                half = normalise_half(2 * L, rstd, nbias)
                mix(L, 0)
                if L == 1:
                    stats(L, 0)
                mix(L, 1)
                if L == 0:
                    stats(L, 1)
                half(0)
                if L == 0:
                    setup_values(0, spread)
                else:
                    stats(L, 1)

                def stats_next(k):
                    if k + 2 < GROUPS:
                        mix(L, k + 2)
                    if k + 1 < GROUPS:
                        half(k + 1)
                    elif L == 0:
                        dve.wait_ge(rw_ps, 1)
                        V.tensor_copy(rw[0][:, :], psL[:, 0:EXPERTS]).then_inc(rw_ready, 1)
                    if k + 2 < GROUPS:
                        stats(L, k + 2)

                def highest(i, u, g):
                    r = u % 2
                    ready(dve, D["s_ps"], N0 + i + 1)
                    V.tensor_reduce(mx[:, r * HEADS:(r + 1) * HEADS], ps_scores(r).rearrange("p (h k) -> p h k", h=HEADS),
                                    axis=AX, op=ALU.max).then_inc(D["mx"], 1)

                def shift(i, u, g):
                    r = u % 2
                    ready(dve, D["mx"], N0 + i + 1)
                    free(dve, D["p"], N0 + i - 1)
                    V.tensor_tensor(shifted[:, r * HK:(r + 1) * HK].rearrange("p (h k) -> p h k", h=HEADS),
                                    ps_scores(r).rearrange("p (h k) -> p h k", h=HEADS),
                                    mx[:, r * HEADS:(r + 1) * HEADS].unsqueeze(2).to_broadcast([P, HEADS, KEYS]),
                                    ALU.subtract).then_inc(D["sh"], 1)

                def invert(i, u, g):
                    r = u % 2
                    ready(dve, D["o_ps"], N0 + i + 1)
                    V.reciprocal(rsum[:, r * HEADS:(r + 1) * HEADS], ps_out.rearrange("p (h d) -> p h d", h=HEADS)[:, :, HD]
                                 ).then_inc(D["rs"], 1)

                def normalise(i, u, g):
                    r = u % 2
                    ready(dve, D["rs"], N0 + i + 1)
                    free(dve, D["oT_ps"], N0 + i - 1)
                    V.tensor_tensor(heads_out[:, r * DIM:(r + 1) * DIM].rearrange("p (h d) -> p h d", h=HEADS),
                                    ps_out.rearrange("p (h d) -> p h d", h=HEADS)[:, :, 0:HD],
                                    rsum[:, r * HEADS:(r + 1) * HEADS].unsqueeze(2).to_broadcast([P, HEADS, HD]),
                                    ALU.mult).then_inc(D["o"], 1)

                def add(i, u, g):
                    ready(dve, D["y_ps"], N0 + i + 1)
                    ready(dve, D["xb"], N0 + i + 1)
                    V.tensor_tensor(cols(x, i), ps_y, xb[:, u * DIM:(u + 1) * DIM], ALU.add).then_inc(D["x1"], 1)

                def row_stats(i, u, g):
                    ready(dve, D["x1"], N0 + i + 1)
                    if u == 0:
                        free(dve, D["mr2"], L * GROUPS + g)
                    settle(dve, waited["vector"])
                    V.bn_stats(bst2[:, 6 * u:6 * u + 6], cols(x, i)).then_inc(D["stat2"], 1)

                def aggregate(i, u, g):
                    ready(dve, D["stat2"], N0 + i + 1)
                    settle(dve, waited["vector"])
                    V.bn_aggr(mv2[:, 2 * u:2 * u + 2], bst2[:, 6 * u:6 * u + 6]).then_inc(D["mv2"], 1)

                half2 = normalise_half(2 * L + 1, rstd2, nbias2)
                rest = [[0, 1], [2], [], [], [3]]

                def normalise_rest(k):
                    for g in rest[k]:
                        half2(g)
                pipelined(dve, TILES, [(1, highest), (5, row_stats), (1, shift), (3, invert), (5, aggregate),
                                       (3, normalise), (4, add)],
                          head=stats_next, tail=normalise_rest)

                K = TOPK[L]
                NT = SLOT_TILES[L]

                def te(t):
                    return t.rearrange("p (t e) -> p t e", e=EXPERTS)

                def et(t):
                    return t.rearrange("p (e t) -> p e t", t=TILES)

                def fetch_gather(j, half):
                    V.tensor_copy(idx_ring[:, half * BLOCK:(half + 1) * BLOCK], gidx[L][:, bass.ds(j, BLOCK)]
                                  ).then_inc(F[L]["idx"], 1)

                SUM, RM = red[:, 0, :], red[:, 1, :]
                tops = [red[:, 4, :], red[:, 5, :]]

                def choose(first, last):
                    t = slice(first * GROUP, last * GROUP)
                    n = (last - first) * GROUP
                    w = slice(first * GROUP * EXPERTS, last * GROUP * EXPERTS)
                    ps = ps_logits(last - 1)
                    dve.wait_ge(logit, N0 + last * GROUP)
                    logits = ps[:, w] if L == 0 else lg[:, w]
                    if L == 1:
                        link(V.tensor_tensor(te(lg[:, w]), te(ps[:, w]),
                                             rb[:, :].unsqueeze(1).to_broadcast([P, n, EXPERTS]), ALU.add))
                    for k in range(K):
                        link(V.tensor_reduce(tops[k][:, t], te(logits), axis=AX, op=ALU.max))
                        link(V.tensor_tensor(te(tmp[:, w]), te(logits),
                                             tops[k][:, t].unsqueeze(2).to_broadcast([P, n, EXPERTS]), ALU.is_equal))
                        link(V.tensor_tensor(te(tmp2[:, w]), te(tmp[:, w]),
                                             prefer[:, :].unsqueeze(1).to_broadcast([P, n, EXPERTS]), ALU.mult))
                        link(V.tensor_reduce(RM[:, t], te(tmp2[:, w]), axis=AX, op=ALU.max))
                        link(V.tensor_tensor(te(oh[k][:, w]), te(tmp2[:, w]),
                                             RM[:, t].unsqueeze(2).to_broadcast([P, n, EXPERTS]), ALU.is_equal))
                        if k + 1 < K:
                            link(V.scalar_tensor_tensor(lg[:, w], oh[k][:, w], -3e38, logits, ALU.mult, ALU.add))
                            logits = lg[:, w]
                    out16 = oh16[:, :].rearrange("p (e t) -> p t e", t=TILES)[:, t]
                    if K == 2:
                        link(V.tensor_tensor(out16, te(oh[0][:, w]), te(oh[1][:, w]), ALU.add))
                    else:
                        link(V.tensor_copy(out16, te(oh[0][:, w])))

                choose(0, GROUPS - 1)
                choose(GROUPS - 1, GROUPS)
                dve.sem_inc(R[L]["onehot"], 1)
                in_tile, in_tiles = psL[:, 128:128 + TE], psL[:, 256:256 + TE]
                dve.wait_ge(R[L]["prefix"], 1)
                link(V.tensor_tensor_scan(incl[:, :], carry[:, :], in_tiles, 0.0, ALU.mult, ALU.add))
                count = et(incl[:, :])[:, :, TILES - 1]
                chain(V.tensor_tensor(et(cmp[:, :]), count.unsqueeze(2).to_broadcast([P, EXPERTS, TILES]),
                                      steps128[:, :].unsqueeze(1).to_broadcast([P, EXPERTS, TILES]), ALU.is_gt))
                link(V.tensor_tensor(tot[:, :], incl[:, :], in_tiles, ALU.subtract))
                ntile, upto, base = (etile[:, k, :] for k in range(3))
                chain(V.tensor_reduce(ntile, et(cmp[:, :]), axis=AX, op=ALU.add))
                link(V.tensor_tensor(slotmat[:, :], in_tile, tot[:, :], ALU.add))
                link(V.tensor_tensor_scan(upto, ones8[:, :], ntile, 0.0, ALU.mult, ALU.add))
                link(V.tensor_tensor(base, upto, ntile, ALU.subtract))
                link(V.scalar_tensor_tensor(et(slotmat[:, :]), base.unsqueeze(2).to_broadcast([P, EXPERTS, TILES]),
                                            float(P), et(slotmat[:, :]), ALU.mult, ALU.add))
                for k in range(K):
                    chain(V.tensor_tensor(te((tmp, tmp2)[k][:, :]), slotmat[:, :].rearrange("p (e t) -> p t e", t=TILES),
                                          te(oh[k][:, :]), ALU.mult))
                link()
                for k in range(K):
                    chain(V.tensor_reduce(slotf[:, k * TILES:(k + 1) * TILES], te((tmp, tmp2)[k][:, :]), axis=AX, op=ALU.add))
                link()
                KT = K * TILES
                link(V.tensor_copy(slot[L][:, 0:KT], slotf[:, 0:KT]))
                chain(V.tensor_scalar(slot_j[:, 0:KT], slot[L][:, 0:KT], 7, None, ALU.logical_shift_right))
                link(V.tensor_scalar(slot_r[:, 0:KT], slot[L][:, 0:KT], P - 1, None, ALU.bitwise_and))
                V.tensor_copy(rowf[:, 0:KT], slot_r[:, 0:KT]).then_inc(R[L]["slots"], 1)
                col3 = colhot[:, 0:KT * NT].rearrange("p (q j) -> p q j", j=NT)
                V.tensor_tensor(col3, iota_tiles[:, 0:NT].unsqueeze(1).to_broadcast([P, KT, NT]),
                                slot_j[:, 0:KT].unsqueeze(2).to_broadcast([P, KT, NT]), ALU.is_equal
                                ).then_inc(R[L]["columns"], 1)
                dve.wait_ge(R[L]["slots"], 1)
                for q in range(HOTS_ACT[L], KT):
                    V.tensor_scalar(rowhot[:, q * P:(q + 1) * P], iota_row[:, :], rowf[:, q:q + 1], None,
                                    ALU.is_equal).then_inc(R[L]["hots"], 1)
                rows_out = K * TOKENS
                dve.wait_ge(R[L]["table"], 1)
                tab, mag, pad = (tabf[:, k * MAXT:k * MAXT + NT] for k in range(3))
                link(V.tensor_copy(tab, psL[:, 384:384 + NT]))
                link(V.scalar_tensor_tensor(mag, tab, -1.0, tab, ALU.mult, ALU.max))
                link(V.tensor_scalar(gidx[L][:, 0:NT], mag, -1.0, 0.0, ALU.add, ALU.max))
                for b in range(2):
                    fetch_gather(b * BLOCK, b)
                cj = cmpj[:, 0:NT * EXPERTS].rearrange("p (j e) -> p j e", e=EXPERTS)
                link(V.tensor_tensor(cj, upto.unsqueeze(1).to_broadcast([P, NT, EXPERTS]),
                                     tile_no[:, 0:NT].unsqueeze(2).to_broadcast([P, NT, EXPERTS]), ALU.is_le))
                link(V.tensor_reduce(etabf[:, 0:NT], cj, axis=AX, op=ALU.add))
                link(V.tensor_scalar(etab[L][:, 0:NT], etabf[:, 0:NT], float(EXPERTS - 1), None, ALU.min))
                dve.sem_inc(R[L]["experts"], 1)
                if K == 2:
                    V.tensor_tensor(red[:, 2, :], tops[1], tops[0], ALU.subtract).then_inc(R[L]["gap"], 1)
                link(V.tensor_scalar(pad, tab, 0.0, 2.0 * rows_out, ALU.is_equal, ALU.mult))
                link(V.scalar_tensor_tensor(pad, mag, -1.0, pad, ALU.add, ALU.add))
                link(V.tensor_scalar(tab, tab, 0.0, float(TOKENS), ALU.is_lt, ALU.mult))
                link(V.tensor_tensor(sidx[L][:, 0:NT], tab, pad, ALU.add))
                dve.wait_ge(vchain, links[0])
                if K == 2:
                    dve.wait_ge(R[L]["exp"], 1)
                    link(V.tensor_scalar(SUM, gexp[:, :], 1.0, None, ALU.add))
                    link(V.reciprocal(gate[0][:, :], SUM))
                    link(V.tensor_tensor(gate[1][:, :], gexp[:, :], gate[0][:, :], ALU.mult))
                    dve.sem_inc(gates_ready, 1)

                E = F[L]

                def fetch_indices(j, u, g):
                    if u % BLOCK or (isinstance(j, int) and j + BLOCK >= NT):
                        return
                    if isinstance(j, int) and j == 0:
                        return
                    free(dve, F[L]["T_ps"], j)
                    settle(dve, waited["vector"])
                    fetch_gather(j + BLOCK, (u // BLOCK + 1) % 2)

                def fetch_scatter(j, u, g):
                    if u % BLOCK:
                        return
                    if L == 1 or not (isinstance(j, int) and j == 0):
                        free(dve, landed, (0, SLOT_TILES[0])[L] + j - BLOCK)
                    settle(dve, waited["vector"])
                    V.tensor_copy(idx2_ring[:, u:u + BLOCK], sidx[L][:, bass.ds(j, BLOCK)]).then_inc(F[L]["idx2"], 1)

                def copy_weights(j, u, g):
                    r, v = u % 2, u % BLOCK
                    e = dve.value_load(etab[L][0:1, bass.ds(j, 1)], min_val=0, max_val=EXPERTS - 1)
                    free(dve, E["h_ps"], j - 1)
                    if L == 1:
                        free(dve, E["hid"], j - 1)
                        free(dve, E["act"], j - 1)
                    settle(dve, waited["vector"])
                    V.tensor_copy(w_ring[:, r * WC[1]:r * WC[1] + WC[L]], w1[L][:, bass.ds(e * WC[L], WC[L])]
                                  ).then_inc(E["w"], 1)
                    if L == 1:
                        dve.wait_ge(gathered[L][v], 16 * landed_in_ring(L, u, g))
                        free(dve, E["y"], j + 1 - BLOCK)
                        settle(dve, waited["vector"])
                        V.tensor_tensor(xkeep[:, v * DIM:(v + 1) * DIM], rows[:, (2 * v + 1) * DIM:(2 * v + 2) * DIM],
                                        b2[:, bass.ds(e * DIM, DIM)], ALU.add).then_inc(E["keep"], 1)

                def glu(j, u, g):
                    r = u % 2
                    ready(dve, E["act"], j + 1)
                    free(dve, E["y_ps"], j - 1)
                    for c in range(CH):
                        w = slice(r * HID + c * P, r * HID + (c + 1) * P)
                        last = V.scalar_tensor_tensor(hidT[:, w], psA[:, 2 * r * 512 + c * P:2 * r * 512 + (c + 1) * P],
                                                      b1_column(r, c), sig[:, w], ALU.add, ALU.mult)
                    last.then_inc(E["hid"], 1)

                def residual(j, u, g):
                    ready(dve, E["y_ps"], j + 1)
                    ready(dve, E["keep"], j + 1)
                    free(dve, landed, SLOT_TILES[0] + j + 1 - BLOCK)
                    v = u % BLOCK
                    V.tensor_tensor(yout[:, v * DIM:(v + 1) * DIM], ps_rows[u % 2],
                                    xkeep[:, v * DIM:(v + 1) * DIM], ALU.add).then_inc(E["y"], 1)

                dve.wait_ge((in_e0, in_e1)[L], 32)
                if L == 0:
                    pipelined(dve, NT, [(0, fetch_indices), (0, copy_weights), (2, fetch_scatter)], block=FBLOCK)
                else:
                    dve.wait_ge(in_bias, 32)
                    pipelined(dve, NT, [(0, fetch_indices), (0, copy_weights), (1, glu), (2, residual),
                                        (2, fetch_scatter)], block=FBLOCK)

        @block.tensor
        def _(pe):
            give_credit(pe, "tensor")
            T = nc.tensor
            done = [0]

            def setup(emit):
                n = done[0]
                if n > 7:
                    pe.wait_ge(sb_set, n - 7)
                emit(setup_banks[n % 8]).then_inc(ps_set, 1)
                done[0] += 1

            def setup_keys_values(L):
                if L == 0:
                    pe.wait_ge(in_wk, 16)
                    pe.wait_ge(sb_set, 1)
                setup(lambda d: T.matmul(d, wk[L][:, :], ctxT[:, :], start=True, stop=True))
                if L == 0:
                    pe.wait_ge(in_wv, 16)
                    pe.wait_ge(rep_ready, 1)
                else:
                    ready(pe, F[0]["y"], SLOT_TILES[0])
                for b in range(BATCH):
                    setup(lambda d: T.matmul(d, ctxrep[:, b * P:(b + 1) * P], wv[L][:, :], start=True, stop=True))

            def setup_layer1():
                pe.wait_ge(in_w1, 16 * 4)
                for k in range(4):
                    setup(lambda d: T.transpose(d, wload[:, k * DIM:(k + 1) * DIM], ident[:, :]))
                pe.wait_ge(sb_set, done[0])
                setup_keys_values(1)
                pe.wait_ge(in_bias, 32)
                setup(lambda d: T.transpose(d[:, 0:EXPERTS * 2 * CH], b1_in[:, :],
                                            ident[0:EXPERTS * 2 * CH, 0:EXPERTS * 2 * CH]))
                pe.wait_ge(sb_set, done[0])

            pe.wait_ge(ident_ready, 1)
            pe.wait_ge(in_ctx, 16)
            setup(lambda d: T.transpose(d, ctx_sb[:, :], ident[:, :]))
            setup_keys_values(0)

            for L in range(2):
                D, N0 = A, L * TILES

                def transpose_x(n):
                    def emit(g):
                        before_it = g - 1 if n % 2 else g
                        positive(pe, xT_ready, GROUPS * n + before_it)
                        for t in range(GROUP):
                            pe.wait_ge(xn_ready[t // 2], (TILES * n + GROUP * g) // 2 + t % 2 + 1)
                            last = T.transpose(ps_group[n % 2][g][:, t * P:(t + 1) * P],
                                               xn[:, ((g % 2) * GROUP + t) * P:((g % 2) * GROUP + t + 1) * P],
                                               ident[:, :])
                        last.then_inc(xT_ps, 1)
                    return emit

                def logits(g):
                    pe.wait_ge(rw_ready, 1)
                    pe.wait_ge(xT_ready, GROUPS * (2 * L + 1) + g + 1)
                    for i in range(g * GROUP, (g + 1) * GROUP):
                        T.matmul(ps_logits(g)[:, i * EXPERTS:(i + 1) * EXPERTS], xT[:, i * P:(i + 1) * P], rw[L][:, :],
                                 start=True, stop=True).then_inc(logit, 1)

                def queries(i, u, g):
                    free(pe, D["qT"], N0 + i)
                    T.matmul(ps_q, wq[L][:, :], cols(xT, i), start=True, stop=True).then_inc(D["q_ps"], 1)

                def scores(i, u, g):
                    r = u % 2
                    if isinstance(i, int) and i == 0:
                        pe.wait_ge(keys_ready, L + 1)
                    ready(pe, D["qT"], N0 + i + 1)
                    free(pe, D["sh"], N0 + i - 1)
                    last = T.matmul(ps_scores(r), qT[:, r * P:(r + 1) * P], cols(kbd[L], g, HK), start=True, stop=L == 0)
                    if L == 1:
                        last = T.matmul(ps_scores(r), onesb[0:1, :], cols(maskrow, g, HK), start=False, stop=True)
                    last.then_inc(D["s_ps"], 1)

                def transpose_p(i, u, g):
                    r = u % 2
                    ready(pe, D["p"], N0 + i + 1)
                    free(pe, D["pT"], N0 + i - 1)
                    for c in range(CH):
                        last = T.transpose(ps_probsT(r)[:, c * P:(c + 1) * P],
                                           probs[:, r * HK + c * P:r * HK + (c + 1) * P], ident[:, :])
                    last.then_inc(D["pT_ps"], 1)

                def values(i, u, g):
                    r = u % 2
                    ready(pe, D["pT"], N0 + i + 1)
                    free(pe, D["o"], N0 + i)
                    if isinstance(i, int) and i == 0:
                        pe.wait_ge(vaug_ready[L], 2 * BATCH)
                    for c in range(CH):
                        last = T.matmul(ps_out[:, c * VW:(c + 1) * VW],
                                        probsT[:, r * HK + c * P:r * HK + (c + 1) * P],
                                        vaug[L][:, bass.ds(g * CH * VW + c * VW, VW)], start=True, stop=True)
                    last.then_inc(D["o_ps"], 1)

                def transpose_o(i, u, g):
                    r = u % 2
                    ready(pe, D["o"], N0 + i + 1)
                    free(pe, D["x1"], N0 + i)
                    T.transpose(ps_oT, heads_out[:, r * DIM:(r + 1) * DIM], ident[:, :]).then_inc(D["oT_ps"], 1)

                def project(i, u, g):
                    r = u % 2
                    ready(pe, D["oT"], N0 + i + 1)
                    T.matmul(ps_y, headsT[:, r * P:(r + 1) * P], wo[L][:, :], start=True, stop=True).then_inc(D["y_ps"], 1)

                if L == 1:
                    setup_layer1()
                first = transpose_x(2 * L)
                first(0)
                pe.wait_ge(xT_ready, GROUPS * 2 * L + 1)
                if L == 0:
                    pe.wait_ge(in_w0, 32)
                if L == 1:
                    pe.wait_ge(mrow_ready, 1)
                transpose = transpose_x(2 * L + 1)

                def transpose_next(k):
                    if k + 1 < GROUPS:
                        first(k + 1)
                    else:
                        pe.wait_ge(xT_ready, GROUPS * (2 * L + 1))
                        pe.wait_ge(kbd_ready[L], BATCH - 1)
                        if L == 0:
                            pe.wait_ge(in_router, 16 * 3)
                            T.transpose(psL[:, 0:EXPERTS], rw_in[:, :], ident[0:EXPERTS, 0:EXPERTS]).then_inc(rw_ps, 1)

                rest = [[], [(transpose, 0)], [(transpose, 1), (logits, 0)], [(transpose, 2), (logits, 1)]]

                def transpose_rest(k):
                    if k == 1:
                        ready(pe, D["sh"], N0 + TILES)
                    for stage, g in rest[k]:
                        stage(g)
                pipelined(pe, TILES, [(1, scores), (4, transpose_o), (3, values), (0, queries), (2, transpose_p),
                                      (4, project)], head=transpose_next, tail=transpose_rest)
                logits(GROUPS - 2)
                transpose(GROUPS - 1)
                logits(GROUPS - 1)

                NT = SLOT_TILES[L]
                pe.wait_ge(R[L]["onehot"], 1)
                T.matmul(psL[:, 128:128 + TE], before[:, :], oh16[:, :], start=True, stop=True)
                T.matmul(psL[:, 256:256 + TE], ones16[:, :], oh16[:, :], start=True, stop=True
                         ).then_inc(R[L]["prefix"], 1)
                KT = TOPK[L] * TILES
                for n, q in enumerate(hot_order(L)):
                    pe.wait_ge(R[L]["tokens"], n // HOTS_CHUNK + 1)
                    if q >= HOTS_ACT[L]:
                        pe.wait_ge(R[L]["hots"], q - HOTS_ACT[L] + 1)
                    else:
                        pe.wait_ge(R[L]["hots_act"], q + 1)
                    last = T.matmul(psL[:, 384:384 + NT], rowhot[:, q * P:(q + 1) * P],
                                    colhot[:, q * NT:(q + 1) * NT], start=n == 0, stop=n == KT - 1)
                last.then_inc(R[L]["table"], 1)

                E = F[L]
                pe.wait_ge(R[L]["experts"], 1)
                pe.wait_ge((in_e0, in_e1)[L], 32)
                W = (L + 1) * DIM

                def transpose_rows(j, u, g):
                    r = u % 2
                    v = u % RING[L]
                    pe.wait_ge(gathered[L][v], 16 * landed_in_ring(L, u, g))
                    free(pe, E["xT"], j - 1)
                    T.transpose(ps_slots[r], rows[:, v * W:v * W + DIM], ident[:, :]).then_inc(E["T_ps"], 1)

                def up(j, u, g):
                    r = u % 2
                    ready(pe, E["xT"], j + 1)
                    ready(pe, E["w"], j + 1)
                    free(pe, E["hid"], j - 1)
                    for c in range((L + 1) * CH):
                        at = ((L + 1) * r + c // CH) * 512 + c % CH * P
                        last = T.matmul(psA[:, at:at + P], w_ring[:, r * WC[1] + c * P:r * WC[1] + (c + 1) * P],
                                        slotsT[:, r * P:(r + 1) * P], start=True, stop=True)
                    last.then_inc(E["h_ps"], 1)

                def down(j, u, g):
                    r = u % 2
                    e = pe.value_load(etab[L][0:1, bass.ds(j, 1)], min_val=0, max_val=EXPERTS - 1)
                    ready(pe, E["hid"], j + 1)
                    free(pe, E["y"], j - 1)
                    for c in range(CH):
                        last = T.matmul(ps_rows[r], hidT[:, r * HID + c * P:r * HID + (c + 1) * P],
                                        w2[L][:, bass.ds(e * HID + c * DIM, DIM)], start=c == 0, stop=c == CH - 1)
                    last.then_inc(E["y_ps"], 1)

                pipelined(pe, NT, [(0, transpose_rows), (1, up), (2, down)], block=FBLOCK)


_INS = ['x', 'ctx_1024', 'mask_BxS2_bf1'] + [
    f'L{L}_xattn_{n}' for L in range(2) for n in ('Wq', 'bq', 'Wk', 'bk', 'Wv', 'bv', 'Wo', 'bo')] + [
    'L0_ffn_router_w', 'L0_ffn_w1', 'L0_ffn_w2', 'L1_ffn_router_w', 'L1_ffn_router_b',
    'L1_ffn_w1', 'L1_ffn_b1', 'L1_ffn_w2', 'L1_ffn_b2']


def kernel(**inputs):
    import concourse.bacc as bacc
    from concourse.bass_utils import run_bass_kernel_spmd

    nc = bacc.Bacc("TRN2", target_bir_lowering=False, num_devices=1)
    arrays, aps = {}, {}
    for name in _INS:
        v = np.ascontiguousarray(inputs[name])
        if v.dtype == np.bool_:
            v = v.view(np.uint8)
        arrays[f"in_{name}"] = v
        aps[name] = nc.dram_tensor(f"in_{name}", v.shape, mybir.dt.from_np(v.dtype), kind="ExternalInput").ap()
    out = nc.dram_tensor("out", (BATCH, SEQ, DIM), F32, kind="ExternalOutput").ap()
    build(nc, aps, out)
    r = run_bass_kernel_spmd(nc, [arrays], core_ids=[0])
    return r.results[0]["out"]
```
